# Optimizing a Trainium2 kernel written in Bass

```python
import numpy as np
import jax
import jax.numpy as jnp

def _softmax(x, axis=-1):
    return jax.nn.softmax(x, axis=axis)

def _gelu(x):
    return jax.nn.gelu(x, approximate=True)

def _silu(x):
    return jax.nn.silu(x)

def _sigmoid(x):
    return jax.nn.sigmoid(x)

def _layernorm(x, axis=-1, eps=1e-05):
    m = jnp.mean(x, axis=axis, keepdims=True)
    v = jnp.var(x, axis=axis, keepdims=True)
    return (x - m) / jnp.sqrt(v + eps)

def _scatter_add(tgt, idx, src, axis=0):
    return tgt.at[idx].add(src)

def _segment_sum(src, seg, n):
    return jax.ops.segment_sum(src, seg, n)
kernel_name = 'mk_gnn_preln_d4_gnn_r16_d17c29'

def setup_inputs(seed: int=0):
    np.random.seed(seed)
    _w = jnp.asarray

    def _rec_inputs():
        import jax
        import jax.numpy as jnp
        _gk = jax.random.key(seed)
        x = -0.0003713 + 1 * jax.random.normal(jax.random.fold_in(_gk, 1), (6250, 256), jnp.float32)
        _s = jax.random.randint(jax.random.fold_in(_gk, 2), (50000,), 0, 6250, jnp.int32)
        _d = jax.random.randint(jax.random.fold_in(_gk, 3), (50000,), 0, 6250, jnp.int32)
        _loop = jnp.arange(6250, dtype=jnp.int32)
        src = jnp.concatenate([_s, _d, _loop])
        dst = jnp.concatenate([_d, _s, _loop])
        _o = jnp.argsort(dst, stable=True)
        src = src[_o]
        dst = dst[_o]
        edge_type_8 = jax.random.randint(jax.random.fold_in(_gk, 13), (106250,), 0, 8, jnp.int32)
        return (x, src, dst, edge_type_8)
    x, src, dst, edge_type_8 = _rec_inputs()

    def _L0_gnn_setup():
        import jax, jax.numpy as jnp
        import numpy as np
        N_NODES = 3125
        N_EDGES = 50000
        DIM = 256
        HEADS = 8
        DIM_OUT = 32
        key = jax.random.key(seed)
        ks = jax.random.split(key, 9)
        s = 1.0 / np.sqrt(DIM)
        inner = HEADS * DIM_OUT
        return {'x': jax.random.normal(ks[0], (N_NODES, DIM), dtype=jnp.float32), 'Wq': jax.random.uniform(ks[1], (DIM, inner), jnp.float32, -s, s), 'bq': jax.random.uniform(ks[2], (inner,), jnp.float32, -s, s), 'Wk': jax.random.uniform(ks[3], (DIM, inner), jnp.float32, -s, s), 'bk': jax.random.uniform(ks[4], (inner,), jnp.float32, -s, s), 'Wv': jax.random.uniform(ks[5], (DIM, inner), jnp.float32, -s, s), 'bv': jax.random.uniform(ks[6], (inner,), jnp.float32, -s, s), 'src': jax.random.randint(ks[7], (N_EDGES,), 0, N_NODES), 'dst': jax.random.randint(ks[8], (N_EDGES,), 0, N_NODES)}
    _L0_gnn_all = _L0_gnn_setup()
    _L0_gnn_in = {k: v for k, v in _L0_gnn_all.items() if k in ('Wq', 'bq', 'Wk', 'bk', 'Wv', 'bv')}
    del _L0_gnn_all

    def _L1_gnn_setup():
        import jax, jax.numpy as jnp
        import numpy as np
        N = 3125
        DIM = 256
        E = 50000

        def _srgnn_conv(x, W, b, src, dst, num_nodes):
            xl = x @ W.T + b
            msgs = xl[src]
            agg = jax.ops.segment_sum(msgs, dst, num_segments=num_nodes)
            cnt = jax.ops.segment_sum(jnp.ones((src.shape[0],), x.dtype), dst, num_segments=num_nodes)
            return agg / jnp.maximum(cnt, 1.0)[:, None]
        key = jax.random.key(seed)
        ks = jax.random.split(key, 11)
        stdv = 1.0 / np.sqrt(DIM)
        u = lambda k, shape: jax.random.uniform(k, shape, jnp.float32, -stdv, stdv)
        hidden = jax.random.normal(ks[0], (N, DIM), jnp.float32)
        edge_index = jax.random.randint(ks[1], (2, E), 0, N, jnp.int64)
        return {'hidden': hidden, 'edge_index': edge_index, 'W_in': u(ks[2], (DIM, DIM)), 'b_in': u(ks[3], (DIM,)), 'W_out': u(ks[4], (DIM, DIM)), 'b_out': u(ks[5], (DIM,)), 'W_ih': u(ks[6], (3 * DIM, 2 * DIM)), 'b_ih': u(ks[7], (3 * DIM,)), 'W_hh': u(ks[8], (3 * DIM, DIM)), 'b_hh': u(ks[9], (3 * DIM,))}
    _L1_gnn_all = _L1_gnn_setup()
    _L1_gnn_in = {k: v for k, v in _L1_gnn_all.items() if k in ('W_in', 'b_in', 'W_out', 'b_out', 'W_ih', 'b_ih', 'W_hh', 'b_hh')}
    del _L1_gnn_all

    def _L2_gnn_setup():
        import jax, jax.numpy as jnp
        import numpy as np
        N = 3125
        E = 50000
        DIN = 256
        DOUT = 256
        R = 8
        key = jax.random.key(seed)
        k1, k2, k3, k4, k5, k6 = jax.random.split(key, 6)
        h = jax.random.normal(k1, (N, DIN), dtype=jnp.float32)
        weight = jax.random.normal(k2, (R, DIN, DOUT), dtype=jnp.float32) * (1.0 / np.sqrt(DIN))
        sl_w = jax.random.normal(k3, (DOUT, DIN), dtype=jnp.float32) * (1.0 / np.sqrt(DIN))
        sl_b = jax.random.normal(k4, (DOUT,), dtype=jnp.float32) * 0.01
        edge_index = jax.random.randint(k5, (2, E), 0, N, dtype=jnp.int32)
        edge_type = jax.random.randint(k6, (E,), 0, R, dtype=jnp.int32)
        return {'h': h, 'weight': weight, 'sl_w': sl_w, 'sl_b': sl_b, 'edge_index': edge_index, 'edge_type': edge_type, 'num_nodes': N}
    _L2_gnn_all = _L2_gnn_setup()
    _L2_gnn_in = {k: v for k, v in _L2_gnn_all.items() if k in ('weight', 'sl_w', 'sl_b')}
    del _L2_gnn_all

    def _L3_gnn_setup():
        import jax, jax.numpy as jnp
        import numpy as np
        N_NODES = 6250
        N_EDGES = 100000
        D_IN = 256
        HEADS = 8
        D_HEAD = 32
        NEG_SLOPE = 0.2
        BN_EPS = 1e-05
        key = jax.random.key(seed)
        ks = jax.random.split(key, 8)
        x = jax.random.normal(ks[0], (N_NODES, D_IN), dtype=jnp.float32)
        edge_index = jax.random.randint(ks[1], (2, N_EDGES), 0, N_NODES, dtype=jnp.int32)
        W = jax.random.normal(ks[2], (D_IN, HEADS * D_HEAD), dtype=jnp.float32) / np.sqrt(D_IN)
        att_src = jax.random.normal(ks[3], (HEADS, D_HEAD), dtype=jnp.float32) / np.sqrt(D_HEAD)
        att_dst = jax.random.normal(ks[4], (HEADS, D_HEAD), dtype=jnp.float32) / np.sqrt(D_HEAD)
        bias = jax.random.normal(ks[5], (HEADS * D_HEAD,), dtype=jnp.float32) * 0.01
        gamma = jnp.ones((HEADS * D_HEAD,), dtype=jnp.float32)
        beta = jnp.zeros((HEADS * D_HEAD,), dtype=jnp.float32)
        return {'x': x, 'edge_index': edge_index, 'W': W, 'att_src': att_src, 'att_dst': att_dst, 'bias': bias, 'gamma': gamma, 'beta': beta}
    _L3_gnn_all = _L3_gnn_setup()
    _L3_gnn_in = {k: v for k, v in _L3_gnn_all.items() if k in ('W', 'att_src', 'att_dst', 'bias', 'gamma', 'beta')}
    del _L3_gnn_all
    return {'x': x, 'src': src, 'dst': dst, 'edge_type_8': edge_type_8, 'L0_gnn_Wq': _L0_gnn_in['Wq'], 'L0_gnn_bq': _L0_gnn_in['bq'], 'L0_gnn_Wk': _L0_gnn_in['Wk'], 'L0_gnn_bk': _L0_gnn_in['bk'], 'L0_gnn_Wv': _L0_gnn_in['Wv'], 'L0_gnn_bv': _L0_gnn_in['bv'], 'L1_gnn_W_in': _L1_gnn_in['W_in'], 'L1_gnn_b_in': _L1_gnn_in['b_in'], 'L1_gnn_W_out': _L1_gnn_in['W_out'], 'L1_gnn_b_out': _L1_gnn_in['b_out'], 'L1_gnn_W_ih': _L1_gnn_in['W_ih'], 'L1_gnn_b_ih': _L1_gnn_in['b_ih'], 'L1_gnn_W_hh': _L1_gnn_in['W_hh'], 'L1_gnn_b_hh': _L1_gnn_in['b_hh'], 'L2_gnn_weight': _L2_gnn_in['weight'], 'L2_gnn_sl_w': _L2_gnn_in['sl_w'], 'L2_gnn_sl_b': _L2_gnn_in['sl_b'], 'L3_gnn_W': _L3_gnn_in['W'], 'L3_gnn_att_src': _L3_gnn_in['att_src'], 'L3_gnn_att_dst': _L3_gnn_in['att_dst'], 'L3_gnn_bias': _L3_gnn_in['bias'], 'L3_gnn_gamma': _L3_gnn_in['gamma'], 'L3_gnn_beta': _L3_gnn_in['beta']}

def reference(x, src, dst, edge_type_8, L0_gnn_Wq, L0_gnn_bq, L0_gnn_Wk, L0_gnn_bk, L0_gnn_Wv, L0_gnn_bv, L1_gnn_W_in, L1_gnn_b_in, L1_gnn_W_out, L1_gnn_b_out, L1_gnn_W_ih, L1_gnn_b_ih, L1_gnn_W_hh, L1_gnn_b_hh, L2_gnn_weight, L2_gnn_sl_w, L2_gnn_sl_b, L3_gnn_W, L3_gnn_att_src, L3_gnn_att_dst, L3_gnn_bias, L3_gnn_gamma, L3_gnn_beta):
    import jax
    import jax.numpy as jnp

    def _L0_gnn_ref(x, Wq, bq, Wk, bk, Wv, bv, src, dst):
        import jax, jax.numpy as jnp
        import numpy as np
        N_NODES = 3125
        N_EDGES = 50000
        DIM = 256
        HEADS = 8
        DIM_OUT = 32
        n = x.shape[0]
        q = (x @ Wq + bq).reshape(n, HEADS, DIM_OUT)
        k = (x @ Wk + bk).reshape(n, HEADS, DIM_OUT)
        v = (x @ Wv + bv).reshape(n, HEADS, DIM_OUT)
        scores = jnp.einsum('ehd,ehd->eh', q[src], k[dst]) / jnp.sqrt(jnp.asarray(DIM_OUT, dtype=x.dtype))
        m = jax.ops.segment_max(scores, dst, num_segments=n)
        m = jnp.where(jnp.isfinite(m), m, 0.0)
        e = jnp.exp(scores - m[dst])
        z = jax.ops.segment_sum(e, dst, num_segments=n)
        p = e / jnp.maximum(z[dst], 1e-16)
        out = jax.ops.segment_sum(v[src] * p[:, :, None], dst, num_segments=n)
        return out.reshape(n, HEADS * DIM_OUT)

    def _L1_gnn_ref(hidden, edge_index, W_in, b_in, W_out, b_out, W_ih, b_ih, W_hh, b_hh):
        import jax, jax.numpy as jnp
        import numpy as np
        N = 3125
        DIM = 256
        E = 50000

        def _srgnn_conv(x, W, b, src, dst, num_nodes):
            xl = x @ W.T + b
            msgs = xl[src]
            agg = jax.ops.segment_sum(msgs, dst, num_segments=num_nodes)
            cnt = jax.ops.segment_sum(jnp.ones((src.shape[0],), x.dtype), dst, num_segments=num_nodes)
            return agg / jnp.maximum(cnt, 1.0)[:, None]
        src, dst = (edge_index[0], edge_index[1])
        n = hidden.shape[0]
        input_in = _srgnn_conv(hidden, W_in, b_in, src, dst, n)
        input_out = _srgnn_conv(hidden, W_out, b_out, dst, src, n)
        inputs = jnp.concatenate([input_in, input_out], axis=-1)
        gi = inputs @ W_ih.T + b_ih
        gh = hidden @ W_hh.T + b_hh
        i_r, i_i, i_n = jnp.split(gi, 3, axis=-1)
        h_r, h_i, h_n = jnp.split(gh, 3, axis=-1)
        reset_gate = jax.nn.sigmoid(i_r + h_r)
        input_gate = jax.nn.sigmoid(i_i + h_i)
        new_gate = jnp.tanh(i_n + reset_gate * h_n)
        return (1.0 - input_gate) * hidden + input_gate * new_gate

    def _L2_gnn_ref(h, weight, sl_w, sl_b, edge_index, edge_type, num_nodes):
        import jax, jax.numpy as jnp
        import numpy as np
        N = 3125
        E = 50000
        DIN = 256
        DOUT = 256
        R = 8
        src, dst = (edge_index[0], edge_index[1])
        hW = jnp.einsum('nd,rde->rne', h, weight)
        msg = hW[edge_type, src]
        m = jax.ops.segment_sum(msg, dst, num_segments=num_nodes)
        deg = jax.ops.segment_sum(jnp.ones_like(dst, dtype=h.dtype), dst, num_segments=num_nodes)
        deg = jnp.maximum(deg, 1.0)[:, None]
        return h @ sl_w.T + sl_b + m / deg

    def _L3_gnn_ref(x, edge_index, W, att_src, att_dst, bias, gamma, beta):
        import jax, jax.numpy as jnp
        import numpy as np
        N_NODES = 6250
        N_EDGES = 100000
        D_IN = 256
        HEADS = 8
        D_HEAD = 32
        NEG_SLOPE = 0.2
        BN_EPS = 1e-05
        N = x.shape[0]
        H, D = att_src.shape
        xh = (x @ W).reshape(N, H, D)
        a_src = jnp.einsum('nhd,hd->nh', xh, att_src)
        a_dst = jnp.einsum('nhd,hd->nh', xh, att_dst)
        loops = jnp.arange(N, dtype=edge_index.dtype)
        src = jnp.concatenate([edge_index[0], loops])
        dst = jnp.concatenate([edge_index[1], loops])
        e = jax.nn.leaky_relu(a_src[src] + a_dst[dst], NEG_SLOPE)
        m = jax.ops.segment_max(e, dst, num_segments=N)
        e = jnp.exp(e - m[dst])
        denom = jax.ops.segment_sum(e, dst, num_segments=N)
        alpha = e / denom[dst]
        msg = xh[src] * alpha[:, :, None]
        out = jax.ops.segment_sum(msg, dst, num_segments=N).reshape(N, H * D) + bias
        mean = jnp.mean(out, axis=0)
        var = jnp.var(out, axis=0)
        out = (out - mean) * jax.lax.rsqrt(var + BN_EPS) * gamma + beta
        return out + x
    edge_index = jnp.stack([src, dst])
    h = jnp.maximum(_layernorm(x, axis=-1), 0.0)
    x = x + _L0_gnn_ref(h, L0_gnn_Wq, L0_gnn_bq, L0_gnn_Wk, L0_gnn_bk, L0_gnn_Wv, L0_gnn_bv, src, dst)
    h = jnp.maximum(_layernorm(x, axis=-1), 0.0)
    x = x + _L1_gnn_ref(h, edge_index, L1_gnn_W_in, L1_gnn_b_in, L1_gnn_W_out, L1_gnn_b_out, L1_gnn_W_ih, L1_gnn_b_ih, L1_gnn_W_hh, L1_gnn_b_hh)
    h = jnp.maximum(_layernorm(x, axis=-1), 0.0)
    x = x + _L2_gnn_ref(h, L2_gnn_weight, L2_gnn_sl_w, L2_gnn_sl_b, edge_index, edge_type_8, 6250)
    h = jnp.maximum(_layernorm(x, axis=-1), 0.0)
    x = x + _L3_gnn_ref(h, edge_index, L3_gnn_W, L3_gnn_att_src, L3_gnn_att_dst, L3_gnn_bias, L3_gnn_gamma, L3_gnn_beta)
    return x

_drawn_inputs = setup_inputs


def setup_inputs(seed=0):
    import zlib

    import numpy as np

    out = dict(_drawn_inputs(seed))
    spreads = {'L3_gnn_gamma': (1.0, 0.2), 'L3_gnn_beta': (0.0, 0.1)}
    factors = {'L0_gnn_Wq': 4.43,
     'L0_gnn_bq': 8.0,
     'L0_gnn_Wk': 4.563,
     'L0_gnn_bk': 8.0,
     'L1_gnn_b_in': 8.0,
     'L1_gnn_b_out': 7.361,
     'L1_gnn_b_ih': 4.593,
     'L1_gnn_b_hh': 6.729,
     'L2_gnn_sl_b': 8.0,
     'L3_gnn_bias': 8.0}
    for name, (base, spread) in spreads.items():
        noise = np.random.default_rng([zlib.crc32(name.encode()), seed]).standard_normal(out[name].shape)
        drawn = base * np.exp(spread * noise) if base else spread * noise
        out[name] = jnp.asarray(drawn.astype(out[name].dtype))
    for name, factor in factors.items():
        out[name] = (out[name] * factor).astype(out[name].dtype)
    return out
```

```python
from contextlib import ExitStack

import numpy as np

import concourse.bass as bass
from concourse import mybir

F32, I32, U8 = mybir.dt.float32, mybir.dt.int32, mybir.dt.uint8
ALU, ACT, AX = mybir.AluOpType, mybir.ActivationFunctionType, mybir.AxisListType
DVE = mybir.EngineType.DVE
PE = mybir.EngineType.PE

P = 128
N, D, HEADS, DH, RELS, EDGES = 6250, 256, 8, 32, 8, 106250
TILES = 50
NP = TILES * P
COLS = 16 * -(-EDGES // (16 * P))
SLOTS = 896
GROUP = 8
RING = 16
ITERS = SLOTS // RING
NBLK = SLOTS // P
ACCW = D + HEADS
KHW = D + 1
ROW = 2 * D + HEADS
NOWHERE = 32767
BIG = 1e38
SUMW = D + 4
TABLES = 4
TROWS = NP + P
MIDS = 4 * D
assert COLS + TILES <= SLOTS and SLOTS % P == 0 and SLOTS * P % RING == 0


class Chain:

    def __init__(self, sem):
        self.sem, self.base, self.n = sem, 0, 0

    def bind(self, eng):
        self.eng = eng
        return self

    def enter(self, k, per):
        self.start = self.base + self.n
        self.per = per
        self.base, self.n = self.start + k * per, 0

    def leave(self, iters):
        assert self.n == self.per, f"{self.n} steps in an iteration, {self.per} were stated"
        self.base, self.n = self.start + iters * self.per, 0

    def step(self, ins):
        ins.then_inc(self.sem, 1)
        self.n += 1
        return self.n

    def wait(self, n=None):
        self.eng.wait_ge(self.sem, self.base + (self.n if n is None else n))

    def then(self, ins):
        self.step(ins)
        self.wait()


def program(nc, a, out):
    with ExitStack() as ctx:
        build(nc, ctx, a, out)


def build(nc, ctx, a, out):
    def sb(name, shape, dt=F32):
        return ctx.enter_context(nc.sbuf_tensor(name, shape, dt))

    def sem(name):
        return ctx.enter_context(nc.semaphore(name))

    def dram(name, shape, dt=F32):
        return nc.dram_tensor(name, shape, dt).ap()

    def tile_rows(table, t, width=None):
        return table[bass.ds(t * P, P), :] if width is None else table[bass.ds(t * P, P), 0:width]

    rec = dram("rec", [SLOTS * P, 2], I32)
    flags = dram("flags", [SLOTS, P], U8)
    qv_tab = dram("qv_tab", [NP, 2 * D])
    h1_tab = dram("h1_tab", [NP, D])
    src_sum = [dram(f"src_sum{k}", [TROWS, SUMW]) for k in range(TABLES)]
    hw_tab = dram("hw_tab", [NP * RELS, D])
    xh_tab = dram("xh_tab", [NP, ACCW])
    x1_tab, x2_tab, xs_tab, x3_tab = (dram(n, [NP, D]) for n in ("x1_tab", "x2_tab", "xs_tab", "x3_tab"))

    acc = sb("acc", [P, TILES * ACCW])
    kh = sb("kh", [P, TILES * KHW])
    acc3 = acc[:, :].rearrange("p (t f) -> p t f", f=ACCW)
    kh3 = kh[:, :].rearrange("p (t f) -> p t f", f=KHW)
    rows = sb("rows", [P, RING, ROW])
    oh = sb("oh", [P, 2, GROUP, P])
    oht = sb("oht", [P, 2, GROUP, P])
    mnode = sb("mnode", [P, TILES * HEADS])
    m3 = mnode[:, :].rearrange("p (t h) -> p t h", h=HEADS)
    bcast = kh[:, 1024:1024 + 5 * D]
    adst = kh[:, 2560:2560 + TILES * HEADS]
    adst3 = adst.rearrange("p (t h) -> p t h", h=HEADS)
    src_i = sb("src_i", [P, SLOTS], I32)
    rel_i = sb("rel_i", [P, SLOTS], I32)
    dl = sb("dl", [P, SLOTS])
    last = sb("last", [P, SLOTS])
    shared = sb("shared", [P, SLOTS // GROUP * P], U8)
    starts = shared[0:HEADS * GROUP, :].rearrange("p (g e) -> p g e", e=P)
    tile_i = shared[64:65, 0:4 * SLOTS].bitcast(I32)
    wts = sb("wts", [P, 22 * D])
    brow = oht[0:1, :, :, :].rearrange("p h g e -> p (h g e)")
    ident, lower, iota_row = sb("ident", [P, P]), sb("lower", [P, P]), sb("iota_row", [P, P])
    ones = sb("ones", [P, P])
    lt_tile = sb("lt_tile", [TILES, TILES])
    spare = sb("spare", [P, 1])
    idx = sb("idx", [P, RING], I32)
    idx2 = sb("idx2", [P, RING], I32)
    rdeg = sb("rdeg", [P, TILES])
    small = sb("small", [P, 64])
    psum = ctx.enter_context(nc.psum_tensor("psum", [P, 8, 512], F32))

    stage = sem("stage")
    ring = [sem(f"ring{b}") for b in range(RING)]
    RANK_ITERS = COLS // RING

    def landed(use):
        return 16 * (use + 2)

    waits = {e: sem(f"waits_{e}") for e in ("pool", "pe", "dve", "sp")}

    def waited(eng, name="pool"):
        eng.sem_inc(waits[name], 1)

    def now(i, p, n=2):
        return n * i + p + n + 1

    def prev(i, p, n=2):
        return n * i + p + 1

    progs = {k: [] for k in ("sync", "gpsimd", "vector", "scalar", "tensor")}

    def stage_of(**parts):
        for k in progs:
            progs[k].append(parts.get(k))

    weights_sem = sem("weights")
    weights = [0]

    u_src = oht[:, 0].rearrange("p a b -> p (a b)")[:, 0:COLS].bitcast(I32)
    u_dst = oht[:, 1].rearrange("p a b -> p (a b)")[:, 0:COLS].bitcast(I32)
    kh_i = kh[:, :].bitcast(I32)
    u_typ = kh_i[:, 0:COLS]
    key_f = kh[:, 1 * COLS:2 * COLS]
    hi_f = kh[:, 2 * COLS:3 * COLS]
    lo_f = kh[:, 3 * COLS:4 * COLS]
    hi_i = kh_i[:, 4 * COLS:5 * COLS]
    lo_i = kh_i[:, 5 * COLS:6 * COLS]
    u_rec = kh_i[:, 6 * COLS:8 * COLS].rearrange("p (c w) -> p c w", w=2)
    base_f = kh[:, 8 * COLS:9 * COLS]
    rank_f = kh[:, 9 * COLS:10 * COLS]
    iota_slot = kh[:, 10 * COLS:10 * COLS + SLOTS]
    tile_f = kh[:, 10 * COLS + SLOTS:10 * COLS + 2 * SLOTS]
    ge = kh[:, 10 * COLS + 2 * SLOTS:10 * COLS + 3 * SLOTS]
    blank = rows[:, :, :].rearrange("p r w -> p (r w)").bitcast(I32)[:, 0:2 * SLOTS] \
        .rearrange("p (s w) -> p s w", w=2)
    ohhi = wts[:, 0:16 * TILES].rearrange("p (h g t) -> p h g t", h=2, g=GROUP)
    ohhit = wts[:, 1024:1024 + 16 * P].rearrange("p (h g e) -> p h g e", h=2, g=GROUP)
    hist = wts[0:TILES, 3200:3328]
    incl = wts[0:TILES, 3328:3456]
    count = wts[0:TILES, 3456:3584]
    scrap = wts[:, 3584:3712]
    keyb = wts[:, 3712:3728].rearrange("p (h g) -> p h g", h=2)
    posb = idx2[:, :].rearrange("p (h g) -> p h g", h=2)
    recb = wts[:, 3728:3760].bitcast(I32).rearrange("p (h g w) -> p h g w", h=2, w=2)
    posf = wts[:, 3760:3776].rearrange("p (h g) -> p h g", h=2)

    loaded = sem("loaded")
    consts = sem("consts")
    blank_set = sem("blank_set")
    table_done = [sem(f"table_done{k}") for k in range(TABLES)]
    ZEROED = 96
    zero_set = sem("zero_set")
    filled = sem("filled")
    v_own = Chain(sem("v_own"))

    def const_sync(sp):
        sp.dma_start(u_src, a["src"]).then_inc(loaded, 16)
        sp.dma_start(u_dst, a["dst"]).then_inc(loaded, 16)
        sp.dma_start(u_typ, a["typ"]).then_inc(loaded, 16)
        sp.wait_ge(blank_set, 2)
        sp.dma_start(rec.rearrange("(p s) w -> p (s w)", p=P), blank.rearrange("p s w -> p (s w)")) \
            .then_inc(filled, 16)
        sp.wait_ge(filled, 16)

    def const_gpsimd(pool):
        g = nc.gpsimd
        for b in range(RING):
            pool.dma_start(oh[:, 0, b, 0:8] if b < GROUP else oh[:, 1, b - GROUP, 0:8],
                           a["x"][0:P, 0:8]).then_inc(ring[b], 16)
        imprecise = dict(allow_small_or_imprecise_dtypes=True)
        g.iota(iota_row[:, :], [[1, P]], base=0, channel_multiplier=0, **imprecise).then_inc(consts, 1)
        g.iota(spare[:, :], [[1, 1]], base=NP, channel_multiplier=1, **imprecise).then_inc(consts, 1)
        g.iota(iota_slot[:, :], [[1, SLOTS]], base=0, channel_multiplier=0, **imprecise).then_inc(consts, 1)
        g.memset(ones[:, :], 1.0).then_inc(consts, 1)
        g.memset(ident[:, :], 0.0).then_inc(consts, 1)
        g.memset(lower[:, :], 1.0).then_inc(consts, 1)
        g.memset(lt_tile[:, :], 1.0).then_inc(consts, 1)
        pool.wait_ge(consts, 7)
        g.affine_select(out=ident[:, :], in_=ident[:, :], compare_op=ALU.not_equal, fill=1.0,
                        base=0, pattern=[[-1, P]], channel_multiplier=1).then_inc(consts, 1)
        g.affine_select(out=lower[:, :], in_=lower[:, :], compare_op=ALU.is_gt, fill=0.0,
                        base=0, pattern=[[-1, P]], channel_multiplier=1).then_inc(consts, 1)
        g.affine_select(out=lt_tile[:, :], in_=lt_tile[:, :], compare_op=ALU.is_gt, fill=0.0,
                        base=0, pattern=[[1, TILES]], channel_multiplier=-1).then_inc(consts, 1)
        pool.wait_ge(consts, 10)
        pool.wait_ge(zero_set, 1)
        for k in range(TABLES):
            view = src_sum[k].rearrange("(p j) f -> p (j f)", p=P)
            piece = TROWS // P * SUMW // 3
            for n in range(3):
                pool.dma_start(view[:, n * piece:(n + 1) * piece], acc[:, 0:piece]).then_inc(table_done[k], 32)
        for k in range(TABLES):
            pool.wait_ge(table_done[k], ZEROED)
        for b in range(RING):
            pool.wait_ge(ring[b], landed(-1))

    def const_vector(dve):
        v, c = nc.vector, v_own.bind(dve)
        v.memset(blank[:, :, 0], N).then_inc(blank_set, 1)
        v.memset(blank[:, :, 1], NOWHERE).then_inc(blank_set, 1)
        v.memset(acc[:, :], 0.0).then_inc(zero_set, 1)
        c.step(v.memset(hist, 0.0))
        dve.wait_ge(loaded, 48)
        c.step(v.tensor_scalar(hi_i, u_dst, 7, None, ALU.logical_shift_right))
        c.step(v.tensor_scalar(lo_i, u_dst, P - 1, None, ALU.bitwise_and))
        c.step(v.tensor_copy(key_f, u_dst))
        c.wait()
        c.step(v.tensor_copy(hi_f, hi_i))
        c.step(v.tensor_copy(lo_f, lo_i))
        c.step(v.tensor_copy(u_rec[:, :, 1], u_dst))
        c.then(v.scalar_tensor_tensor(u_rec[:, :, 0], u_typ, 8192.0, u_src, ALU.mult, ALU.add))

    stage_of(sync=const_sync, gpsimd=const_gpsimd, vector=const_vector)

    hot_ready = sem("hot_ready")
    hist_ps = sem("hist_ps")
    hist_add = sem("hist_add")
    hp = psum[0:TILES, 0:2, 0:P]

    def hot_pair(dve, i, half, signal):
        cols = bass.ds(i * RING + half * GROUP, GROUP)
        nc.vector.tensor_tensor(
            ohhi[:, half], iota_row[:, 0:TILES].unsqueeze(1).to_broadcast([P, GROUP, TILES]),
            hi_f[:, cols].unsqueeze(2).to_broadcast([P, GROUP, TILES]), ALU.is_equal).then_inc(signal, 1)
        nc.vector.tensor_tensor(
            oh[:, half], iota_row[:, :].unsqueeze(1).to_broadcast([P, GROUP, P]),
            lo_f[:, cols].unsqueeze(2).to_broadcast([P, GROUP, P]), ALU.is_equal).then_inc(signal, 1)

    def hist_vector(dve):
        dve.sem_inc(hist_add, 2)
        with dve.Fori(0, RANK_ITERS) as i:
            for h in range(2):
                dve.wait_ge(hist_ps, 2 * i + h + 1)
                hot_pair(dve, i, h, hot_ready)
            for h in range(2):
                dve.wait_ge(hist_ps, 2 * i + h + 3)
                dve.wait_ge(hist_add, 2 * i + h + 2)
                nc.vector.tensor_tensor(hist, hist, hp[:, h], ALU.add).then_inc(hist_add, 1)
        dve.wait_ge(hist_add, 2 * RANK_ITERS + 2)

    def hist_tensor(pe):
        pe.sem_inc(hist_ps, 2)
        with pe.Fori(0, RANK_ITERS) as i:
            for h in range(2):
                pe.wait_ge(hot_ready, 4 * i + 2 * h + 2)
                pe.wait_ge(hist_add, 2 * i + h + 1)
                for b in range(GROUP):
                    mm = nc.tensor.matmul(hp[:, h], ohhi[:, h, b], oh[:, h, b],
                                          start=b == 0, stop=b == GROUP - 1)
                mm.then_inc(hist_ps, 1)

    stage_of(vector=hist_vector, tensor=hist_tensor)

    n_f, n_i = small[0:TILES, 0:1], small[0:TILES, 1:2].bitcast(I32)
    sl_i, sl_f = small[0:TILES, 2:3].bitcast(I32), small[0:TILES, 3:4]
    first, end = small[0:TILES, 4:5], small[0:TILES, 5:6]
    nslots_ready = sem("nslots_ready")
    first_ps = sem("first_ps")
    ge_ready = sem("ge_ready")
    tile_ps = sem("tile_ps")

    def layout_vector(dve):
        v, c = nc.vector, v_own.bind(dve)
        c.then(v.reduce_sum(n_f, hist, axis=AX.X))
        c.then(v.tensor_scalar(n_i, n_f, float(P - 1), None, ALU.add))
        c.then(v.tensor_scalar(sl_i, n_i, 7, None, ALU.logical_shift_right))
        v.tensor_copy(sl_f, sl_i).then_inc(nslots_ready, 1)
        c.then(v.tensor_tensor_scan(incl, ones[0:TILES, :], hist, 0.0, ALU.mult, ALU.add))
        dve.wait_ge(nslots_ready, 1)
        dve.wait_ge(first_ps, 1)
        c.step(v.tensor_scalar(first, psum[0:TILES, 0, 0:1], float(P), None, ALU.mult))
        c.then(v.tensor_tensor(end, psum[0:TILES, 0, 0:1], sl_f, ALU.add))
        c.step(v.scalar_tensor_tensor(count, incl, first, hist, ALU.add, ALU.subtract))
        v.tensor_scalar(ge[0:TILES, :], iota_slot[0:TILES, :], end, None, ALU.is_ge).then_inc(ge_ready, 1)
        dve.wait_ge(tile_ps, 1)
        half = SLOTS // 2
        c.then(v.tensor_scalar(tile_f.rearrange("p (a b) -> p a b", a=2), psum[:, 1:3, 0:half],
                               float(TILES - 1), None, ALU.min))
        c.then(v.tensor_copy(tile_i, tile_f[64:65, :]))
        c.then(v.tensor_scalar(tile_f, tile_f, float(P), None, ALU.mult))

    def layout_tensor(pe):
        pe.wait_ge(nslots_ready, 1)
        nc.tensor.matmul(psum[0:TILES, 0, 0:1], lt_tile[:, :], sl_f, start=True, stop=True).then_inc(first_ps, 1)
        pe.wait_ge(ge_ready, 1)
        half = SLOTS // 2
        for k in range(2):
            mm = nc.tensor.matmul(psum[:, 1 + k, 0:half], ones[0:TILES, :],
                                  ge[0:TILES, k * half:(k + 1) * half], start=True, stop=True)
        mm.then_inc(tile_ps, 1)

    stage_of(vector=layout_vector, tensor=layout_tensor)

    rhot = sem("rhot")
    keys_ready = sem("keys_ready")
    hit_ps, hit_sb = sem("hit_ps"), sem("hit_sb")
    look_ps = sem("look_ps")
    looked = sem("looked")
    counted = sem("counted")
    pos_ready = sem("pos_ready")
    swept = sem("swept")

    def rank_vector(dve):
        v = nc.vector
        c = v_own.bind(dve)
        dve.sem_inc(counted, 1)
        dve.sem_inc(looked, 4)
        with dve.Fori(0, RANK_ITERS) as i:
            c.enter(i, 4)
            for h in range(2):
                dve.wait_ge(swept, 2 * i + h + 1)
                hot_pair(dve, i, h, rhot)
                cols = bass.ds(i * RING + h * GROUP, GROUP)
                v.tensor_copy(keyb[:, h], key_f[:, cols]).then_inc(keys_ready, 1)
            for h in range(2):
                dve.wait_ge(keys_ready, 2 * i + 2)
                dve.wait_ge(rhot, 4 * i + 4)
                for b in range(GROUP):
                    n = h * GROUP + b
                    bank = psum[:, n % 2, :]
                    dve.wait_ge(look_ps, i * RING + n + 1)
                    v.tensor_tensor_reduce(out=scrap, in0=bank[:, 0:P], in1=oh[:, h, b], scale=1.0,
                                           scalar=0.0, op0=ALU.mult, op1=ALU.add,
                                           accum_out=base8[:, h, b:b + 1]).then_inc(looked, 1)
                    dve.wait_ge(counted, i * RING + n + 1)
                    v.tensor_tensor(count, count, bank[0:TILES, P:2 * P], ALU.add).then_inc(counted, 1)
                    dve.wait_ge(looked, 2 * (i * RING + n) + 5)
                    v.scalar_tensor_tensor(scrap, bank[:, 2 * P:3 * P], keyb[:, h, b:b + 1], lower[:, :],
                                           ALU.is_equal, ALU.mult,
                                           accum_out=rank8[:, h, b:b + 1]).then_inc(looked, 1)
                    dve.wait_ge(looked, 2 * (i * RING + n) + 6)
                for b in range(GROUP):
                    dve.wait_ge(ring[h * GROUP + b], landed(i - 1))
                c.step(v.tensor_copy(recb[:, h], u_rec[:, bass.ds(i * RING + h * GROUP, GROUP), :]))
                c.then(v.tensor_tensor(posf[:, h], base8[:, h], rank8[:, h], ALU.add))
                v.tensor_copy(posb[:, h], posf[:, h]).then_inc(pos_ready, 1)
        c.leave(RANK_ITERS)

    base8 = wts[:, 3776:3792].rearrange("p (h g) -> p h g", h=2)
    rank8 = wts[:, 3792:3808].rearrange("p (h g) -> p h g", h=2)

    def rank_scalar(act):
        with act.Fori(0, RANK_ITERS) as i:
            for h in range(2):
                for q in range(2):
                    act.wait_ge(hit_ps, 4 * i + 2 * h + q + 1)
                    nc.scalar.copy(ohhit[0:TILES, h, 4 * q:4 * q + 4].rearrange("p g e -> p (g e)"),
                                   psum[0:TILES, 2 + q, :]).then_inc(hit_sb, 1)

    def rank_tensor(pe):
        pe.sem_inc(swept, 2)
        with pe.Fori(0, RANK_ITERS) as i:
            for h in range(2):
                pe.wait_ge(rhot, 4 * i + 2 * h + 2)
                for q in range(2):
                    if h:
                        pe.wait_ge(hit_sb, 4 * i + q + 1)
                    waited(pe, "pe")
                    for b in range(4):
                        mm = nc.tensor.transpose(psum[0:TILES, 2 + q, b * P:(b + 1) * P],
                                                 ohhi[:, h, 4 * q + b], ident[:, :])
                    mm.then_inc(hit_ps, 1)
                pe.wait_ge(hit_sb, 4 * i + 2 * h + 2)
                pe.wait_ge(keys_ready, 2 * i + h + 1)
                for b in range(GROUP):
                    n = h * GROUP + b
                    bank = psum[:, n % 2, :]
                    pe.wait_ge(looked, 2 * (i * RING + n) + 2)
                    pe.wait_ge(counted, i * RING + n + 1)
                    nc.tensor.matmul(bank[:, 0:P], ohhit[0:TILES, h, b], count, start=True, stop=True)
                    nc.tensor.matmul(bank[0:TILES, P:2 * P], ohhi[:, h, b], oh[:, h, b], start=True, stop=True)
                    nc.tensor.matmul(bank[:, 2 * P:3 * P], keyb[:, h, b:b + 1].to_broadcast([P, P]),
                                     ident[:, :], start=True, stop=True).then_inc(look_ps, 1)
                    if b == GROUP - 1:
                        pe.wait_ge(looked, 2 * (i * RING + n) + 6)
                        pe.sem_inc(swept, 1)

    def rank_gpsimd(pool):
        with pool.Fori(0, RANK_ITERS) as i:
            for b in range(RING):
                if b % GROUP == 0:
                    pool.wait_ge(pos_ready, 2 * i + b // GROUP + 1)
                    waited(pool)
                nc.gpsimd.indirect_dma_start(
                    rec, bass.IndirectOffsetOnAxis(posb[:, b // GROUP, b % GROUP:b % GROUP + 1], 0),
                    recb[:, b // GROUP, b % GROUP, :], None).then_inc(ring[b], 16)
        for b in range(RING):
            pool.wait_ge(ring[b], landed(RANK_ITERS - 1))

    stage_of(vector=rank_vector, scalar=rank_scalar, tensor=rank_tensor, gpsimd=rank_gpsimd)

    rs = kh_i[:, 0:2 * SLOTS].rearrange("p (k e w) -> p k e w", k=NBLK, w=2)
    rsf = kh[:, 2 * SLOTS:4 * SLOTS].rearrange("p (k e w) -> p k e w", k=NBLK, w=2)
    flag_f = kh[:, 4 * SLOTS:5 * SLOTS].rearrange("p (k e) -> p k e", k=NBLK)
    last_f = kh[:, 5 * SLOTS:6 * SLOTS].rearrange("p (k e) -> p k e", k=NBLK)
    word0, word1 = kh[:, 6 * SLOTS:7 * SLOTS], kh[:, 7 * SLOTS:8 * SLOTS]
    word0_i, typ_i = wts[:, 0:SLOTS].bitcast(I32), wts[:, SLOTS:2 * SLOTS].bitcast(I32)
    flag_u = wts[:, 2 * SLOTS:3 * SLOTS].bitcast(U8)[:, 0:SLOTS].rearrange("p (k e) -> p k e", k=NBLK)
    assert 8 * SLOTS <= 10 * COLS + SLOTS
    records_in = sem("records_in")
    flags_set = sem("flags_set")
    flags_out = sem("flags_out")
    starts_in = sem("starts_in")
    words_f = sem("words_f")
    turned = sem("turned")

    def reload_sync(sp):
        sp.dma_start(rs.rearrange("p k e w -> p k (e w)"),
                     rec.rearrange("(k s e) w -> s k (e w)", s=P, e=P)).then_inc(records_in, 16)
        sp.wait_ge(flags_set, 1)
        sp.dma_start(flags.rearrange("(k s) e -> s k e", s=P), flag_u).then_inc(flags_out, 16)
        sp.wait_ge(flags_out, 16)
        for h in range(HEADS):
            sp.dma_start(starts[h * GROUP:(h + 1) * GROUP, :, :],
                         flags.rearrange("(g s) e -> s g e", s=GROUP)).then_inc(starts_in, 16)
        sp.wait_ge(starts_in, 16 * HEADS)

    def reload_vector(dve):
        v, c = nc.vector, v_own.bind(dve)
        dve.wait_ge(records_in, 16)
        c.step(v.tensor_copy(rsf.rearrange("p k e w -> p (k e w)"), rs.rearrange("p k e w -> p (k e w)")))
        c.step(v.memset(flag_f[:, :, 0:1], 1.0))
        c.then(v.memset(last_f[:, :, P - 1:P], 1.0))
        c.step(v.tensor_tensor(flag_f[:, :, 1:P], rsf[:, :, 1:P, 1], rsf[:, :, 0:P - 1, 1], ALU.not_equal))
        v.tensor_tensor(last_f[:, :, 0:P - 1], rsf[:, :, 0:P - 1, 1], rsf[:, :, 1:P, 1],
                        ALU.not_equal).then_inc(words_f, 1)
        c.wait()
        v.tensor_copy(flag_u, flag_f).then_inc(flags_set, 1)
        dve.wait_ge(turned, 3 * NBLK)
        for w, to in enumerate((word0, word1, last[:, :])):
            c.step(v.tensor_copy(to[:, 0:4 * P], psum[:, w, 0:4 * P]))
            c.step(v.tensor_copy(to[:, 4 * P:], psum[:, w + 3, 0:(NBLK - 4) * P]))
        c.wait()
        c.step(v.tensor_tensor(dl[:, :], word1, tile_f, ALU.subtract))
        c.then(v.tensor_copy(word0_i, word0))
        c.step(v.tensor_scalar(src_i[:, :], word0_i, 8191, None, ALU.bitwise_and))
        c.then(v.tensor_scalar(typ_i, word0_i, 13, None, ALU.logical_shift_right))
        c.then(v.scalar_tensor_tensor(rel_i[:, :], src_i[:, :], float(RELS), typ_i, ALU.mult, ALU.add))

    def reload_tensor(pe):
        pe.wait_ge(words_f, 1)
        for w in range(3):
            for k in range(NBLK):
                block = last_f[:, k, :] if w == 2 else rsf[:, k, :, w]
                nc.tensor.transpose(psum[:, w + 3 * (k // 4), (k % 4) * P:(k % 4 + 1) * P],
                                    block, ident[:, :]).then_inc(turned, 1)

    stage_of(sync=reload_sync, vector=reload_vector, tensor=reload_tensor)

    TI = TILES // 2
    flat = rows[:, :, :].rearrange("p r w -> p (r w)")
    place = [0]

    def carve(*shape, part=P, of=flat):
        size = int(np.prod(shape))
        at = place[0]
        place[0] += 2 * size
        assert place[0] <= of.shape[1]
        return [of[0:part, at + p * size:at + (p + 1) * size] for p in range(2)]

    xb, nb, ht = carve(D), carve(D), carve(D)
    stats, mv = carve(6), carve(2)
    ve, sd, rsd, zinv = carve(1), carve(1), carve(1), carve(HEADS)
    common_end = place[0]
    x_in, out_a, out_b = ([sem(f"{n}{p}") for p in range(2)] for n in ("x_in", "out_a", "out_b"))
    var_ready, std_ready, norm_ready = sem("var_ready"), sem("std_ready"), sem("norm_ready")
    turn_ps, ht_ready, proj_ps = sem("turn_ps"), sem("ht_ready"), sem("proj_ps")
    act_evac, dve_evac = sem("act_evac"), sem("dve_evac")
    a_ready, b_ready = sem("a_ready"), sem("b_ready")

    def give(eng, n, *sems):
        for s in sems:
            eng.sem_inc(s, n)

    def load_x(sp, i, t, table):
        for p in range(2):
            sp.wait_ge(b_ready, prev(i, p))
            sp.dma_start(xb[p], tile_rows(table, t + p)).then_inc(x_in[p], 16)

    def stats_of(dve, c, i, x):
        for p in range(2):
            c.then(nc.vector.bn_stats(stats[p], x[p]))
            waited(dve, "dve")
            c.then(nc.vector.bn_aggr(mv[p], stats[p]))
            nc.vector.tensor_scalar_add(ve[p], mv[p][:, 1:2], 1e-5).then_inc(var_ready, 1)

    def roots(act, i):
        for p in range(2):
            act.wait_ge(var_ready, now(i, p))
            nc.scalar.activation(sd[p], ve[p], ACT.Sqrt).then_inc(std_ready, 1)

    def normalise(dve, c, i, x):
        for p in range(2):
            dve.wait_ge(std_ready, now(i, p))
            c.then(nc.vector.reciprocal(rsd[p], sd[p]))
            nc.vector.tensor_scalar(nb[p], x[p], mv[p][:, 0:1], rsd[p], ALU.subtract,
                                    ALU.mult).then_inc(norm_ready, 1)

    def turn(pe, i, ip):
        for p in range(2):
            pe.wait_ge(norm_ready, now(i, p))
            for k in range(2):
                mm = nc.tensor.transpose(psum[:, p, k * P:(k + 1) * P], nb[p][:, k * P:(k + 1) * P], ident[:, :])
            mm.then_inc(turn_ps, 1)

    def turned_relu(act, ip):
        for p in range(2):
            act.wait_ge(turn_ps, now(ip, p))
            nc.scalar.activation(ht[p], psum[:, p, 0:D], ACT.Relu).then_inc(ht_ready, 1)

    def project(to, p, w, width, at, size, bias=None):
        for k in range(2):
            mm = nc.tensor.matmul(to, ht[p][:, k * P:(k + 1) * P], w[:, k * width + at:k * width + at + size],
                                  start=k == 0, stop=bias is None and k == 1)
        if bias is not None:
            mm = nc.tensor.matmul(to, ones[0:1, :], bias, start=False, stop=True)
        return mm

    def load_weights(sp, *pairs):
        for to, of in pairs:
            sp.dma_start(to, of).then_inc(weights_sem, 16)

    def kmajor(w, k):
        return w.rearrange("(k p) n -> p k n", p=P)

    W0 = 3 * D
    qv = carve(2 * D)
    scale_q = 1.0 / float(np.sqrt(DH))

    def l0_sync(sp):
        load_weights(sp, (wts[:, 0:2 * W0].rearrange("p (k n) -> p k n", k=2), kmajor(a["w0"], 2)),
                     (brow[:, 0:W0], a["b0"]))
        with sp.Fori(0, TI) as i:
            load_x(sp, i, 2 * i, a["x"])
            for p in range(2):
                sp.wait_ge(a_ready, now(i, p))
                sp.dma_start(tile_rows(qv_tab, 2 * i + p), qv[p]).then_inc(out_a[p], 16)
        for p in range(2):
            sp.wait_ge(out_a[p], 16 * (TI + 1))

    def l0_vector(dve):
        c = v_own.bind(dve)
        c.then(nc.vector.memset(mnode[:, :], -BIG))
        with dve.Fori(0, TI) as i:
            c.enter(i, 6)
            for p in range(2):
                dve.wait_ge(x_in[p], 16 * (i + 2))
            stats_of(dve, c, i, xb)
            normalise(dve, c, i, xb)
            for p in range(2):
                dve.wait_ge(proj_ps, now(i, p))
                nc.vector.tensor_copy(kh3[:, bass.ds(2 * i + p, 1), 0:D].rearrange("p a f -> p (a f)"),
                                      psum[:, 4 + p, 0:D]).then_inc(dve_evac, 1)
                dve.wait_ge(norm_ready, now(i, p))
                dve.sem_inc(b_ready, 1)
        c.leave(TI)

    def l0_scalar(act):
        with act.Fori(0, TI) as i:
            roots(act, i)
            turned_relu(act, i)
            for p in range(2):
                act.wait_ge(proj_ps, now(i, p))
                act.wait_ge(out_a[p], 16 * (i + 1))
                nc.scalar.mul(qv[p][:, 0:D], psum[:, 2 + p, 0:D], scale_q)
                nc.scalar.copy(qv[p][:, D:], psum[:, 2 + p, D:2 * D]).then_inc(a_ready, 1)

    def l0_tensor(pe):
        pe.wait_ge(weights_sem, 32)
        with pe.Fori(0, TI) as i:
            turn(pe, i, i)
            for p in range(2):
                pe.wait_ge(ht_ready, now(i, p))
                pe.wait_ge(a_ready, prev(i, p))
                pe.wait_ge(dve_evac, prev(i, p))
                project(psum[:, 2 + p, :], p, wts, W0, 0, 2 * D, brow[:, 0:2 * D])
                project(psum[:, 4 + p, 0:D], p, wts, W0, 2 * D, D, brow[:, 2 * D:3 * D]).then_inc(proj_ps, 1)

    stage_of(sync=l0_sync, vector=l0_vector, scalar=l0_scalar, tensor=l0_tensor)

    idx_ready = sem("idx_ready")
    oh_ready, agg_done, acc_done = sem("oh_ready"), sem("agg_done"), sem("acc_done")

    def use(j):
        return j + RANK_ITERS

    def fetch_indices(pool, j, s0, h, table_idx):
        pool.wait_ge(ring[h * GROUP + GROUP - 1], landed(use(j) - 1))
        nc.gpsimd.tensor_copy(idx[:, h * GROUP:(h + 1) * GROUP],
                              table_idx[:, bass.ds(s0 + h * GROUP, GROUP)]).then_inc(idx_ready, 1)
        pool.wait_ge(idx_ready, 2 * j + h + 1)

    def gather(pool, j, b, table, width):
        pool.wait_ge(agg_done, prev(j, b, RING))
        waited(pool)
        nc.gpsimd.indirect_dma_start(rows[:, b, 0:width], None, table,
                                     bass.IndirectOffsetOnAxis(idx[:, b:b + 1], 0)).then_inc(ring[b], 16)

    def slot_tiles(engine, s0):
        _, tiles = nc.values_load_multi_w_load_instructions(
            tile_i[0:1, bass.ds(s0, RING)], engines=[engine], min_val=0, max_val=TILES - 1,
            skip_runtime_bounds_check_because="a minimum with TILES - 1 made them")
        return tiles

    def one_hots(dve, j, s0, h):
        dve.wait_ge(agg_done, prev(j, h * GROUP + GROUP - 1, RING))
        nc.vector.tensor_tensor(
            oh[:, h], iota_row[:, :].unsqueeze(1).to_broadcast([P, GROUP, P]),
            dl[:, bass.ds(s0 + h * GROUP, GROUP)].unsqueeze(2).to_broadcast([P, GROUP, P]),
            ALU.is_equal).then_inc(oh_ready, 1)

    def aggregate(pe, j, b, at, width):
        pe.wait_ge(acc_done, now(j, b - 2, RING))
        nc.tensor.matmul(psum[:, 6 + b % 2, 0:width], oh[:, b // GROUP, b % GROUP], rows[:, b, at:at + width],
                         start=True, stop=True).then_inc(agg_done, 1)

    def accumulate(dve, j, b, tile, width):
        dve.wait_ge(agg_done, now(j, b, RING))
        dve.wait_ge(acc_done, now(j, b - 1, RING))
        to = acc3[:, bass.ds(tile, 1), 0:width].rearrange("p a f -> p (a f)")
        nc.vector.tensor_tensor(to, to, psum[:, 6 + b % 2, 0:width], ALU.add).then_inc(acc_done, 1)

    oht_ps, oht_sb = sem("oht_ps"), sem("oht_sb")
    key_ps, pair_used, adst_ps = sem("key_ps"), sem("pair_used"), sem("adst_ps")
    score_ready, score_ps, seg_ready = sem("score_ready"), sem("score_ps"), sem("seg_ready")
    scan_ready, back_ps, best_ready = sem("scan_ready"), sem("back_ps"), sem("best_ready")
    best_ps, max_ready, max_ps = sem("best_ps"), sem("max_ready"), sem("max_ps")
    fall_ready, alpha_ready = sem("fall_ready"), sem("alpha_ready")
    shifted, weight_ready, msg_ready = sem("shifted"), sem("weight_ready"), sem("msg_ready")

    def att_place(*shape, part=P, count=2):
        size = int(np.prod(shape))
        at = att_at[0]
        att_at[0] += count * size
        assert att_at[0] <= wts.shape[1]
        return [wts[0:part, at + k * size:at + (k + 1) * size] for k in range(count)]

    att_at = [0]
    GH = GROUP * HEADS
    score = att_place(GH)
    shift = att_place(GH)
    best = att_place(GROUP * (HEADS + 1))
    seg = att_place(P, part=GH)
    run = att_place(P, part=GH)
    pen = att_place(GROUP)
    mloc = att_place(GH)
    mold = att_place(HEADS)
    alpha = att_place(HEADS)

    def hs(ap):
        return ap.rearrange("p (h s) -> p h s", s=GROUP)

    def sh(ap):
        return ap.rearrange("p (s h) -> p s h", h=HEADS)

    ps_turn = lambda q: psum[:, q, :]
    ps_pair = lambda q: psum[:, 2 + q % 2, :]
    ps_score = psum[0:GH, 4, 0:P]
    ps_back = psum[:, 4, P:P + GH]
    ps_best = psum[:, 4, 256:256 + GROUP * 9].rearrange("p (s c) -> p s c", c=9)
    ps_max = psum[:, 5, 0:GH]
    ps_tgt = psum[:, 5, GH:2 * GH]

    def attention(k, ka, dot, table, width, vat):
        lo = k * ITERS
        shift_j = lo - ka * ITERS

        def on_gpsimd(pool):
            with pool.Fori(lo, lo + ITERS) as j:
                for h in range(2):
                    fetch_indices(pool, j, (j - lo) * RING, h, src_i)
                    for b in range(h * GROUP, (h + 1) * GROUP):
                        gather(pool, j, b, table, width)

        def on_tensor(pe):
            t = nc.tensor
            with pe.Fori(lo, lo + ITERS) as j:
                i = j - shift_j
                tiles = slot_tiles(PE, (j - lo) * RING)
                for h in range(2):
                    pe.wait_ge(oh_ready, 2 * j + h + 1)
                    for q in range(2):
                        pe.wait_ge(oht_sb, now(i, 2 * h + q - 2, 4))
                        for b in range(4):
                            mm = t.transpose(ps_turn(q)[:, b * P:(b + 1) * P], oh[:, h, 4 * q + b], ident[:, :])
                        mm.then_inc(oht_ps, 1)
                    pe.wait_ge(oht_sb, now(i, 2 * h + 1, 4))
                    if dot:
                        for q in range(4):
                            pe.wait_ge(pair_used, now(i, 4 * h + q - 2, 8))
                            for b in range(2):
                                s = 2 * q + b
                                tile = kh3[:, bass.ds(tiles[h * GROUP + s], 1), 0:D].rearrange("p a f -> p (a f)")
                                mm = t.matmul(ps_pair(q)[:, b * D:(b + 1) * D], oht[:, h, s], tile,
                                              start=True, stop=True)
                            mm.then_inc(key_ps, 1)
                    else:
                        pe.wait_ge(score_ready, now(i, h - 1))
                        for s in range(GROUP):
                            tile = adst3[:, bass.ds(tiles[h * GROUP + s], 1), :].rearrange("p a f -> p (a f)")
                            mm = t.matmul(sh(ps_tgt)[:, s, :], oht[:, h, s], tile, start=True, stop=True)
                        mm.then_inc(adst_ps, 1)
                    pe.wait_ge(score_ready, now(i, h))
                    waited(pe, "pe")
                    t.transpose(ps_score, score[h], ident[:, :]).then_inc(score_ps, 1)
                    pe.wait_ge(scan_ready, now(i, h))
                    waited(pe, "pe")
                    t.transpose(ps_back, run[h], ident[0:GH, 0:GH]).then_inc(back_ps, 1)
                    pe.wait_ge(best_ready, now(i, h))
                    for s in range(GROUP):
                        mm = t.matmul(ps_best[:, s, :], oh[:, h, s],
                                      best[h].rearrange("p (c s) -> p c s", s=GROUP)[:, :, s],
                                      start=True, stop=True)
                    mm.then_inc(best_ps, 1)
                    pe.wait_ge(max_ready, now(i, h))
                    for s in range(GROUP):
                        tile = m3[:, bass.ds(tiles[h * GROUP + s], 1), :].rearrange("p a f -> p (a f)")
                        mm = t.matmul(sh(ps_max)[:, s, :], oht[:, h, s], tile, start=True, stop=True)
                    mm.then_inc(max_ps, 1)
                    for s in range(GROUP):
                        if s % 4 == 0:
                            pe.wait_ge(msg_ready, now(i, 2 * h + s // 4, 4))
                        aggregate(pe, j, h * GROUP + s, vat, ACCW)

        def on_scalar(act):
            with act.Fori(lo, lo + ITERS) as j:
                i = j - shift_j
                for h in range(2):
                    for q in range(2):
                        act.wait_ge(oht_ps, now(i, 2 * h + q, 4))
                        nc.scalar.copy(oht[:, h, 4 * q:4 * q + 4].rearrange("p g e -> p (g e)"),
                                       ps_turn(q)).then_inc(oht_sb, 1)
                    act.wait_ge(scan_ready, prev(i, h))
                    nc.scalar.mul(seg[h], starts[:, bass.ds(2 * (j - lo) + h, 1), :].rearrange("p a e -> p (a e)"),
                                  -BIG).then_inc(seg_ready, 1)
                    act.wait_ge(fall_ready, now(i, h))
                    nc.scalar.activation(alpha[h], mold[h], ACT.Exp).then_inc(alpha_ready, 1)
                    act.wait_ge(shifted, now(i, h))
                    nc.scalar.activation(rows[:, h * GROUP:(h + 1) * GROUP, vat + D:vat + ACCW], sh(shift[h]),
                                         ACT.Exp).then_inc(weight_ready, 1)

        def on_vector(dve):
            v, c = nc.vector, v_own.bind(dve)
            c.then(v.memset(acc[:, :], 0.0))
            with dve.Fori(lo, lo + ITERS) as j:
                i = j - shift_j
                s0 = (j - lo) * RING
                c.enter(j - lo, ATT_STEPS[dot])
                tiles = slot_tiles(DVE, s0)
                for h in range(2):
                    at = h * GROUP
                    group = rows[:, at:at + GROUP, :]
                    one_hots(dve, j, s0, h)
                    for b in range(GROUP):
                        dve.wait_ge(ring[at + b], landed(use(j)))
                    if dot:
                        for q in range(4):
                            dve.wait_ge(key_ps, now(i, 4 * h + q, 8))
                            pair = rows[:, at + 2 * q:at + 2 * q + 2, 0:D]
                            v.tensor_tensor(pair, ps_pair(q).rearrange("p (s f) -> p s f", s=2), pair,
                                            ALU.mult).then_inc(pair_used, 1)
                        dve.wait_ge(pair_used, now(i, 4 * h + 3, 8))
                        v.tensor_reduce(score[h].rearrange("p (h s) -> p s h", s=GROUP),
                                        group[:, :, 0:D].rearrange("p s (h d) -> p s h d", h=HEADS),
                                        axis=AX.X, op=ALU.add).then_inc(score_ready, 1)
                    else:
                        dve.wait_ge(adst_ps, now(j - lo, h))
                        c.then(v.tensor_tensor(score[h].rearrange("p (h s) -> p s h", s=GROUP),
                                               group[:, :, D:ACCW], sh(ps_tgt), ALU.add))
                        v.scalar_tensor_tensor(score[h], score[h], 0.2, score[h], ALU.mult,
                                               ALU.max).then_inc(score_ready, 1)
                    dve.wait_ge(score_ps, now(i, h))
                    dve.wait_ge(seg_ready, now(i, h))
                    v.tensor_tensor_scan(run[h], seg[h], ps_score, -BIG, ALU.add, ALU.max).then_inc(scan_ready, 1)
                    lastg = last[:, bass.ds(s0 + at, GROUP)]
                    c.step(v.tensor_copy(best[h][:, GH:], lastg))
                    dve.wait_ge(back_ps, now(i, h))
                    v.tensor_tensor(hs(best[h][:, 0:GH]), hs(ps_back), lastg.unsqueeze(1).to_broadcast([P, HEADS, GROUP]),
                                    ALU.mult).then_inc(best_ready, 1)
                    dve.wait_ge(best_ps, now(i, h))
                    c.then(v.tensor_scalar(pen[h].unsqueeze(2), ps_best[:, :, HEADS:HEADS + 1], -1.0, BIG,
                                           ALU.add, ALU.mult))
                    c.step(v.tensor_tensor(sh(mloc[h]), ps_best[:, :, 0:HEADS],
                                           pen[h].unsqueeze(2).to_broadcast([P, GROUP, HEADS]), ALU.add))
                    tile0 = m3[:, bass.ds(tiles[at], 1), :].rearrange("p a f -> p (a f)")
                    c.then(v.tensor_copy(mold[h], tile0))
                    for s in range(GROUP):
                        tile = m3[:, bass.ds(tiles[at + s], 1), :].rearrange("p a f -> p (a f)")
                        c.then(v.tensor_tensor(tile, tile, sh(mloc[h])[:, s, :], ALU.max))
                    dve.sem_inc(max_ready, 1)
                    v.tensor_tensor(mold[h], mold[h], tile0, ALU.subtract).then_inc(fall_ready, 1)
                    dve.wait_ge(max_ps, now(i, h))
                    v.tensor_tensor(sh(shift[h]), score[h].rearrange("p (h s) -> p s h", s=GROUP), sh(ps_max),
                                    ALU.subtract).then_inc(shifted, 1)
                    dve.wait_ge(alpha_ready, now(i, h))
                    acc0 = acc3[:, bass.ds(tiles[at], 1), :].rearrange("p a f -> p (a f)")
                    dve.wait_ge(acc_done, now(j, at - 1, RING))
                    c.step(v.tensor_tensor(acc0[:, 0:D].rearrange("p (h d) -> p h d", h=HEADS),
                                           acc0[:, 0:D].rearrange("p (h d) -> p h d", h=HEADS),
                                           alpha[h].unsqueeze(2).to_broadcast([P, HEADS, DH]), ALU.mult))
                    c.then(v.tensor_tensor(acc0[:, D:ACCW], acc0[:, D:ACCW], alpha[h], ALU.mult))
                    dve.wait_ge(weight_ready, now(i, h))
                    for q in range(2):
                        val = group[:, 4 * q:4 * q + 4, vat:vat + D].rearrange("p s (h d) -> p s h d", h=HEADS)
                        wgt = group[:, 4 * q:4 * q + 4, vat + D:vat + ACCW]
                        v.tensor_tensor(val, val, wgt.unsqueeze(3).to_broadcast([P, 4, HEADS, DH]),
                                        ALU.mult).then_inc(msg_ready, 1)
                    for s in range(GROUP):
                        accumulate(dve, j, at + s, tiles[at + s], ACCW)
            c.leave(ITERS)
            dve.wait_ge(acc_done, now(lo + ITERS - 1, RING - 1, RING))

        stage_of(gpsimd=on_gpsimd, tensor=on_tensor, scalar=on_scalar, vector=on_vector)

    ATT_STEPS = {True: 2 * (1 + 1 + 2 + GROUP + 2), False: 2 * (1 + 1 + 1 + 2 + GROUP + 2)}
    attention(0, 0, True, qv_tab, 2 * D, D)

    place[0] = common_end
    x1b, h1f = carve(D), carve(2)

    def l0e_sync(sp):
        with sp.Fori(TI, 2 * TI) as i:
            t = 2 * (i - TI)
            load_x(sp, i, t, a["x"])
            for p in range(2):
                sp.wait_ge(a_ready, now(i, p))
                sp.dma_start(tile_rows(x1_tab, t + p), x1b[p]).then_inc(out_a[p], 16)
            for p in range(2):
                sp.wait_ge(b_ready, now(i, p))
                sp.dma_start(tile_rows(h1_tab, t + p),
                             kh3[:, bass.ds(t + p, 1), 0:D].rearrange("p a f -> p (a f)")).then_inc(out_b[p], 16)
        for p in range(2):
            sp.wait_ge(out_a[p], 16 * (2 * TI + 1))
            sp.wait_ge(out_b[p], 16 * (TI + 1))

    def l0e_vector(dve):
        v, c = nc.vector, v_own.bind(dve)
        c.then(v.memset(kh3[:, :, D:KHW], 1.0))
        with dve.Fori(TI, 2 * TI) as i:
            c.enter(i - TI, 12)
            t = 2 * (i - TI)
            for p in range(2):
                total = acc3[:, bass.ds(t + p, 1), :].rearrange("p a f -> p (a f)")
                c.then(v.tensor_scalar_max(zinv[p], total[:, D:ACCW], 1e-16))
                c.then(v.reciprocal(zinv[p], zinv[p]))
                dve.wait_ge(out_a[p], 16 * (i + 1))
                c.then(v.tensor_tensor(x1b[p].rearrange("p (h d) -> p h d", h=HEADS),
                                       total[:, 0:D].rearrange("p (h d) -> p h d", h=HEADS),
                                       zinv[p].unsqueeze(2).to_broadcast([P, HEADS, DH]), ALU.mult))
                dve.wait_ge(x_in[p], 16 * (i + 2))
                v.tensor_tensor(x1b[p], x1b[p], xb[p], ALU.add).then_inc(a_ready, 1)
                dve.wait_ge(a_ready, now(i, p))
            stats_of(dve, c, i, x1b)
            normalise(dve, c, i, x1b)
            for p in range(2):
                dve.wait_ge(norm_ready, now(i, p))
                v.tensor_scalar_max(kh3[:, bass.ds(t + p, 1), 0:D].rearrange("p a f -> p (a f)"), nb[p],
                                    0.0).then_inc(b_ready, 1)
        c.leave(TI)

    def l0e_scalar(act):
        with act.Fori(TI, 2 * TI) as i:
            roots(act, i)

    stage_of(sync=l0e_sync, vector=l0e_vector, scalar=l0e_scalar)

    OUT_AT = ROW - SUMW
    srcb = [wts[:, h * GROUP:(h + 1) * GROUP] for h in range(2)]
    dup = [wts[:, 16 + h * GROUP:16 + (h + 1) * GROUP] for h in range(2)]
    away = [wts[:, 32 + h * GROUP:32 + (h + 1) * GROUP] for h in range(2)]
    scrap1 = wts[:, 64:64 + P]
    src_f = wts[:, 2560:2560 + SLOTS]
    merged = wts[:, 256:256 + 2 * GROUP * P].rearrange("p (h g e) -> p h g e", h=2, g=GROUP)
    srcb_ready, row_ps, same_ready = sem("srcb_ready"), sem("row_ps"), sem("same_ready")
    merged_ps, merged_sb = sem("merged_ps"), sem("merged_sb")
    out_ps, out_sb, idx2_ready = sem("out_ps"), sem("out_sb"), sem("idx2_ready")
    USES = RING // TABLES
    same = oht
    K1 = ITERS

    def l1_gpsimd(pool):
        pool.wait_ge(ones_set, 1)
        with pool.Fori(K1, K1 + ITERS) as j:
            i = j - K1
            for h in range(2):
                fetch_indices(pool, j, i * RING, h, src_i)
                for b in range(h * GROUP, (h + 1) * GROUP):
                    gather(pool, j, b, h1_tab, D)
                for b in range(h * GROUP, (h + 1) * GROUP):
                    k, n = b % TABLES, b // TABLES
                    pool.wait_ge(out_sb, now(i, b, RING))
                    pool.wait_ge(idx2_ready, now(i, h))
                    pool.wait_ge(table_done[k], ZEROED + 16 * (i * USES + n))
                    waited(pool)
                    nc.gpsimd.indirect_dma_start(
                        src_sum[k], bass.IndirectOffsetOnAxis(idx2[:, b:b + 1], 0),
                        rows[:, b, OUT_AT:OUT_AT + SUMW], None, compute_op=ALU.add).then_inc(table_done[k], 16)
        for k in range(TABLES):
            pool.wait_ge(table_done[k], ZEROED + 16 * ITERS * USES)

    def l1_vector(dve):
        v, c = nc.vector, v_own.bind(dve)
        v.memset(acc[:, :], 0.0)
        v.memset(rows[:, :, :], 1.0)
        c.then(v.tensor_copy(src_f, src_i[:, :]))
        dve.sem_inc(ones_set, 1)
        with dve.Fori(K1, K1 + ITERS) as j:
            i = j - K1
            c.enter(i, 2 * (GROUP + 2))
            s0 = i * RING
            tiles = slot_tiles(DVE, s0)
            for h in range(2):
                one_hots(dve, j, s0, h)
                for q in range(2):
                    dve.wait_ge(out_ps, prev(i, h * GROUP + 4 * q + 3, RING))
                v.tensor_copy(srcb[h], src_f[:, bass.ds(s0 + h * GROUP, GROUP)]).then_inc(srcb_ready, 1)
                dve.wait_ge(srcb_ready, now(i, h))
                for q in range(2):
                    dve.wait_ge(row_ps, now(i, 2 * h + q, 4))
                    v.tensor_tensor(same[:, h, 4 * q:4 * q + 4], psum[:, q, :].rearrange("p (g e) -> p g e", g=4),
                                    srcb[h][:, 4 * q:4 * q + 4].unsqueeze(2).to_broadcast([P, 4, P]),
                                    ALU.is_equal).then_inc(same_ready, 1)
                for q in range(2):
                    dve.wait_ge(same_ready, now(i, 2 * h + q, 4))
                    for b in range(4):
                        c.then(v.tensor_tensor_reduce(out=scrap1, in0=same[:, h, 4 * q + b], in1=lower[:, :],
                                                      scale=1.0, scalar=0.0, op0=ALU.mult, op1=ALU.add,
                                                      accum_out=dup[h][:, 4 * q + b:4 * q + b + 1]))
                c.then(v.tensor_scalar(away[h], srcb[h], -1.0, spare[:, :], ALU.mult, ALU.add))
                c.then(v.scalar_tensor_tensor(away[h], dup[h], 1.0, away[h], ALU.min, ALU.mult))
                for k in range(TABLES):
                    dve.wait_ge(table_done[k], ZEROED + 16 * ((i - 1) * USES + 2 * h + 2))
                v.tensor_tensor(idx2[:, h * GROUP:(h + 1) * GROUP], away[h], srcb[h], ALU.add).then_inc(idx2_ready, 1)
                for b in range(h * GROUP, (h + 1) * GROUP):
                    accumulate(dve, j, b, tiles[b], KHW)
        c.leave(ITERS)
        dve.wait_ge(acc_done, now(K1 + ITERS - 1, RING - 1, RING))

    def l1_scalar(act):
        act.wait_ge(ones_set, 1)
        with act.Fori(K1, K1 + ITERS) as j:
            i = j - K1
            for h in range(2):
                for q in range(2):
                    act.wait_ge(merged_ps, now(i, 2 * h + q, 4))
                    nc.scalar.copy(merged[:, h, 4 * q:4 * q + 4].rearrange("p g e -> p (g e)"),
                                   psum[:, 2 + q, :]).then_inc(merged_sb, 1)
                for b in range(h * GROUP, (h + 1) * GROUP):
                    act.wait_ge(out_ps, now(i, b, RING))
                    act.wait_ge(table_done[b % TABLES], ZEROED + 16 * ((i - 1) * USES + b // TABLES + 1))
                    nc.scalar.copy(rows[:, b, OUT_AT:OUT_AT + KHW], psum[:, 4 + b % 2, 0:KHW]).then_inc(out_sb, 1)

    def l1_tensor(pe):
        t = nc.tensor
        pe.wait_ge(ones_set, 1)
        with pe.Fori(K1, K1 + ITERS) as j:
            i = j - K1
            tiles = slot_tiles(PE, i * RING)
            for h in range(2):
                pe.wait_ge(srcb_ready, now(i, h))
                for q in range(2):
                    pe.wait_ge(same_ready, now(i, 2 * h + q - 2, 4))
                    for b in range(4):
                        mm = t.matmul(psum[:, q, b * P:(b + 1) * P],
                                      srcb[h][:, 4 * q + b:4 * q + b + 1].to_broadcast([P, P]), ident[:, :],
                                      start=True, stop=True)
                    mm.then_inc(row_ps, 1)
                pe.wait_ge(oh_ready, 2 * j + h + 1)
                for q in range(2):
                    pe.wait_ge(same_ready, now(i, 2 * h + q, 4))
                    pe.wait_ge(merged_sb, now(i, 2 * h + q - 2, 4))
                    for b in range(4):
                        mm = t.matmul(psum[:, 2 + q, b * P:(b + 1) * P], oh[:, h, 4 * q + b],
                                      same[:, h, 4 * q + b], start=True, stop=True)
                    mm.then_inc(merged_ps, 1)
                for b in range(GROUP):
                    n = h * GROUP + b
                    if b % 4 == 0:
                        pe.wait_ge(merged_sb, now(i, 2 * h + b // 4, 4))
                    pe.wait_ge(out_sb, now(i, n - 2, RING))
                    tile = kh3[:, bass.ds(tiles[n], 1), :].rearrange("p a f -> p (a f)")
                    t.matmul(psum[:, 4 + b % 2, 0:KHW], merged[:, h, b], tile, start=True, stop=True).then_inc(out_ps, 1)
                for b in range(GROUP):
                    n = h * GROUP + b
                    pe.wait_ge(ring[n], landed(use(j)))
                    aggregate(pe, j, n, 0, KHW)

    ones_set = sem("ones_set")
    stage_of(gpsimd=l1_gpsimd, vector=l1_vector, scalar=l1_scalar, tensor=l1_tensor)

    place[0] = 0
    gx, gsum, gin, gout, gh, ght = (carve(n) for n in (D, TABLES * SUMW, D, D, D, D))
    gate, cand, cnt, cmax, cinv, cone = (carve(n) for n in (2 * D, D, 2, 2, 2, 2))
    gind = carve(2 * P, part=1)
    oh_flat, place[0] = oh[:, :, :, :].rearrange("p h g e -> p (h g e)"), 0
    gt, gct = carve(4 * P, of=oh_flat), carve(4 * P, of=oh_flat)
    w_in, w_out = wts[:, 0:2 * D], wts[:, 2 * D:4 * D]
    w_ih, w_hh = wts[:, 4 * D:16 * D], wts[:, 16 * D:22 * D]
    b_in, b_out, b_ih, b_hh = brow[:, 0:D], brow[:, D:2 * D], brow[:, 2 * D:5 * D], brow[:, 5 * D:8 * D]
    g_in = [sem("g_in0"), sem("g_in1")]
    g_out = [sem("g_out0"), sem("g_out1")]
    pre_ready, gt_ps, gt_sb, conv_ps, conv_sb = (sem(n) for n in ("pre_ready", "gt_ps", "gt_sb", "conv_ps", "conv_sb"))
    gate_ps, gate_sb, new_ready, cand_ready, x2_ready = (
        sem(n) for n in ("gate_ps", "gate_sb", "new_ready", "cand_ready", "x2_ready"))

    def gru_sync(sp):
        load_weights(sp, (w_in.rearrange("p (k n) -> p k n", k=2), kmajor(a["w_in"], 2)),
                     (w_out.rearrange("p (k n) -> p k n", k=2), kmajor(a["w_out"], 2)),
                     (w_ih.rearrange("p (k n) -> p k n", k=4), kmajor(a["w_ih"], 4)),
                     (w_hh.rearrange("p (k n) -> p k n", k=2), kmajor(a["w_hh"], 2)),
                     (brow[:, 0:8 * D], a["b1"]))
        with sp.Fori(0, TI) as i:
            for p in range(2):
                sp.wait_ge(x2_ready, prev(i, p))
                sp.wait_ge(g_out[p], 16 * (i + 1))
                sp.dma_start(gx[p], tile_rows(x1_tab, 2 * i + p)).then_inc(g_in[p], 16)
                for k in range(TABLES):
                    sp.dma_start(gsum[p][:, k * SUMW:(k + 1) * SUMW],
                                 tile_rows(src_sum[k], 2 * i + p)).then_inc(g_in[p], 16)
            for p in range(2):
                sp.wait_ge(x2_ready, now(i, p))
                sp.dma_start(tile_rows(x2_tab, 2 * i + p), gx[p]).then_inc(g_out[p], 16)
        for p in range(2):
            sp.wait_ge(g_out[p], 16 * (TI + 1))

    def gru_vector(dve):
        v, c = nc.vector, v_own.bind(dve)
        with dve.Fori(0, TI) as i:
            c.enter(i, 2 * (9 + 5))
            for p in range(2):
                t = 2 * i + p
                total = acc3[:, bass.ds(t, 1), :].rearrange("p a f -> p (a f)")
                part = [gsum[p][:, k * SUMW:k * SUMW + KHW] for k in range(TABLES)]
                dve.wait_ge(g_in[p], 16 * (TABLES + 1) * (i + 1))
                for k in range(1, TABLES):
                    c.then(v.tensor_tensor(part[0], part[0], part[k], ALU.add))
                c.step(v.tensor_copy(cnt[p][:, 0:1], total[:, D:KHW]))
                c.then(v.tensor_copy(cnt[p][:, 1:2], part[0][:, D:KHW]))
                c.step(v.tensor_scalar_min(cone[p], cnt[p], 1.0))
                c.then(v.tensor_scalar_max(cmax[p], cnt[p], 1.0))
                c.then(v.reciprocal(cinv[p], cmax[p]))
                c.step(v.tensor_copy(rdeg[:, bass.ds(t, 1)], cinv[p][:, 0:1]))
                v.tensor_scalar(gin[p], total[:, 0:D], cinv[p][:, 0:1], None, ALU.mult)
                v.tensor_scalar(gout[p], part[0][:, 0:D], cinv[p][:, 1:2], None, ALU.mult)
                v.tensor_copy(gh[p], kh3[:, bass.ds(t, 1), 0:D].rearrange("p a f -> p (a f)")).then_inc(pre_ready, 1)
            for p in range(2):
                dve.wait_ge(gate_sb, now(i, p))
                c.then(v.tensor_tensor(gate[p][:, 0:D], gate[p][:, 0:D], psum[:, 4, D:2 * D], ALU.mult))
                v.tensor_tensor(gate[p][:, 0:D], gate[p][:, 0:D], psum[:, 4, 0:D], ALU.add).then_inc(new_ready, 1)
                c.then(v.tensor_tensor(gx[p], gx[p], gh[p], ALU.add))
                dve.wait_ge(cand_ready, now(i, p))
                c.then(v.tensor_tensor(cand[p], cand[p], gh[p], ALU.subtract))
                c.then(v.tensor_tensor(cand[p], cand[p], gate[p][:, D:2 * D], ALU.mult))
                c.then(v.tensor_tensor(gx[p], gx[p], cand[p], ALU.add))
                dve.sem_inc(x2_ready, 1)
        c.leave(TI)

    def gru_scalar(act):
        s = nc.scalar
        with act.Fori(0, TI) as i:
            for p in range(2):
                act.wait_ge(gt_ps, now(i, p))
                s.copy(gt[p], psum[:, 0, :])
                s.copy(ght[p], psum[:, 1, 0:D])
                s.copy(gind[p], psum[0:1, 1, D:2 * D]).then_inc(gt_sb, 1)
                act.wait_ge(conv_ps, now(i, p))
                s.copy(gct[p], psum[:, 2, :]).then_inc(conv_sb, 1)
                act.wait_ge(gate_ps, now(i, p))
                s.activation(gate[p], psum[:, 3, :], ACT.Sigmoid).then_inc(gate_sb, 1)
                act.wait_ge(new_ready, now(i, p))
                s.activation(cand[p], gate[p][:, 0:D], ACT.Tanh).then_inc(cand_ready, 1)

    def gru_tensor(pe):
        t = nc.tensor
        pe.wait_ge(weights_sem, 32 + 80)
        with pe.Fori(0, TI) as i:
            for p in range(2):
                pe.wait_ge(pre_ready, now(i, p))
                pe.wait_ge(gt_sb, now(i, p - 1))
                for w, of in enumerate((gin[p], gout[p])):
                    for k in range(2):
                        t.transpose(psum[:, 0, (2 * w + k) * P:(2 * w + k + 1) * P], of[:, k * P:(k + 1) * P], ident[:, :])
                for k in range(2):
                    t.transpose(psum[:, 1, k * P:(k + 1) * P], gh[p][:, k * P:(k + 1) * P], ident[:, :])
                for w in range(2):
                    mm = t.matmul(psum[0:1, 1, D + w * P:D + (w + 1) * P], cone[p][:, w:w + 1], ident[:, :],
                                  start=True, stop=True)
                mm.then_inc(gt_ps, 1)
                pe.wait_ge(gt_sb, now(i, p))
                pe.wait_ge(conv_sb, now(i, p - 1))
                for w, (wc, bc) in enumerate(((w_in, b_in), (w_out, b_out))):
                    for o in range(2):
                        to = psum[:, 2, (2 * w + o) * P:(2 * w + o + 1) * P]
                        for k in range(2):
                            t.matmul(to, wc[:, k * D + o * P:k * D + (o + 1) * P],
                                     gt[p][:, (2 * w + k) * P:(2 * w + k + 1) * P], start=k == 0, stop=False)
                        mm = t.matmul(to, bc[:, o * P:(o + 1) * P], gind[p][:, w * P:(w + 1) * P],
                                      start=False, stop=True)
                mm.then_inc(conv_ps, 1)
                pe.wait_ge(conv_sb, now(i, p))
                pe.wait_ge(new_ready, now(i, p - 1))
                for k in range(4):
                    t.matmul(psum[:, 3, :], gct[p][:, k * P:(k + 1) * P], w_ih[:, k * 3 * D:k * 3 * D + 2 * D],
                             start=k == 0, stop=False)
                for k in range(2):
                    t.matmul(psum[:, 3, :], ght[p][:, k * P:(k + 1) * P], w_hh[:, k * 3 * D:k * 3 * D + 2 * D],
                             start=False, stop=False)
                t.matmul(psum[:, 3, :], ones[0:1, :], b_ih[:, 0:2 * D], start=False, stop=False)
                t.matmul(psum[:, 3, :], ones[0:1, :], b_hh[:, 0:2 * D], start=False, stop=True)
                for k in range(4):
                    t.matmul(psum[:, 4, 0:D], gct[p][:, k * P:(k + 1) * P],
                             w_ih[:, k * 3 * D + 2 * D:(k + 1) * 3 * D], start=k == 0, stop=False)
                t.matmul(psum[:, 4, 0:D], ones[0:1, :], b_ih[:, 2 * D:3 * D], start=False, stop=True)
                for k in range(2):
                    t.matmul(psum[:, 4, D:2 * D], ght[p][:, k * P:(k + 1) * P],
                             w_hh[:, k * 3 * D + 2 * D:(k + 1) * 3 * D], start=k == 0, stop=False)
                t.matmul(psum[:, 4, D:2 * D], ones[0:1, :], b_hh[:, 2 * D:3 * D], start=False,
                         stop=True).then_inc(gate_ps, 1)

    stage_of(sync=gru_sync, vector=gru_vector, scalar=gru_scalar, tensor=gru_tensor)

    place[0] = common_end
    W2 = RELS * D + D
    kh_flat = kh[:, :]
    place[0] = 0
    hwb = carve(RELS * D, of=kh_flat)
    xsb = carve(D, of=kh_flat)
    chunk_ps, chunk_act, chunk_dve = sem("chunk_ps"), sem("chunk_act"), sem("chunk_dve")
    CHUNKS = [(0, 512), (512, 512), (1024, 512), (1536, 512), (2048, 256)]
    ON_ACT = 3

    def rel_sync(sp):
        load_weights(sp, (wts[:, 0:2 * W2].rearrange("p (k n) -> p k n", k=2), kmajor(a["w2"], 2)),
                     (brow[:, 0:D], a["b2"]))
        with sp.Fori(2 * TI, 3 * TI) as i:
            li = i - 2 * TI
            load_x(sp, i, 2 * li, x2_tab)
            for p in range(2):
                sp.wait_ge(a_ready, now(i, p))
                waited(sp, "sp")
                sp.wait_ge(chunk_act, now(li, 3 * p + 2, 6))
                sp.dma_start(hw_tab[bass.ds((2 * li + p) * P * RELS, P * RELS), :].rearrange("(n r) f -> n (r f)", r=RELS),
                             hwb[p]).then_inc(out_a[p], 16)
                sp.wait_ge(b_ready, now(i, p))
                sp.dma_start(tile_rows(xs_tab, 2 * li + p), xsb[p]).then_inc(out_b[p], 16)
        for p in range(2):
            sp.wait_ge(out_a[p], 16 * (3 * TI + 1))
            sp.wait_ge(out_b[p], 16 * (2 * TI + 1))

    def rel_vector(dve):
        v, c = nc.vector, v_own.bind(dve)
        c.then(v.memset(acc[:, :], 0.0))
        with dve.Fori(2 * TI, 3 * TI) as i:
            c.enter(i - 2 * TI, 6)
            li = i - 2 * TI
            for p in range(2):
                dve.wait_ge(x_in[p], 16 * (i + 2))
            stats_of(dve, c, i, xb)
            normalise(dve, c, i, xb)
            for p in range(2):
                dve.wait_ge(chunk_ps, now(li, 5 * p + 3, 10))
                dve.wait_ge(out_a[p], 16 * (i + 1))
                v.tensor_copy(hwb[p][:, 1536:2048], psum[:, 5, :]).then_inc(chunk_dve, 1)
                dve.wait_ge(chunk_dve, now(li, 2 * p, 4))
                dve.sem_inc(a_ready, 1)
                dve.wait_ge(chunk_ps, now(li, 5 * p + 4, 10))
                dve.wait_ge(out_b[p], 16 * (i - TI + 1))
                v.tensor_tensor(xsb[p], psum[:, 6, 0:D], xb[p], ALU.add).then_inc(chunk_dve, 1)
                dve.wait_ge(chunk_dve, now(li, 2 * p + 1, 4))
                dve.sem_inc(b_ready, 1)
        c.leave(TI)

    def rel_scalar(act):
        with act.Fori(2 * TI, 3 * TI) as i:
            li = i - 2 * TI
            roots(act, i)
            turned_relu(act, i - TI)
            for p in range(2):
                act.wait_ge(out_a[p], 16 * (i + 1))
                for k, (at, size) in enumerate(CHUNKS[:ON_ACT]):
                    act.wait_ge(chunk_ps, now(li, 5 * p + k, 10))
                    nc.scalar.copy(hwb[p][:, at:at + size], psum[:, 2 + k, :]).then_inc(chunk_act, 1)

    def rel_tensor(pe):
        pe.wait_ge(weights_sem, 32 + 80 + 32)
        with pe.Fori(2 * TI, 3 * TI) as i:
            li = i - 2 * TI
            turn(pe, i, i - TI)
            for p in range(2):
                pe.wait_ge(ht_ready, now(i - TI, p))
                for k, (at, size) in enumerate(CHUNKS):
                    if k < ON_ACT:
                        pe.wait_ge(chunk_act, now(li, 3 * (p - 1) + k, 6))
                    else:
                        pe.wait_ge(chunk_dve, now(li, 2 * (p - 1) + k - ON_ACT, 4))
                    project(psum[:, 2 + k, 0:size], p, wts, W2, at, size,
                            brow[:, 0:D] if k == 4 else None).then_inc(chunk_ps, 1)

    stage_of(sync=rel_sync, vector=rel_vector, scalar=rel_scalar, tensor=rel_tensor)

    K2 = 2 * ITERS

    def l2_gpsimd(pool):
        with pool.Fori(K2, K2 + ITERS) as j:
            for h in range(2):
                fetch_indices(pool, j, (j - K2) * RING, h, rel_i)
                for b in range(h * GROUP, (h + 1) * GROUP):
                    gather(pool, j, b, hw_tab, D)

    def l2_vector(dve):
        with dve.Fori(K2, K2 + ITERS) as j:
            s0 = (j - K2) * RING
            tiles = slot_tiles(DVE, s0)
            for h in range(2):
                one_hots(dve, j, s0, h)
                for b in range(h * GROUP, (h + 1) * GROUP):
                    accumulate(dve, j, b, tiles[b], D)
        dve.wait_ge(acc_done, now(K2 + ITERS - 1, RING - 1, RING))

    def l2_tensor(pe):
        with pe.Fori(K2, K2 + ITERS) as j:
            for h in range(2):
                pe.wait_ge(oh_ready, 2 * j + h + 1)
                for b in range(h * GROUP, (h + 1) * GROUP):
                    pe.wait_ge(ring[b], landed(use(j)))
                    aggregate(pe, j, b, 0, D)

    stage_of(gpsimd=l2_gpsimd, vector=l2_vector, tensor=l2_tensor)

    place[0] = common_end
    x3b, xr = carve(D), carve(ACCW)
    prod, aself, aleak = carve(2 * D), carve(HEADS), carve(HEADS)
    att_in, x_used = sem("att_in"), sem("x_used")
    att_src, att_dst = bcast[:, 0:D], bcast[:, D:2 * D]

    def l3_sync(sp):
        load_weights(sp, (wts[:, 0:2 * D].rearrange("p (k n) -> p k n", k=2), kmajor(a["w3"], 2)))
        sp.dma_start(bcast, a["rows3"].to_broadcast([P, 5 * D])).then_inc(att_in, 16)
        with sp.Fori(3 * TI, 4 * TI) as i:
            t = 2 * (i - 3 * TI)
            load_x(sp, i, t, xs_tab)
            for p in range(2):
                sp.wait_ge(a_ready, now(i, p))
                sp.dma_start(tile_rows(x3_tab, t + p), x3b[p]).then_inc(out_b[p], 16)
            for p in range(2):
                sp.wait_ge(b_ready, now(i, p))
                sp.dma_start(tile_rows(xh_tab, t + p), xr[p]).then_inc(out_a[p], 16)
        for p in range(2):
            sp.wait_ge(out_a[p], 16 * (4 * TI + 1))
            sp.wait_ge(out_b[p], 16 * (3 * TI + 1))

    def l3_vector(dve):
        v, c = nc.vector, v_own.bind(dve)
        dve.wait_ge(att_in, 16)
        with dve.Fori(3 * TI, 4 * TI) as i:
            c.enter(i - 3 * TI, 2 * (3 + 6))
            t = 2 * (i - 3 * TI)
            for p in range(2):
                dve.wait_ge(x_in[p], 16 * (i + 2))
                dve.wait_ge(out_b[p], 16 * (i - TI + 1))
                v.scalar_tensor_tensor(x3b[p], acc3[:, bass.ds(t + p, 1), 0:D].rearrange("p a f -> p (a f)"),
                                       rdeg[:, bass.ds(t + p, 1)], xb[p], ALU.mult, ALU.add).then_inc(x_used, 1)
                dve.wait_ge(x_used, 2 * (i - 3 * TI) + p + 1)
            stats_of(dve, c, i, x3b)
            normalise(dve, c, i, x3b)
            for p in range(2):
                dve.wait_ge(norm_ready, now(i, p))
                v.scalar_tensor_tensor(x3b[p], nb[p], 0.0, x3b[p], ALU.max, ALU.add).then_inc(a_ready, 1)
            for p in range(2):
                dve.wait_ge(act_evac, now(i - 3 * TI, p))
                c.step(v.tensor_tensor(prod[p][:, 0:D], xr[p][:, 0:D], att_src, ALU.mult))
                c.then(v.tensor_tensor(prod[p][:, D:], xr[p][:, 0:D], att_dst, ALU.mult))
                c.step(v.tensor_reduce(xr[p][:, D:ACCW], prod[p][:, 0:D].rearrange("p (h d) -> p h d", h=HEADS),
                                       axis=AX.X, op=ALU.add))
                tgt = adst3[:, bass.ds(t + p, 1), :].rearrange("p a f -> p (a f)")
                c.then(v.tensor_reduce(tgt, prod[p][:, D:].rearrange("p (h d) -> p h d", h=HEADS),
                                       axis=AX.X, op=ALU.add))
                c.then(v.tensor_tensor(aself[p], xr[p][:, D:ACCW], tgt, ALU.add))
                c.then(v.scalar_tensor_tensor(m3[:, bass.ds(t + p, 1), :].rearrange("p a f -> p (a f)"),
                                              aself[p], 0.2, aself[p], ALU.mult, ALU.max))
                dve.sem_inc(b_ready, 1)
        c.leave(TI)

    def l3_scalar(act):
        with act.Fori(3 * TI, 4 * TI) as i:
            t = 2 * (i - 3 * TI)
            roots(act, i)
            turned_relu(act, i - TI)
            for p in range(2):
                act.wait_ge(proj_ps, now(i - 2 * TI, p))
                act.wait_ge(out_a[p], 16 * (i + 1))
                nc.scalar.copy(xr[p][:, 0:D], psum[:, 2 + p, 0:D]).then_inc(act_evac, 1)

    def l3_tensor(pe):
        pe.wait_ge(weights_sem, 32 + 80 + 32 + 16)
        with pe.Fori(3 * TI, 4 * TI) as i:
            turn(pe, i, i - TI)
            for p in range(2):
                pe.wait_ge(ht_ready, now(i - TI, p))
                pe.wait_ge(act_evac, prev(i - 3 * TI, p))
                project(psum[:, 2 + p, 0:D], p, wts, D, 0, D).then_inc(proj_ps, 1)

    stage_of(sync=l3_sync, vector=l3_vector, scalar=l3_scalar, tensor=l3_tensor)
    attention(3, 1, False, xh_tab, ACCW, 0)

    bias_b, gamma_b, beta_b = bcast[:, 2 * D:3 * D], bcast[:, 3 * D:4 * D], bcast[:, 4 * D:5 * D]
    FULL, REST = N // P, N % P
    place[0] = 0
    sq, fx = carve(D), carve(D)
    zi, es, wself, fxh = carve(HEADS), carve(HEADS), carve(HEADS), carve(ACCW)
    xh_in, es_ready, wself_ready, own_added = [sem("xh_in0"), sem("xh_in1")], sem("es_ready"), sem("wself_ready"), sem("own_added")
    sum_b, mean_b, gain_b = (kh[:, k * D:(k + 1) * D] for k in range(3))
    sums_ready, mean_ps, sq_ready, var_ps, var_sb, gain_ready = (
        sem(n) for n in ("sums_ready", "mean_ps", "sq_ready", "var_ps", "var_sb", "gain_ready"))
    f_in, f_out = [sem("f_in0"), sem("f_in1")], [sem("f_out0"), sem("f_out1")]
    f_used, f_ready = sem("f_used"), sem("f_ready")

    def final_vector(dve):
        v, c = nc.vector, v_own.bind(dve)

        def own_loop(t, n, p, i):
            dve.wait_ge(xh_in[p], 16 * (i + 1))
            c.then(v.tensor_tensor(es[p][0:n], fxh[p][0:n, D:ACCW],
                                   adst3[0:n, bass.ds(t, 1), :].rearrange("p a f -> p (a f)"), ALU.add))
            c.then(v.scalar_tensor_tensor(es[p][0:n], es[p][0:n], 0.2, es[p][0:n], ALU.mult, ALU.max))
            v.tensor_tensor(es[p][0:n], es[p][0:n], m3[0:n, bass.ds(t, 1), :].rearrange("p a f -> p (a f)"),
                            ALU.subtract).then_inc(es_ready, 1)

        def finish(t, n, p):
            total = acc3[0:n, bass.ds(t, 1), :].rearrange("p a f -> p (a f)")
            heads = total[:, 0:D].rearrange("p (h d) -> p h d", h=HEADS)
            own = fxh[p][0:n, 0:D].rearrange("p (h d) -> p h d", h=HEADS)
            dve.wait_ge(wself_ready, t + 1)
            c.step(v.tensor_tensor(total[:, D:ACCW], total[:, D:ACCW], wself[p][0:n], ALU.add))
            c.then(v.tensor_tensor(own, own, wself[p][0:n].unsqueeze(2).to_broadcast([n, HEADS, DH]), ALU.mult))
            v.tensor_tensor(total[:, 0:D], total[:, 0:D], fxh[p][0:n, 0:D], ALU.add).then_inc(own_added, 1)
            dve.wait_ge(own_added, t + 1)
            waited(dve, "dve")
            c.then(v.reciprocal(zi[p][0:n], total[:, D:ACCW]))
            c.then(v.tensor_tensor(heads, heads, zi[p][0:n].unsqueeze(2).to_broadcast([n, HEADS, DH]), ALU.mult))
            c.then(v.tensor_tensor(total[:, 0:D], total[:, 0:D], bias_b[0:n], ALU.add))
            c.then(v.tensor_tensor(sum_b[0:n], sum_b[0:n], total[:, 0:D], ALU.add))

        def centre(t, n, p):
            total = acc3[0:n, bass.ds(t, 1), 0:D].rearrange("p a f -> p (a f)")
            c.then(v.tensor_tensor(total, total, mean_b[0:n], ALU.subtract))
            c.then(v.tensor_tensor(sq[p][0:n], total, total, ALU.mult))
            c.then(v.tensor_tensor(sum_b[0:n], sum_b[0:n], sq[p][0:n], ALU.add))

        def scale(t, n, p, i):
            total = acc3[0:n, bass.ds(t, 1), 0:D].rearrange("p a f -> p (a f)")
            c.then(v.tensor_tensor(total, total, gain_b[0:n], ALU.mult))
            c.then(v.tensor_tensor(total, total, beta_b[0:n], ALU.add))
            dve.wait_ge(f_in[p], 16 * (i + 1))
            v.tensor_tensor(fx[p][0:n], fx[p][0:n], total, ALU.add).then_inc(f_ready, 1)

        c.then(v.memset(sum_b, 0.0))
        with dve.Fori(0, FULL // 2) as i:
            c.enter(i, 16)
            for p in range(2):
                own_loop(2 * i + p, P, p, i)
            for p in range(2):
                finish(2 * i + p, P, p)
        c.leave(FULL // 2)
        own_loop(FULL, REST, 0, FULL // 2)
        finish(FULL, REST, 0)
        dve.sem_inc(sums_ready, 1)
        dve.wait_ge(mean_ps, 1)
        c.step(v.tensor_scalar(mean_b, psum[:, 0, 0:D], 1.0 / N, None, ALU.mult))
        c.then(v.memset(sum_b, 0.0))
        with dve.Fori(0, FULL // 2) as i:
            c.enter(i, 6)
            for p in range(2):
                centre(2 * i + p, P, p)
        c.leave(FULL // 2)
        centre(FULL, REST, 0)
        dve.sem_inc(sq_ready, 1)
        dve.wait_ge(var_ps, 1)
        v.tensor_scalar(sum_b, psum[:, 1, 0:D], 1.0 / N, 1e-5, ALU.mult, ALU.add).then_inc(var_sb, 1)
        dve.wait_ge(gain_ready, 1)
        c.then(v.reciprocal(gain_b, gain_b))
        c.then(v.tensor_tensor(gain_b, gain_b, gamma_b, ALU.mult))
        with dve.Fori(0, FULL // 2) as i:
            c.enter(i, 4)
            for p in range(2):
                scale(2 * i + p, P, p, i)
        c.leave(FULL // 2)
        scale(FULL, REST, 0, FULL // 2)

    def final_tensor(pe):
        pe.wait_ge(sums_ready, 1)
        nc.tensor.matmul(psum[:, 0, 0:D], ones[:, :], sum_b, start=True, stop=True).then_inc(mean_ps, 1)
        pe.wait_ge(sq_ready, 1)
        nc.tensor.matmul(psum[:, 1, 0:D], ones[:, :], sum_b, start=True, stop=True).then_inc(var_ps, 1)

    def final_scalar(act):
        with act.Fori(0, FULL // 2) as i:
            for p in range(2):
                act.wait_ge(es_ready, 2 * i + p + 1)
                nc.scalar.activation(wself[p], es[p], ACT.Exp).then_inc(wself_ready, 1)
        act.wait_ge(es_ready, FULL + 1)
        nc.scalar.activation(wself[0][0:REST], es[0][0:REST], ACT.Exp).then_inc(wself_ready, 1)
        act.wait_ge(var_sb, 1)
        nc.scalar.activation(gain_b, sum_b, ACT.Sqrt).then_inc(gain_ready, 1)

    def final_sync(sp):
        for p in range(2):
            sp.dma_start(fxh[p], xh_tab[p * P:(p + 1) * P, :]).then_inc(xh_in[p], 16)
        with sp.Fori(1, FULL // 2) as i:
            for p in range(2):
                sp.wait_ge(own_added, 2 * i + p - 1)
                sp.dma_start(fxh[p], tile_rows(xh_tab, 2 * i + p)).then_inc(xh_in[p], 16)
        sp.wait_ge(own_added, FULL - 1)
        sp.dma_start(fxh[0][0:REST], xh_tab[FULL * P:N, :]).then_inc(xh_in[0], 16)
        with sp.Fori(0, FULL // 2) as i:
            for p in range(2):
                sp.wait_ge(f_out[p], 16 * (i + 1))
                sp.dma_start(fx[p], tile_rows(x3_tab, 2 * i + p)).then_inc(f_in[p], 16)
            for p in range(2):
                sp.wait_ge(f_ready, 2 * i + p + 1)
                sp.dma_start(tile_rows(out, 2 * i + p), fx[p]).then_inc(f_out[p], 16)
        sp.wait_ge(f_out[0], 16 * (FULL // 2 + 1))
        sp.dma_start(fx[0][0:REST], x3_tab[FULL * P:N, :]).then_inc(f_in[0], 16)
        sp.wait_ge(f_ready, FULL + 1)
        sp.dma_start(out[FULL * P:N, :], fx[0][0:REST]).then_inc(f_out[0], 16)
        sp.wait_ge(f_out[0], 16 * (FULL // 2 + 2))
        sp.wait_ge(f_out[1], 16 * (FULL // 2 + 1))

    stage_of(vector=final_vector, tensor=final_tensor, scalar=final_scalar, sync=final_sync)

    def start_sync(sp):
        for s in (*out_a, *out_b, *f_out, *g_out):
            sp.sem_inc(s, 16)
        for s in x_in:
            sp.sem_inc(s, 16)

    def start_gpsimd(pool):
        pass

    def start_vector(dve):
        give(dve, 2, var_ready, norm_ready, dve_evac, a_ready, b_ready, score_ready, scan_ready, best_ready,
             max_ready, fall_ready, shifted, srcb_ready, idx2_ready, pre_ready, new_ready, x2_ready)
        give(dve, 4, msg_ready, same_ready, chunk_dve)
        give(dve, 8, pair_used)
        give(dve, RING, acc_done)

    def start_scalar(act):
        give(act, 2, std_ready, ht_ready, act_evac, seg_ready, alpha_ready, weight_ready, gt_sb, conv_sb,
             gate_sb, cand_ready)
        give(act, 4, oht_sb, merged_sb)
        give(act, 6, chunk_act)
        give(act, RING, out_sb)

    def start_tensor(pe):
        give(pe, 2, turn_ps, proj_ps, score_ps, back_ps, best_ps, max_ps, gt_ps, conv_ps, gate_ps)
        give(pe, 4, oht_ps, row_ps, merged_ps)
        give(pe, 2, adst_ps)
        give(pe, 8, key_ps)
        give(pe, 10, chunk_ps)
        give(pe, RING, agg_done, out_ps)

    starts_of = {"sync": start_sync, "gpsimd": start_gpsimd, "vector": start_vector,
                 "scalar": start_scalar, "tensor": start_tensor}

    def engine_program(name, eng):
        starts_of[name](eng)
        for k, part in enumerate(progs[name][:UPTO]):
            if part is not None:
                part(eng)
            eng.drain().then_inc(stage, 1)
            eng.wait_ge(stage, len(progs) * (k + 1))

    block = ctx.enter_context(nc.Block())

    @block.sync
    def _(sp):
        engine_program("sync", sp)

    @block.gpsimd
    def _(pool):
        engine_program("gpsimd", pool)

    @block.vector
    def _(dve):
        engine_program("vector", dve)

    @block.scalar
    def _(act):
        engine_program("scalar", act)

    @block.tensor
    def _(pe):
        engine_program("tensor", pe)


UPTO = None


def kernel(**inputs):
    import concourse.bacc as bacc
    from concourse.bass_utils import run_bass_kernel_spmd

    g = {k: np.asarray(v) for k, v in inputs.items()}

    def edges(name, fill):
        padded = np.full(P * COLS, fill, np.int32)
        padded[:EDGES] = g[name]
        return padded.reshape(P, COLS)

    x = np.zeros((NP, D), np.float32)
    x[:N] = g["x"]
    row = lambda *names: np.concatenate([g[n].reshape(-1) for n in names])[None]
    arrays = {
        "x": x, "src": edges("src", N), "dst": edges("dst", N), "typ": edges("edge_type_8", 0),
        "w0": np.concatenate([g["L0_gnn_Wq"], g["L0_gnn_Wv"], g["L0_gnn_Wk"]], 1),
        "b0": row("L0_gnn_bq", "L0_gnn_bv", "L0_gnn_bk"),
        "w_in": g["L1_gnn_W_in"].T, "w_out": g["L1_gnn_W_out"].T,
        "w_ih": g["L1_gnn_W_ih"].T, "w_hh": g["L1_gnn_W_hh"].T,
        "b1": row("L1_gnn_b_in", "L1_gnn_b_out", "L1_gnn_b_ih", "L1_gnn_b_hh"),
        "w2": np.concatenate([*g["L2_gnn_weight"], g["L2_gnn_sl_w"].T], 1), "b2": row("L2_gnn_sl_b"),
        "w3": g["L3_gnn_W"],
        "rows3": row("L3_gnn_att_src", "L3_gnn_att_dst", "L3_gnn_bias", "L3_gnn_gamma", "L3_gnn_beta"),
    }
    arrays = {f"in_{k}": np.ascontiguousarray(v) for k, v in arrays.items()}
    nc = bacc.Bacc("TRN2", target_bir_lowering=False, num_devices=1)
    args = {k[3:]: nc.dram_tensor(k, v.shape, mybir.dt.from_np(v.dtype), kind="ExternalInput").ap()
            for k, v in arrays.items()}
    out = nc.dram_tensor("out", (N, D), F32, kind="ExternalOutput").ap()
    program(nc, args, out)
    r = run_bass_kernel_spmd(nc, [arrays], core_ids=[0])
    return r.results[0]["out"]
```

```python
from contextlib import ExitStack

import numpy as np

import concourse.bass as bass
from concourse import mybir

F32, I32, U8 = mybir.dt.float32, mybir.dt.int32, mybir.dt.uint8
ALU, ACT, AX = mybir.AluOpType, mybir.ActivationFunctionType, mybir.AxisListType
DVE = mybir.EngineType.DVE
PE = mybir.EngineType.PE

P = 128
N, D, HEADS, DH, RELS, EDGES = 6250, 256, 8, 32, 8, 106250
TILES = 50
NP = TILES * P
COLS = 16 * -(-EDGES // (16 * P))
SLOTS = 896
GROUP = 8
RING = 16
ITERS = SLOTS // RING
NBLK = SLOTS // P
ACCW = D + HEADS
KHW = D + 1
ROW = 2 * D + HEADS
NOWHERE = 32767
BIG = 1e38
SUMW = D + 4
TABLES = 4
TROWS = NP + P
MIDS = 4 * D
assert COLS + TILES <= SLOTS and SLOTS % P == 0 and SLOTS * P % RING == 0


class Chain:

    def __init__(self, sem):
        self.sem, self.base, self.n = sem, 0, 0

    def bind(self, eng):
        self.eng = eng
        return self

    def enter(self, k, per):
        self.start = self.base + self.n
        self.per = per
        self.base, self.n = self.start + k * per, 0

    def leave(self, iters):
        assert self.n == self.per, f"{self.n} steps in an iteration, {self.per} were stated"
        self.base, self.n = self.start + iters * self.per, 0

    def step(self, ins):
        ins.then_inc(self.sem, 1)
        self.n += 1
        return self.n

    def wait(self, n=None):
        self.eng.wait_ge(self.sem, self.base + (self.n if n is None else n))

    def then(self, ins):
        self.step(ins)
        self.wait()


def program(nc, a, out):
    with ExitStack() as ctx:
        build(nc, ctx, a, out)


def build(nc, ctx, a, out):
    def sb(name, shape, dt=F32):
        return ctx.enter_context(nc.sbuf_tensor(name, shape, dt))

    def sem(name):
        return ctx.enter_context(nc.semaphore(name))

    def dram(name, shape, dt=F32):
        return nc.dram_tensor(name, shape, dt).ap()

    def tile_rows(table, t, width=None):
        return table[bass.ds(t * P, P), :] if width is None else table[bass.ds(t * P, P), 0:width]

    rec = dram("rec", [SLOTS * P, 2], I32)
    flags = dram("flags", [SLOTS, P], U8)
    qv_tab = dram("qv_tab", [NP, 2 * D])
    h1_tab = dram("h1_tab", [NP, D])
    src_sum = [dram(f"src_sum{k}", [TROWS, SUMW]) for k in range(TABLES)]
    hw_tab = dram("hw_tab", [NP * RELS, D])
    xh_tab = dram("xh_tab", [NP, ACCW])
    x1_tab, x2_tab, xs_tab, x3_tab = (dram(n, [NP, D]) for n in ("x1_tab", "x2_tab", "xs_tab", "x3_tab"))

    acc = sb("acc", [P, TILES * ACCW])
    kh = sb("kh", [P, TILES * KHW])
    acc3 = acc[:, :].rearrange("p (t f) -> p t f", f=ACCW)
    kh3 = kh[:, :].rearrange("p (t f) -> p t f", f=KHW)
    rows = sb("rows", [P, RING, ROW])
    oh = sb("oh", [P, 2, GROUP, P])
    oht = sb("oht", [P, 2, GROUP, P])
    mnode = sb("mnode", [P, TILES * HEADS])
    m3 = mnode[:, :].rearrange("p (t h) -> p t h", h=HEADS)
    bcast = kh[:, 1024:1024 + 5 * D]
    adst = kh[:, 2560:2560 + TILES * HEADS]
    own = kh[:, 2560 + TILES * HEADS:2560 + 2 * TILES * HEADS]
    own3 = own.rearrange("p (t h) -> p t h", h=HEADS)
    adst3 = adst.rearrange("p (t h) -> p t h", h=HEADS)
    src_i = sb("src_i", [P, SLOTS], I32)
    rel_i = sb("rel_i", [P, SLOTS], I32)
    dl = sb("dl", [P, SLOTS])
    last = sb("last", [P, SLOTS])
    new_tile = sb("new_tile", [P, SLOTS], U8)
    shared = sb("shared", [P, SLOTS // GROUP * P], U8)
    starts = shared[0:HEADS * GROUP, :].rearrange("p (g e) -> p g e", e=P)
    tile_i = shared[64:65, 0:4 * SLOTS].bitcast(I32)
    wts = sb("wts", [P, 22 * D])
    brow = oht[0:1, :, :, :].rearrange("p h g e -> p (h g e)")
    ident, lower, iota_row = sb("ident", [P, P]), sb("lower", [P, P]), sb("iota_row", [P, P])
    ones = sb("ones", [P, P])
    lt_tile = sb("lt_tile", [TILES, TILES])
    spare = sb("spare", [P, 1])
    idx = sb("idx", [P, RING], I32)
    idx2 = sb("idx2", [P, RING], I32)
    rdeg = sb("rdeg", [P, TILES])
    small = sb("small", [P, 64])
    psum = ctx.enter_context(nc.psum_tensor("psum", [P, 8, 512], F32))

    stage = sem("stage")
    ring = [sem(f"ring{b}") for b in range(RING)]
    RANK_ITERS = COLS // RING

    def landed(use):
        return 16 * (use + 2)

    waits = {e: sem(f"waits_{e}") for e in ("pool", "pe", "dve", "sp")}

    def waited(eng, name="pool"):
        eng.sem_inc(waits[name], 1)

    def now(i, p, n=2):
        return n * i + p + n + 1

    def prev(i, p, n=2):
        return n * i + p + 1

    progs = {k: [] for k in ("sync", "gpsimd", "vector", "scalar", "tensor")}

    def stage_of(**parts):
        for k in progs:
            progs[k].append(parts.get(k))

    weights_sem = sem("weights")
    weights = [0]

    u_src = oht[:, 0].rearrange("p a b -> p (a b)")[:, 0:COLS].bitcast(I32)
    u_dst = oht[:, 1].rearrange("p a b -> p (a b)")[:, 0:COLS].bitcast(I32)
    kh_i = kh[:, :].bitcast(I32)
    u_typ = kh_i[:, 0:COLS]
    key_f = kh[:, 1 * COLS:2 * COLS]
    hi_f = kh[:, 2 * COLS:3 * COLS]
    lo_f = kh[:, 3 * COLS:4 * COLS]
    hi_i = kh_i[:, 4 * COLS:5 * COLS]
    lo_i = kh_i[:, 5 * COLS:6 * COLS]
    u_rec = kh_i[:, 6 * COLS:8 * COLS].rearrange("p (c w) -> p c w", w=2)
    base_f = kh[:, 8 * COLS:9 * COLS]
    rank_f = kh[:, 9 * COLS:10 * COLS]
    iota_slot = kh[:, 10 * COLS:10 * COLS + SLOTS]
    tile_f = kh[:, 10 * COLS + SLOTS:10 * COLS + 2 * SLOTS]
    ge = kh[:, 10 * COLS + 2 * SLOTS:10 * COLS + 3 * SLOTS]
    blank = rows[:, :, :].rearrange("p r w -> p (r w)").bitcast(I32)[:, 0:2 * SLOTS] \
        .rearrange("p (s w) -> p s w", w=2)
    ohhi = wts[:, 0:16 * TILES].rearrange("p (h g t) -> p h g t", h=2, g=GROUP)
    ohhit = wts[:, 1024:1024 + 16 * P].rearrange("p (h g e) -> p h g e", h=2, g=GROUP)
    hist = wts[0:TILES, 3200:3328]
    incl = wts[0:TILES, 3328:3456]
    counts = wts[0:TILES, 3808:3808 + GROUP * P].rearrange("p (b e) -> p b e", e=P)
    count = counts[:, 0]
    keyb = wts[:, 3712:3728].rearrange("p (h g) -> p h g", h=2)
    posb = idx2[:, :].rearrange("p (h g) -> p h g", h=2)
    recb = wts[:, 3728:3760].bitcast(I32).rearrange("p (h g w) -> p h g w", h=2, w=2)
    posf = wts[:, 3760:3776].rearrange("p (h g) -> p h g", h=2)

    loaded = sem("loaded")
    consts = sem("consts")
    blank_set = sem("blank_set")
    table_done = [sem(f"table_done{k}") for k in range(TABLES)]
    ZEROED = 96
    zero_set = sem("zero_set")
    filled = sem("filled")
    v_own = Chain(sem("v_own"))

    def const_sync(sp):
        sp.dma_start(u_src, a["src"]).then_inc(loaded, 16)
        sp.dma_start(u_dst, a["dst"]).then_inc(loaded, 16)
        sp.dma_start(u_typ, a["typ"]).then_inc(loaded, 16)
        sp.wait_ge(blank_set, 2)
        sp.dma_start(rec.rearrange("(p s) w -> p (s w)", p=P), blank.rearrange("p s w -> p (s w)")) \
            .then_inc(filled, 16)
        sp.wait_ge(filled, 16)

    def const_gpsimd(pool):
        g = nc.gpsimd
        for b in range(RING):
            pool.dma_start(oh[:, 0, b, 0:8] if b < GROUP else oh[:, 1, b - GROUP, 0:8],
                           a["x"][0:P, 0:8]).then_inc(ring[b], 16)
        imprecise = dict(allow_small_or_imprecise_dtypes=True)
        g.iota(iota_row[:, :], [[1, P]], base=0, channel_multiplier=0, **imprecise).then_inc(consts, 1)
        g.iota(spare[:, :], [[1, 1]], base=NP, channel_multiplier=1, **imprecise).then_inc(consts, 1)
        g.iota(iota_slot[:, :], [[1, SLOTS]], base=0, channel_multiplier=0, **imprecise).then_inc(consts, 1)
        g.memset(ones[:, :], 1.0).then_inc(consts, 1)
        g.memset(ident[:, :], 0.0).then_inc(consts, 1)
        g.memset(lower[:, :], 1.0).then_inc(consts, 1)
        g.memset(lt_tile[:, :], 1.0).then_inc(consts, 1)
        pool.wait_ge(consts, 7)
        g.affine_select(out=ident[:, :], in_=ident[:, :], compare_op=ALU.not_equal, fill=1.0,
                        base=0, pattern=[[-1, P]], channel_multiplier=1).then_inc(consts, 1)
        g.affine_select(out=lower[:, :], in_=lower[:, :], compare_op=ALU.is_gt, fill=0.0,
                        base=0, pattern=[[-1, P]], channel_multiplier=1).then_inc(consts, 1)
        g.affine_select(out=lt_tile[:, :], in_=lt_tile[:, :], compare_op=ALU.is_gt, fill=0.0,
                        base=0, pattern=[[1, TILES]], channel_multiplier=-1).then_inc(consts, 1)
        pool.wait_ge(consts, 10)
        pool.wait_ge(zero_set, 1)
        for k in range(TABLES):
            view = src_sum[k].rearrange("(p j) f -> p (j f)", p=P)
            piece = TROWS // P * SUMW // 3
            for n in range(3):
                pool.dma_start(view[:, n * piece:(n + 1) * piece], acc[:, 0:piece]).then_inc(table_done[k], 32)
        for k in range(TABLES):
            pool.wait_ge(table_done[k], ZEROED)
        for b in range(RING):
            pool.wait_ge(ring[b], landed(-1))

    def const_vector(dve):
        v, c = nc.vector, v_own.bind(dve)
        v.memset(blank[:, :, 0], N).then_inc(blank_set, 1)
        v.memset(blank[:, :, 1], NOWHERE).then_inc(blank_set, 1)
        v.memset(acc[:, :], 0.0).then_inc(zero_set, 1)
        c.step(v.memset(hist, 0.0))
        dve.wait_ge(loaded, 48)
        c.step(v.tensor_scalar(hi_i, u_dst, 7, None, ALU.logical_shift_right))
        c.step(v.tensor_scalar(lo_i, u_dst, P - 1, None, ALU.bitwise_and))
        c.step(v.tensor_copy(key_f, u_dst))
        c.wait()
        c.step(v.tensor_copy(hi_f, hi_i))
        c.step(v.tensor_copy(lo_f, lo_i))
        c.step(v.tensor_copy(u_rec[:, :, 1], u_dst))
        c.then(v.scalar_tensor_tensor(u_rec[:, :, 0], u_typ, 8192.0, u_src, ALU.mult, ALU.add))

    stage_of(sync=const_sync, gpsimd=const_gpsimd, vector=const_vector)

    hot_ready = sem("hot_ready")
    hist_ps = sem("hist_ps")
    hist_add = sem("hist_add")
    hp = psum[0:TILES, 0:2, 0:P]

    def hot_pair(dve, i, half, signal):
        cols = bass.ds(i * RING + half * GROUP, GROUP)
        nc.vector.tensor_tensor(
            ohhi[:, half], iota_row[:, 0:TILES].unsqueeze(1).to_broadcast([P, GROUP, TILES]),
            hi_f[:, cols].unsqueeze(2).to_broadcast([P, GROUP, TILES]), ALU.is_equal).then_inc(signal, 1)
        nc.vector.tensor_tensor(
            oh[:, half], iota_row[:, :].unsqueeze(1).to_broadcast([P, GROUP, P]),
            lo_f[:, cols].unsqueeze(2).to_broadcast([P, GROUP, P]), ALU.is_equal).then_inc(signal, 1)

    def hist_vector(dve):
        dve.sem_inc(hist_add, 2)
        with dve.Fori(0, RANK_ITERS) as i:
            for h in range(2):
                dve.wait_ge(hist_ps, 2 * i + h + 1)
                hot_pair(dve, i, h, hot_ready)
            for h in range(2):
                dve.wait_ge(hist_ps, 2 * i + h + 3)
                dve.wait_ge(hist_add, 2 * i + h + 2)
                nc.vector.tensor_tensor(hist, hist, hp[:, h], ALU.add).then_inc(hist_add, 1)
        dve.wait_ge(hist_add, 2 * RANK_ITERS + 2)

    def hist_tensor(pe):
        pe.sem_inc(hist_ps, 2)
        with pe.Fori(0, RANK_ITERS) as i:
            for h in range(2):
                pe.wait_ge(hot_ready, 4 * i + 2 * h + 2)
                pe.wait_ge(hist_add, 2 * i + h + 1)
                for b in range(GROUP):
                    mm = nc.tensor.matmul(hp[:, h], ohhi[:, h, b], oh[:, h, b],
                                          start=b == 0, stop=b == GROUP - 1)
                mm.then_inc(hist_ps, 1)

    stage_of(vector=hist_vector, tensor=hist_tensor)

    n_f, n_i = small[0:TILES, 0:1], small[0:TILES, 1:2].bitcast(I32)
    sl_i, sl_f = small[0:TILES, 2:3].bitcast(I32), small[0:TILES, 3:4]
    first, end = small[0:TILES, 4:5], small[0:TILES, 5:6]
    nslots_ready = sem("nslots_ready")
    first_ps = sem("first_ps")
    ge_ready = sem("ge_ready")
    tile_ps = sem("tile_ps")

    def layout_vector(dve):
        v, c = nc.vector, v_own.bind(dve)
        c.then(v.reduce_sum(n_f, hist, axis=AX.X))
        c.then(v.tensor_scalar(n_i, n_f, float(P - 1), None, ALU.add))
        c.then(v.tensor_scalar(sl_i, n_i, 7, None, ALU.logical_shift_right))
        v.tensor_copy(sl_f, sl_i).then_inc(nslots_ready, 1)
        c.then(v.tensor_tensor_scan(incl, ones[0:TILES, :], hist, 0.0, ALU.mult, ALU.add))
        dve.wait_ge(nslots_ready, 1)
        dve.wait_ge(first_ps, 1)
        c.step(v.tensor_scalar(first, psum[0:TILES, 0, 0:1], float(P), None, ALU.mult))
        c.then(v.tensor_tensor(end, psum[0:TILES, 0, 0:1], sl_f, ALU.add))
        c.step(v.scalar_tensor_tensor(count, incl, first, hist, ALU.add, ALU.subtract))
        v.tensor_scalar(ge[0:TILES, :], iota_slot[0:TILES, :], end, None, ALU.is_ge).then_inc(ge_ready, 1)
        dve.wait_ge(tile_ps, 1)
        half = SLOTS // 2
        c.then(v.tensor_scalar(tile_f.rearrange("p (a b) -> p a b", a=2), psum[:, 1:3, 0:half],
                               float(TILES - 1), None, ALU.min))
        c.step(v.tensor_copy(tile_i, tile_f[64:65, :]))
        c.step(v.memset(new_tile[:, 0:1], 1))
        c.then(v.tensor_tensor(new_tile[:, 1:], tile_f[:, 1:], tile_f[:, 0:SLOTS - 1], ALU.not_equal))
        c.then(v.tensor_scalar(tile_f, tile_f, float(P), None, ALU.mult))

    def layout_tensor(pe):
        pe.wait_ge(nslots_ready, 1)
        nc.tensor.matmul(psum[0:TILES, 0, 0:1], lt_tile[:, :], sl_f, start=True, stop=True).then_inc(first_ps, 1)
        pe.wait_ge(ge_ready, 1)
        half = SLOTS // 2
        for k in range(2):
            mm = nc.tensor.matmul(psum[:, 1 + k, 0:half], ones[0:TILES, :],
                                  ge[0:TILES, k * half:(k + 1) * half], start=True, stop=True)
        mm.then_inc(tile_ps, 1)

    stage_of(vector=layout_vector, tensor=layout_tensor)

    rhot, keys_ready = sem("rhot"), sem("keys_ready")
    hit_ps, hit_sb = sem("hit_ps"), sem("hit_sb")
    added_ps, keyrow_ps, look_ps = sem("added_ps"), sem("keyrow_ps"), sem("look_ps")
    counted, ranked, looked, pos_ready = sem("counted"), sem("ranked"), sem("looked"), sem("pos_ready")
    AHEAD = {"hit_sb": 3, "counted": 6, "ranked": 6, "looked": 10, "look_ps": 4}

    def quad(bank, q):
        return psum[:, bank + q, :].rearrange("p (b e) -> p b e", b=4)

    def halves_of(step, i, final=False):
        step(i, 0, i, 1)
        step(i, 1, None if final else i + 1, 0)

    def rank_vector(dve):
        v = nc.vector
        c = v_own.bind(dve)

        def hots(i, h):
            m, n = 4 * i + 2 * h, i * RING + h * GROUP
            dve.wait_ge(look_ps, m - 3 + AHEAD["look_ps"])
            dve.wait_ge(looked, n - 9 + AHEAD["looked"])
            hot_pair(dve, i, h, rhot)
            v.tensor_copy(keyb[:, h], key_f[:, bass.ds(i * RING + h * GROUP, GROUP)]).then_inc(keys_ready, 1)

        def step(i, h, jn, hn):
            n = i * RING + h * GROUP
            if jn is not None:
                hots(jn, hn)
            dve.wait_ge(keys_ready, 2 * i + h + 1)
            dve.wait_ge(rhot, 4 * i + 2 * h + 2)
            m = 4 * i + 2 * h
            for b in range(GROUP):
                q = b // 4
                if b % 4 == 0:
                    dve.wait_ge(keyrow_ps, 4 * i + 2 * h + q + 1)
                    dve.wait_ge(added_ps, 4 * i + 2 * h + q + 1)
                if b < 4:
                    dve.wait_ge(looked, n + b - 4 + AHEAD["looked"])
                else:
                    dve.wait_ge(ranked, n + b - 4 + AHEAD["ranked"])
                v.scalar_tensor_tensor(scraps[:, b % 4], quad(6, q)[:, b % 4], keyb[:, h, b:b + 1], lower[:, :],
                                       ALU.is_equal, ALU.mult, accum_out=rank8[:, h, b:b + 1]).then_inc(ranked, 1)
                if b == GROUP - 1:
                    dve.wait_ge(look_ps, m + AHEAD["look_ps"])
                dve.wait_ge(counted, n + b - 1 + AHEAD["counted"])
                v.tensor_tensor(counts[:, (b + 1) % GROUP], counts[:, b], quad(4, q)[0:TILES, b % 4],
                                ALU.add).then_inc(counted, 1)
            for b in range(GROUP):
                q = b // 4
                if b % 4 == 0:
                    dve.wait_ge(look_ps, m + q + AHEAD["look_ps"])
                if b < 4:
                    dve.wait_ge(ranked, n + b + 4 + AHEAD["ranked"])
                else:
                    dve.wait_ge(looked, n + b - 4 + AHEAD["looked"])
                v.tensor_tensor_reduce(out=scraps[:, b % 4], in0=quad(0, q)[:, b % 4], in1=oh[:, h, b], scale=1.0,
                                       scalar=0.0, op0=ALU.mult, op1=ALU.add,
                                       accum_out=base8[:, h, b:b + 1]).then_inc(looked, 1)
            for b in range(GROUP):
                dve.wait_ge(ring[h * GROUP + b], landed(i - 1))
            dve.wait_ge(looked, n + GROUP - 1 + AHEAD["looked"])
            c.step(v.tensor_copy(recb[:, h], u_rec[:, bass.ds(i * RING + h * GROUP, GROUP), :]))
            c.then(v.tensor_tensor(posf[:, h], base8[:, h], rank8[:, h], ALU.add))
            v.tensor_copy(posb[:, h], posf[:, h]).then_inc(pos_ready, 1)

        for s in ("counted", "ranked", "looked"):
            dve.sem_inc({"counted": counted, "ranked": ranked, "looked": looked}[s], AHEAD[s] - 1)
        hots(0, 0)
        with dve.Fori(0, RANK_ITERS - 1) as i:
            c.enter(i, 4)
            halves_of(step, i)
        c.leave(RANK_ITERS - 1)
        halves_of(step, RANK_ITERS - 1, True)

    base8 = wts[:, 3776:3792].rearrange("p (h g) -> p h g", h=2)
    rank8 = wts[:, 3792:3808].rearrange("p (h g) -> p h g", h=2)
    scraps = wts[:, 3808 + GROUP * P:3808 + (GROUP + 4) * P].rearrange("p (b e) -> p b e", e=P)

    def rank_scalar(act):
        act.sem_inc(hit_sb, AHEAD["hit_sb"] - 1)
        with act.Fori(0, RANK_ITERS) as i:
            for h in range(2):
                for q in range(2):
                    act.wait_ge(hit_ps, 4 * i + 2 * h + q + 1)
                    nc.scalar.copy(ohhit[0:TILES, h, 4 * q:4 * q + 4].rearrange("p g e -> p (g e)"),
                                   psum[0:TILES, 2 + q, :]).then_inc(hit_sb, 1)

    def rank_tensor(pe):
        t = nc.tensor

        def prepare(i, h):
            m = 4 * i + 2 * h
            pe.wait_ge(rhot, 4 * i + 2 * h + 2)
            for q in range(2):
                pe.wait_ge(hit_sb, m + q - 2 + AHEAD["hit_sb"])
                waited(pe, "pe")
                for b in range(4):
                    mm = t.transpose(psum[0:TILES, 2 + q, b * P:(b + 1) * P], ohhi[:, h, 4 * q + b], ident[:, :])
                mm.then_inc(hit_ps, 1)
            for q in range(2):
                pe.wait_ge(counted, 4 * (m + q) - 5 + AHEAD["counted"])
                for b in range(4):
                    mm = t.matmul(quad(4, q)[0:TILES, b], ohhi[:, h, 4 * q + b], oh[:, h, 4 * q + b],
                                  start=True, stop=True)
                mm.then_inc(added_ps, 1)
            pe.wait_ge(keys_ready, 2 * i + h + 1)
            for q in range(2):
                pe.wait_ge(ranked, 4 * (m + q) - 5 + AHEAD["ranked"])
                for b in range(4):
                    mm = t.matmul(quad(6, q)[:, b], keyb[:, h, 4 * q + b:4 * q + b + 1].to_broadcast([P, P]),
                                  ident[:, :], start=True, stop=True)
                mm.then_inc(keyrow_ps, 1)

        def step(i, h, jn, hn):
            m = 4 * i + 2 * h
            for q in range(2):
                pe.wait_ge(hit_sb, m + q + AHEAD["hit_sb"])
                pe.wait_ge(looked, 4 * (m + q) - 5 + AHEAD["looked"])
                pe.wait_ge(counted, 4 * (m + q) + 2 + AHEAD["counted"])
                for b in range(4 * q, 4 * q + 4):
                    mm = t.matmul(quad(0, q)[:, b % 4], ohhit[0:TILES, h, b], counts[:, b], start=True, stop=True)
                mm.then_inc(look_ps, 1)
            if jn is not None:
                prepare(jn, hn)

        pe.sem_inc(look_ps, AHEAD["look_ps"] - 1)
        prepare(0, 0)
        with pe.Fori(0, RANK_ITERS - 1) as i:
            halves_of(step, i)
        halves_of(step, RANK_ITERS - 1, True)

    def rank_gpsimd(pool):
        with pool.Fori(0, RANK_ITERS) as i:
            for b in range(RING):
                if b % GROUP == 0:
                    pool.wait_ge(pos_ready, 2 * i + b // GROUP + 1)
                    waited(pool)
                nc.gpsimd.indirect_dma_start(
                    rec, bass.IndirectOffsetOnAxis(posb[:, b // GROUP, b % GROUP:b % GROUP + 1], 0),
                    recb[:, b // GROUP, b % GROUP, :], None).then_inc(ring[b], 16)
        for b in range(RING):
            pool.wait_ge(ring[b], landed(RANK_ITERS - 1))

    stage_of(vector=rank_vector, scalar=rank_scalar, tensor=rank_tensor, gpsimd=rank_gpsimd)

    rs = kh_i[:, 0:2 * SLOTS].rearrange("p (k e w) -> p k e w", k=NBLK, w=2)
    rsf = kh[:, 2 * SLOTS:4 * SLOTS].rearrange("p (k e w) -> p k e w", k=NBLK, w=2)
    flag_f = kh[:, 4 * SLOTS:5 * SLOTS].rearrange("p (k e) -> p k e", k=NBLK)
    last_f = kh[:, 5 * SLOTS:6 * SLOTS].rearrange("p (k e) -> p k e", k=NBLK)
    word0, word1 = kh[:, 6 * SLOTS:7 * SLOTS], kh[:, 7 * SLOTS:8 * SLOTS]
    word0_i, typ_i = wts[:, 0:SLOTS].bitcast(I32), wts[:, SLOTS:2 * SLOTS].bitcast(I32)
    flag_u = wts[:, 2 * SLOTS:3 * SLOTS].bitcast(U8)[:, 0:SLOTS].rearrange("p (k e) -> p k e", k=NBLK)
    assert 8 * SLOTS <= 10 * COLS + SLOTS
    records_in = sem("records_in")
    flags_set = sem("flags_set")
    flags_out = sem("flags_out")
    starts_in = sem("starts_in")
    words_f = sem("words_f")
    turned = sem("turned")

    def reload_sync(sp):
        sp.dma_start(rs.rearrange("p k e w -> p k (e w)"),
                     rec.rearrange("(k s e) w -> s k (e w)", s=P, e=P)).then_inc(records_in, 16)
        sp.wait_ge(flags_set, 1)
        sp.dma_start(flags.rearrange("(k s) e -> s k e", s=P), flag_u).then_inc(flags_out, 16)
        sp.wait_ge(flags_out, 16)
        for h in range(HEADS):
            sp.dma_start(starts[h * GROUP:(h + 1) * GROUP, :, :],
                         flags.rearrange("(g s) e -> s g e", s=GROUP)).then_inc(starts_in, 16)
        sp.wait_ge(starts_in, 16 * HEADS)

    def reload_vector(dve):
        v, c = nc.vector, v_own.bind(dve)
        dve.wait_ge(records_in, 16)
        c.step(v.tensor_copy(rsf.rearrange("p k e w -> p (k e w)"), rs.rearrange("p k e w -> p (k e w)")))
        c.step(v.memset(flag_f[:, :, 0:1], 1.0))
        c.then(v.memset(last_f[:, :, P - 1:P], 1.0))
        c.step(v.tensor_tensor(flag_f[:, :, 1:P], rsf[:, :, 1:P, 1], rsf[:, :, 0:P - 1, 1], ALU.not_equal))
        v.tensor_tensor(last_f[:, :, 0:P - 1], rsf[:, :, 0:P - 1, 1], rsf[:, :, 1:P, 1],
                        ALU.not_equal).then_inc(words_f, 1)
        c.wait()
        v.tensor_copy(flag_u, flag_f).then_inc(flags_set, 1)
        dve.wait_ge(turned, 3 * NBLK)
        for w, to in enumerate((word0, word1, last[:, :])):
            c.step(v.tensor_copy(to[:, 0:4 * P], psum[:, w, 0:4 * P]))
            c.step(v.tensor_copy(to[:, 4 * P:], psum[:, w + 3, 0:(NBLK - 4) * P]))
        c.wait()
        c.step(v.tensor_tensor(dl[:, :], word1, tile_f, ALU.subtract))
        c.then(v.tensor_copy(word0_i, word0))
        c.step(v.tensor_scalar(src_i[:, :], word0_i, 8191, None, ALU.bitwise_and))
        c.then(v.tensor_scalar(typ_i, word0_i, 13, None, ALU.logical_shift_right))
        c.then(v.scalar_tensor_tensor(rel_i[:, :], src_i[:, :], float(RELS), typ_i, ALU.mult, ALU.add))

    def reload_tensor(pe):
        pe.wait_ge(words_f, 1)
        for w in range(3):
            for k in range(NBLK):
                block = last_f[:, k, :] if w == 2 else rsf[:, k, :, w]
                nc.tensor.transpose(psum[:, w + 3 * (k // 4), (k % 4) * P:(k % 4 + 1) * P],
                                    block, ident[:, :]).then_inc(turned, 1)

    stage_of(sync=reload_sync, vector=reload_vector, tensor=reload_tensor)

    TI = TILES // 2
    flat = rows[:, :, :].rearrange("p r w -> p (r w)")
    place = [0]

    def carve(*shape, part=P, of=flat):
        size = int(np.prod(shape))
        at = place[0]
        place[0] += 2 * size
        assert place[0] <= of.shape[1]
        return [of[0:part, at + p * size:at + (p + 1) * size] for p in range(2)]

    xb, nb, ht = carve(D), carve(D), carve(D)
    stats, mv = carve(6), carve(2)
    ve, sd, rsd, zinv = carve(1), carve(1), carve(1), carve(HEADS)
    common_end = place[0]
    x_in, out_a, out_b = ([sem(f"{n}{p}") for p in range(2)] for n in ("x_in", "out_a", "out_b"))
    var_ready, std_ready, norm_ready = sem("var_ready"), sem("std_ready"), sem("norm_ready")
    turn_ps, ht_ready, proj_ps = sem("turn_ps"), sem("ht_ready"), sem("proj_ps")
    act_evac, dve_evac = sem("act_evac"), sem("dve_evac")
    a_ready, b_ready = sem("a_ready"), sem("b_ready")

    def give(eng, n, *sems):
        for s in sems:
            eng.sem_inc(s, n)

    def load_x(sp, i, t, table):
        for p in range(2):
            sp.wait_ge(b_ready, prev(i, p))
            sp.dma_start(xb[p], tile_rows(table, t + p)).then_inc(x_in[p], 16)

    def stats_of(dve, c, i, x):
        for p in range(2):
            c.then(nc.vector.bn_stats(stats[p], x[p]))
            waited(dve, "dve")
            c.then(nc.vector.bn_aggr(mv[p], stats[p]))
            nc.vector.tensor_scalar_add(ve[p], mv[p][:, 1:2], 1e-5).then_inc(var_ready, 1)

    def roots(act, i):
        for p in range(2):
            act.wait_ge(var_ready, now(i, p))
            nc.scalar.activation(sd[p], ve[p], ACT.Sqrt).then_inc(std_ready, 1)

    def normalise(dve, c, i, x):
        for p in range(2):
            dve.wait_ge(std_ready, now(i, p))
            c.then(nc.vector.reciprocal(rsd[p], sd[p]))
            nc.vector.tensor_scalar(nb[p], x[p], mv[p][:, 0:1], rsd[p], ALU.subtract,
                                    ALU.mult).then_inc(norm_ready, 1)

    def turn(pe, i, ip):
        for p in range(2):
            pe.wait_ge(norm_ready, now(i, p))
            for k in range(2):
                mm = nc.tensor.transpose(psum[:, p, k * P:(k + 1) * P], nb[p][:, k * P:(k + 1) * P], ident[:, :])
            mm.then_inc(turn_ps, 1)

    def turned_relu(act, ip):
        for p in range(2):
            act.wait_ge(turn_ps, now(ip, p))
            nc.scalar.activation(ht[p], psum[:, p, 0:D], ACT.Relu).then_inc(ht_ready, 1)

    def project(to, p, w, width, at, size, bias=None):
        for k in range(2):
            mm = nc.tensor.matmul(to, ht[p][:, k * P:(k + 1) * P], w[:, k * width + at:k * width + at + size],
                                  start=k == 0, stop=bias is None and k == 1)
        if bias is not None:
            mm = nc.tensor.matmul(to, ones[0:1, :], bias, start=False, stop=True)
        return mm

    def load_weights(sp, *pairs):
        for to, of in pairs:
            sp.dma_start(to, of).then_inc(weights_sem, 16)

    def kmajor(w, k):
        return w.rearrange("(k p) n -> p k n", p=P)

    W0 = 3 * D
    qv = carve(2 * D)
    scale_q = 1.0 / float(np.sqrt(DH))

    def l0_sync(sp):
        load_weights(sp, (wts[:, 0:2 * W0].rearrange("p (k n) -> p k n", k=2), kmajor(a["w0"], 2)),
                     (brow[:, 0:W0], a["b0"]))
        with sp.Fori(0, TI) as i:
            load_x(sp, i, 2 * i, a["x"])
            for p in range(2):
                sp.wait_ge(a_ready, now(i, p))
                sp.dma_start(tile_rows(qv_tab, 2 * i + p), qv[p]).then_inc(out_a[p], 16)
        for p in range(2):
            sp.wait_ge(out_a[p], 16 * (TI + 1))

    def l0_vector(dve):
        c = v_own.bind(dve)
        with dve.Fori(0, TI) as i:
            c.enter(i, 6)
            for p in range(2):
                dve.wait_ge(x_in[p], 16 * (i + 2))
            stats_of(dve, c, i, xb)
            normalise(dve, c, i, xb)
            for p in range(2):
                dve.wait_ge(proj_ps, now(i, p))
                nc.vector.tensor_copy(kh3[:, bass.ds(2 * i + p, 1), 0:D].rearrange("p a f -> p (a f)"),
                                      psum[:, 4 + p, 0:D]).then_inc(dve_evac, 1)
                dve.wait_ge(norm_ready, now(i, p))
                dve.sem_inc(b_ready, 1)
        c.leave(TI)

    def l0_scalar(act):
        with act.Fori(0, TI) as i:
            roots(act, i)
            turned_relu(act, i)
            for p in range(2):
                act.wait_ge(proj_ps, now(i, p))
                act.wait_ge(out_a[p], 16 * (i + 1))
                nc.scalar.mul(qv[p][:, 0:D], psum[:, 2 + p, 0:D], scale_q)
                nc.scalar.copy(qv[p][:, D:], psum[:, 2 + p, D:2 * D]).then_inc(a_ready, 1)

    def l0_tensor(pe):
        pe.wait_ge(weights_sem, 32)
        with pe.Fori(0, TI) as i:
            turn(pe, i, i)
            for p in range(2):
                pe.wait_ge(ht_ready, now(i, p))
                pe.wait_ge(a_ready, prev(i, p))
                pe.wait_ge(dve_evac, prev(i, p))
                project(psum[:, 2 + p, :], p, wts, W0, 0, 2 * D, brow[:, 0:2 * D])
                project(psum[:, 4 + p, 0:D], p, wts, W0, 2 * D, D, brow[:, 2 * D:3 * D]).then_inc(proj_ps, 1)

    stage_of(sync=l0_sync, vector=l0_vector, scalar=l0_scalar, tensor=l0_tensor)

    idx_ready = sem("idx_ready")
    oh_ready, agg_done, acc_done = sem("oh_ready"), sem("agg_done"), sem("acc_done")

    def use(j):
        return j + RANK_ITERS

    def fetch_indices(pool, j, s0, h, table_idx):
        pool.wait_ge(ring[h * GROUP + GROUP - 1], landed(use(j) - 1))
        nc.gpsimd.tensor_copy(idx[:, h * GROUP:(h + 1) * GROUP],
                              table_idx[:, bass.ds(s0 + h * GROUP, GROUP)]).then_inc(idx_ready, 1)
        pool.wait_ge(idx_ready, 2 * j + h + 1)

    def gather(pool, j, b, table, width):
        pool.wait_ge(agg_done, prev(j, b, RING))
        waited(pool)
        nc.gpsimd.indirect_dma_start(rows[:, b, 0:width], None, table,
                                     bass.IndirectOffsetOnAxis(idx[:, b:b + 1], 0)).then_inc(ring[b], 16)

    def slot_tiles(engine, s0, count=RING):
        _, tiles = nc.values_load_multi_w_load_instructions(
            tile_i[0:1, bass.ds(s0, count)], engines=[engine], min_val=0, max_val=TILES - 1,
            skip_runtime_bounds_check_because="a minimum with TILES - 1 made them")
        return tiles

    def one_hots(dve, j, s0, h):
        dve.wait_ge(agg_done, prev(j, h * GROUP + GROUP - 1, RING))
        nc.vector.tensor_tensor(
            oh[:, h], iota_row[:, :].unsqueeze(1).to_broadcast([P, GROUP, P]),
            dl[:, bass.ds(s0 + h * GROUP, GROUP)].unsqueeze(2).to_broadcast([P, GROUP, P]),
            ALU.is_equal).then_inc(oh_ready, 1)

    def aggregate(pe, j, b, at, width, banks=(6, 7)):
        pe.wait_ge(acc_done, now(j, b - len(banks), RING))
        nc.tensor.matmul(psum[:, banks[b % len(banks)], 0:width], oh[:, b // GROUP, b % GROUP],
                         rows[:, b, at:at + width], start=True, stop=True).then_inc(agg_done, 1)

    def accumulate(dve, j, b, tile, width, banks=(6, 7)):
        dve.wait_ge(agg_done, now(j, b, RING))
        dve.wait_ge(acc_done, now(j, b - 1, RING))
        to = acc3[:, bass.ds(tile, 1), 0:width].rearrange("p a f -> p (a f)")
        nc.vector.tensor_tensor(to, to, psum[:, banks[b % len(banks)], 0:width], ALU.add).then_inc(acc_done, 1)

    oht_ps, oht_sb = sem("oht_ps"), sem("oht_sb")
    key_ps, pair_used = sem("key_ps"), sem("pair_used")
    score_ready, score_ps, seg_ready = sem("score_ready"), sem("score_ps"), sem("seg_ready")
    scan_ready, back_ps, best_ready = sem("scan_ready"), sem("back_ps"), sem("best_ready")
    best_ps, max_ready, max_ps = sem("best_ps"), sem("max_ready"), sem("max_ps")
    fall_ready, alpha_ready = sem("fall_ready"), sem("alpha_ready")
    shifted, weight_ready, msg_ready = sem("shifted"), sem("weight_ready"), sem("msg_ready")
    mark_ready, kept, halves_set = sem("mark_ready"), sem("kept"), sem("halves_set")

    def att_place(*shape, part=P, count=2):
        size = int(np.prod(shape))
        at = att_at[0]
        att_at[0] += count * size
        assert att_at[0] <= wts.shape[1]
        return [wts[0:part, at + k * size:at + (k + 1) * size] for k in range(count)]

    att_at = [0]
    GH = GROUP * HEADS
    score = att_place(GH)
    shift = att_place(GH)
    best = att_place(GROUP * (HEADS + 1))
    seg = att_place(P, part=GH)
    run = att_place(P, part=GH)
    pen = att_place(GROUP)
    mark = att_place(9 * HEADS + 1)
    found, ahead = att_place(9 * HEADS), att_place(9 * HEADS)
    both = att_place(2 * 9 * HEADS)
    top, halves = [b[:, 0:9 * HEADS] for b in both], [b[:, 9 * HEADS:] for b in both]
    pair2 = att_place(2 * HEADS)
    edge_half, edge_sum = att_place(2 * GH), att_place(2 * GH)
    mold = att_place(HEADS)
    alpha = att_place(HEADS)

    def hs(ap):
        return ap.rearrange("p (h s) -> p h s", s=GROUP)

    def sh(ap):
        return ap.rearrange("p (s h) -> p s h", h=HEADS)

    def both9(h):
        return both[h].rearrange("p (k h s) -> p k h s", k=2, s=GROUP + 1)

    def h9(ap):
        return ap.rearrange("p (h s) -> p h s", s=GROUP + 1)

    ps_turn = psum[:, 0, :]
    ps_pair = lambda q: psum[:, 2 + q % 2, :]
    ps_score = psum[0:GH, 4, 0:P]
    ps_back = psum[:, 4, P:P + GH]
    ps_best = psum[:, 4, 256:256 + GROUP * 9].rearrange("p (s c) -> p s c", c=9)
    ps_max = psum[:, 4, 384:384 + GH]
    ps_both = psum[:, 4, 384:384 + 2 * GH].rearrange("p (s k h) -> p s k h", k=2, h=HEADS)

    def attention(k, ka, dot, table, width, vat):
        lo = k * ITERS
        shift_j = lo - ka * ITERS
        hi = lo + ITERS - 1
        banks = (1, 5, 6, 7)

        def steps(step, j, final=False):
            step(j, 0, j, 1)
            step(j, 1, None if final else j + 1, 0)

        def slot(j, h):
            return (j - lo) * RING + h * GROUP

        def on_gpsimd(pool):
            with pool.Fori(lo, lo + ITERS) as j:
                for h in range(2):
                    fetch_indices(pool, j, (j - lo) * RING, h, src_i)
                    for b in range(h * GROUP, (h + 1) * GROUP):
                        gather(pool, j, b, table, width)

        def turn_hot(pe, j, h, q):
            i = j - shift_j
            if q == 0:
                pe.wait_ge(oh_ready, 2 * j + h + 1)
            pe.wait_ge(oht_sb, now(i, 2 * h + q - 1, 4))
            for b in range(4):
                mm = nc.tensor.transpose(ps_turn[:, b * P:(b + 1) * P], oh[:, h, 4 * q + b], ident[:, :])
            mm.then_inc(oht_ps, 1)

        def keys_of(pe, j, h, q, tiles):
            i = j - shift_j
            pe.wait_ge(oht_sb, now(i, 2 * h + 1, 4))
            pe.wait_ge(pair_used, now(i, 4 * h + q - 2, 8))
            for b in range(2):
                tile = kh3[:, bass.ds(tiles[2 * q + b], 1), 0:D].rearrange("p a f -> p (a f)")
                mm = nc.tensor.matmul(ps_pair(q)[:, b * D:(b + 1) * D], oht[:, h, 2 * q + b], tile,
                                      start=True, stop=True)
            mm.then_inc(key_ps, 1)

        def turn_scores(pe, j, h):
            pe.wait_ge(score_ready, now(j - shift_j, h))
            waited(pe, "pe")
            nc.tensor.transpose(ps_score, score[h], ident[:, :]).then_inc(score_ps, 1)

        def turn_back(pe, j, h):
            pe.wait_ge(scan_ready, now(j - shift_j, h))
            waited(pe, "pe")
            nc.tensor.transpose(ps_back, run[h], ident[0:GH, 0:GH]).then_inc(back_ps, 1)

        def best_of(pe, j, h):
            pe.wait_ge(best_ready, now(j - shift_j, h))
            for s in range(GROUP):
                mm = nc.tensor.matmul(ps_best[:, s, :], oh[:, h, s],
                                      best[h].rearrange("p (c s) -> p c s", s=GROUP)[:, :, s],
                                      start=True, stop=True)
            mm.then_inc(best_ps, 1)

        def maxima_of(pe, j, h):
            pe.wait_ge(oht_sb, now(j - shift_j, 2 * h + 1, 4))
            if not dot:
                pe.wait_ge(halves_set, 2 * (j - lo) + h + 1)
            pe.wait_ge(max_ready, now(j - shift_j, h))
            for s in range(GROUP):
                if dot:
                    mm = nc.tensor.matmul(sh(ps_max)[:, s, :], oht[:, h, s], h9(top[h])[:, :, s + 1],
                                          start=True, stop=True)
                else:
                    mm = nc.tensor.matmul(ps_both[:, s], oht[:, h, s], both9(h)[:, :, :, s + 1],
                                          start=True, stop=True)
            mm.then_inc(max_ps, 1)

        def sums_of(pe, j, h, slots):
            for s in slots:
                if s % 4 == 0:
                    pe.wait_ge(msg_ready, now(j - shift_j, 2 * h + s // 4, 4))
                aggregate(pe, j, h * GROUP + s, vat, ACCW, banks)

        def tensor_step(pe, j, h, jn, hn):
            more = jn is not None
            if more and dot:
                tiles = slot_tiles(PE, slot(jn, hn), GROUP)
            best_of(pe, j, h)
            if more:
                turn_hot(pe, jn, hn, 0)
            maxima_of(pe, j, h)
            if more:
                turn_hot(pe, jn, hn, 1)
                if dot:
                    keys_of(pe, jn, hn, 0, tiles)
                    keys_of(pe, jn, hn, 1, tiles)
            sums_of(pe, j, h, range(0, 4))
            if more and dot:
                keys_of(pe, jn, hn, 2, tiles)
                keys_of(pe, jn, hn, 3, tiles)
            if more and not dot:
                turn_scores(pe, jn, hn)
            sums_of(pe, j, h, range(4, 8))
            if more and dot:
                turn_scores(pe, jn, hn)
            if more:
                turn_back(pe, jn, hn)

        def on_tensor(pe):
            turn_hot(pe, lo, 0, 0)
            turn_hot(pe, lo, 0, 1)
            if dot:
                tiles = slot_tiles(PE, 0, GROUP)
                for q in range(4):
                    keys_of(pe, lo, 0, q, tiles)
            turn_scores(pe, lo, 0)
            turn_back(pe, lo, 0)
            with pe.Fori(lo, hi) as j:
                steps(lambda *a: tensor_step(pe, *a), j)
            steps(lambda *a: tensor_step(pe, *a), hi, True)

        def keep_turned(act, j, h, q):
            act.wait_ge(oht_ps, now(j - shift_j, 2 * h + q, 4))
            if q == 0:
                act.wait_ge(max_ps, prev(j - shift_j, h))
            nc.scalar.copy(oht[:, h, 4 * q:4 * q + 4].rearrange("p g e -> p (g e)"),
                           ps_turn).then_inc(oht_sb, 1)

        def marks_of(act, j, h):
            i = j - shift_j
            act.wait_ge(scan_ready, prev(i, h))
            nc.scalar.mul(seg[h], starts[:, bass.ds(2 * (j - lo) + h, 1), :].rearrange("p a e -> p (a e)"),
                          -BIG).then_inc(seg_ready, 1)
            act.wait_ge(max_ready, prev(i, h))
            nc.scalar.mul(h9(mark[h][:, 0:9 * HEADS])[:, :, 1:9],
                          new_tile[:, bass.ds(slot(j, h), GROUP)].unsqueeze(1).to_broadcast([P, HEADS, GROUP]),
                          -BIG).then_inc(mark_ready, 1)

        def fetch_halves(act, j, h):
            act.wait_ge(shifted, prev(j - shift_j, h))
            tiles = slot_tiles(mybir.EngineType.Activation, slot(j, h), GROUP)
            for s in range(GROUP):
                ins = nc.scalar.copy(h9(halves[h])[:, :, s + 1],
                                     adst3[:, bass.ds(tiles[s], 1), :].rearrange("p a f -> p (a f)"))
            ins.then_inc(halves_set, 1)

        def scalar_step(act, j, h, jn, hn):
            i = j - shift_j
            if not dot:
                tiles = slot_tiles(mybir.EngineType.Activation, slot(j, h), GROUP)
            if jn is not None:
                keep_turned(act, jn, hn, 0)
            act.wait_ge(fall_ready, now(i, h))
            nc.scalar.activation(alpha[h], mold[h], ACT.Exp).then_inc(alpha_ready, 1)
            if jn is not None:
                keep_turned(act, jn, hn, 1)
            act.wait_ge(shifted, now(i, h))
            nc.scalar.activation(rows[:, h * GROUP:(h + 1) * GROUP, vat + D:vat + ACCW], sh(shift[h]),
                                 ACT.Exp).then_inc(weight_ready, 1)
            if jn is not None:
                marks_of(act, jn, hn)
                if not dot:
                    fetch_halves(act, jn, hn)
            if not dot:
                for s in range(GROUP):
                    act.wait_ge(kept, (j - lo) * RING + h * GROUP + s + 1)
                    nc.scalar.copy(m3[:, bass.ds(tiles[s], 1), :].rearrange("p a f -> p (a f)"),
                                   h9(top[h])[:, :, s + 1]).then_inc(kept, 1)

        def on_scalar(act):
            if not dot:
                act.sem_inc(kept, 1)
            keep_turned(act, lo, 0, 0)
            keep_turned(act, lo, 0, 1)
            marks_of(act, lo, 0)
            if not dot:
                fetch_halves(act, lo, 0)
            with act.Fori(lo, hi) as j:
                steps(lambda *a: scalar_step(act, *a), j)
            steps(lambda *a: scalar_step(act, *a), hi, True)

        def group_rows(h):
            return rows[:, h * GROUP:(h + 1) * GROUP, :]

        def multiply_keys(dve, j, h, q):
            for b in range(2):
                dve.wait_ge(ring[h * GROUP + 2 * q + b], landed(use(j)))
            dve.wait_ge(key_ps, now(j - shift_j, 4 * h + q, 8))
            pair = group_rows(h)[:, 2 * q:2 * q + 2, 0:D]
            nc.vector.tensor_tensor(pair, ps_pair(q).rearrange("p (s f) -> p s f", s=2), pair,
                                    ALU.mult).then_inc(pair_used, 1)

        def sum_scores(dve, j, h):
            dve.wait_ge(pair_used, now(j - shift_j, 4 * h + 3, 8))
            nc.vector.tensor_reduce(score[h].rearrange("p (h s) -> p s h", s=GROUP),
                                    group_rows(h)[:, :, 0:D].rearrange("p s (h d) -> p s h d", h=HEADS),
                                    axis=AX.X, op=ALU.add).then_inc(score_ready, 1)

        def source_scores(dve, c, j, h):
            for b in range(GROUP):
                dve.wait_ge(ring[h * GROUP + b], landed(use(j)))
            nc.vector.tensor_copy(score[h].rearrange("p (h s) -> p s h", s=GROUP),
                                  group_rows(h)[:, :, D:ACCW]).then_inc(score_ready, 1)

        def scan_scores(dve, c, j, h):
            i = j - shift_j
            dve.wait_ge(score_ps, now(i, h))
            dve.wait_ge(seg_ready, now(i, h))
            nc.vector.tensor_tensor_scan(run[h], seg[h], ps_score, -BIG, ALU.add, ALU.max).then_inc(scan_ready, 1)
            c.step(nc.vector.tensor_copy(best[h][:, GH:], last[:, bass.ds(slot(j, h), GROUP)]))

        def take_best(dve, j, h):
            dve.wait_ge(back_ps, now(j - shift_j, h))
            lastg = last[:, bass.ds(slot(j, h), GROUP)]
            nc.vector.tensor_tensor(hs(best[h][:, 0:GH]), hs(ps_back), lastg.unsqueeze(1).to_broadcast([P, HEADS, GROUP]),
                                    ALU.mult).then_inc(best_ready, 1)

        def update_maxima(dve, c, j, h):
            v, i = nc.vector, j - shift_j
            dve.wait_ge(best_ps, now(i, h))
            c.then(v.tensor_scalar(pen[h].unsqueeze(2), ps_best[:, :, HEADS:HEADS + 1], -1.0, BIG,
                                   ALU.add, ALU.mult))
            c.step(v.tensor_tensor(h9(found[h])[:, :, 1:9].rearrange("p h s -> p s h"), ps_best[:, :, 0:HEADS],
                                   pen[h].unsqueeze(2).to_broadcast([P, GROUP, HEADS]), ALU.add))
            c.then(v.tensor_copy(h9(found[h])[:, :, 0], h9(top[1 - h])[:, :, 8]))
            dve.wait_ge(mark_ready, now(i, h))
            c.then(v.tensor_tensor_scan(ahead[h], mark[h][:, 0:9 * HEADS], found[h], -BIG, ALU.add, ALU.max))
            v.tensor_tensor_scan(top[h][:, ::-1], mark[h][:, 1:9 * HEADS + 1][:, ::-1], ahead[h][:, ::-1],
                                 -BIG, ALU.add, ALU.max).then_inc(max_ready, 1)
            dve.wait_ge(max_ready, now(i, h))
            old, new = h9(found[h])[:, :, 0], h9(top[h])[:, :, 0]
            if not dot:
                dve.wait_ge(halves_set, 2 * (j - lo) + h + 1)
                half = h9(halves[h])[:, :, 1]
                c.step(v.tensor_tensor(pair2[h][:, 0:HEADS], old, half, ALU.add))
                c.then(v.tensor_tensor(pair2[h][:, HEADS:], new, half, ALU.add))
                c.then(v.scalar_tensor_tensor(pair2[h], pair2[h], 0.2, pair2[h], ALU.mult, ALU.max))
                old, new = pair2[h][:, 0:HEADS], pair2[h][:, HEADS:]
            v.tensor_tensor(mold[h], old, new, ALU.subtract).then_inc(fall_ready, 1)

        def shift_scores(dve, c, j, h):
            v, i = nc.vector, j - shift_j
            dve.wait_ge(max_ps, now(i, h))
            if dot:
                v.tensor_tensor(sh(shift[h]), score[h].rearrange("p (h s) -> p s h", s=GROUP), sh(ps_max),
                                ALU.subtract).then_inc(shifted, 1)
                return
            c.then(v.tensor_copy(edge_half[h], ps_both.rearrange("p s k h -> p (s k h)")))
            part = edge_half[h].rearrange("p (s k h) -> p s k h", k=2, h=HEADS)
            sums = edge_sum[h].rearrange("p (k s h) -> p k s h", k=2, h=HEADS)
            c.step(v.tensor_tensor(sums[:, 0], score[h].rearrange("p (h s) -> p s h", s=GROUP), part[:, :, 1],
                                   ALU.add))
            c.then(v.tensor_tensor(sums[:, 1], part[:, :, 0], part[:, :, 1], ALU.add))
            c.then(v.scalar_tensor_tensor(edge_sum[h], edge_sum[h], 0.2, edge_sum[h], ALU.mult, ALU.max))
            v.tensor_tensor(shift[h], edge_sum[h][:, 0:GH], edge_sum[h][:, GH:], ALU.subtract).then_inc(shifted, 1)

        def lower_sums(dve, c, j, h, tile):
            v = nc.vector
            dve.wait_ge(alpha_ready, now(j - shift_j, h))
            acc0 = acc3[:, bass.ds(tile, 1), :].rearrange("p a f -> p (a f)")
            dve.wait_ge(acc_done, now(j, h * GROUP - 1, RING))
            c.step(v.tensor_tensor(acc0[:, 0:D].rearrange("p (h d) -> p h d", h=HEADS),
                                   acc0[:, 0:D].rearrange("p (h d) -> p h d", h=HEADS),
                                   alpha[h].unsqueeze(2).to_broadcast([P, HEADS, DH]), ALU.mult))
            c.step(v.tensor_tensor(acc0[:, D:ACCW], acc0[:, D:ACCW], alpha[h], ALU.mult))

        def weigh_values(dve, j, h, q):
            if q == 0:
                dve.wait_ge(weight_ready, now(j - shift_j, h))
            val = group_rows(h)[:, 4 * q:4 * q + 4, vat:vat + D].rearrange("p s (h d) -> p s h d", h=HEADS)
            wgt = group_rows(h)[:, 4 * q:4 * q + 4, vat + D:vat + ACCW]
            nc.vector.tensor_tensor(val, val, wgt.unsqueeze(3).to_broadcast([P, 4, HEADS, DH]),
                                    ALU.mult).then_inc(msg_ready, 1)

        def vector_step(dve, c, j, h, jn, hn, first=False):
            more = jn is not None
            back = 0 if first else 4
            tiles = slot_tiles(DVE, slot(j, h) - back, GROUP + back)
            take_best(dve, j, h)
            if more:
                one_hots(dve, jn, slot(jn, 0), hn)
            update_maxima(dve, c, j, h)
            for s in range(back):
                b = h * GROUP - back + s
                accumulate(dve, j if b >= 0 else j - 1, b % RING, tiles[s], ACCW, banks)
            shift_scores(dve, c, j, h)
            lower_sums(dve, c, j, h, tiles[back])
            weigh_values(dve, j, h, 0)
            if more and dot:
                multiply_keys(dve, jn, hn, 0)
                multiply_keys(dve, jn, hn, 1)
            weigh_values(dve, j, h, 1)
            c.wait()
            for s in range(0, 2):
                accumulate(dve, j, h * GROUP + s, tiles[back + s], ACCW, banks)
            if more and not dot:
                source_scores(dve, c, jn, hn)
            for s in range(2, 4):
                accumulate(dve, j, h * GROUP + s, tiles[back + s], ACCW, banks)
            if more and dot:
                multiply_keys(dve, jn, hn, 2)
                multiply_keys(dve, jn, hn, 3)
                sum_scores(dve, jn, hn)
            if more:
                scan_scores(dve, c, jn, hn)
            else:
                for s in range(4, 8):
                    accumulate(dve, j, h * GROUP + s, tiles[back + s], ACCW, banks)

        def on_vector(dve):
            v, c = nc.vector, v_own.bind(dve)
            c.step(v.memset(acc[:, :], 0.0))
            for h in range(2):
                c.step(v.memset(h9(mark[h][:, 0:9 * HEADS])[:, :, 0], -BIG))
                c.step(v.memset(mark[h][:, 9 * HEADS:], -BIG))
            c.then(v.memset(top[1], -BIG))
            one_hots(dve, lo, 0, 0)
            if dot:
                for q in range(4):
                    multiply_keys(dve, lo, 0, q)
                sum_scores(dve, lo, 0)
            else:
                source_scores(dve, c, lo, 0)
            scan_scores(dve, c, lo, 0)
            vector_step(dve, c, lo, 0, lo, 1, first=True)
            vector_step(dve, c, lo, 1, lo + 1, 0)
            with dve.Fori(lo + 1, hi) as j:
                c.enter(j - lo - 1, ATT_STEPS[dot])
                steps(lambda *a: vector_step(dve, c, *a), j)
            c.leave(ITERS - 2)
            steps(lambda *a: vector_step(dve, c, *a), hi, True)
            dve.wait_ge(acc_done, now(hi, RING - 1, RING))

        stage_of(gpsimd=on_gpsimd, tensor=on_tensor, scalar=on_scalar, vector=on_vector)

    ATT_STEPS = {True: 2 * 7, False: 2 * 14}
    attention(0, 0, True, qv_tab, 2 * D, D)

    place[0] = common_end
    x1b, h1f = carve(D), carve(2)

    def l0e_sync(sp):
        with sp.Fori(TI, 2 * TI) as i:
            t = 2 * (i - TI)
            load_x(sp, i, t, a["x"])
            for p in range(2):
                sp.wait_ge(a_ready, now(i, p))
                sp.dma_start(tile_rows(x1_tab, t + p), x1b[p]).then_inc(out_a[p], 16)
            for p in range(2):
                sp.wait_ge(b_ready, now(i, p))
                sp.dma_start(tile_rows(h1_tab, t + p),
                             kh3[:, bass.ds(t + p, 1), 0:D].rearrange("p a f -> p (a f)")).then_inc(out_b[p], 16)
        for p in range(2):
            sp.wait_ge(out_a[p], 16 * (2 * TI + 1))
            sp.wait_ge(out_b[p], 16 * (TI + 1))

    def l0e_vector(dve):
        v, c = nc.vector, v_own.bind(dve)
        c.then(v.memset(kh3[:, :, D:KHW], 1.0))
        with dve.Fori(TI, 2 * TI) as i:
            c.enter(i - TI, 12)
            t = 2 * (i - TI)
            for p in range(2):
                total = acc3[:, bass.ds(t + p, 1), :].rearrange("p a f -> p (a f)")
                c.then(v.tensor_scalar_max(zinv[p], total[:, D:ACCW], 1e-16))
                c.then(v.reciprocal(zinv[p], zinv[p]))
                dve.wait_ge(out_a[p], 16 * (i + 1))
                c.then(v.tensor_tensor(x1b[p].rearrange("p (h d) -> p h d", h=HEADS),
                                       total[:, 0:D].rearrange("p (h d) -> p h d", h=HEADS),
                                       zinv[p].unsqueeze(2).to_broadcast([P, HEADS, DH]), ALU.mult))
                dve.wait_ge(x_in[p], 16 * (i + 2))
                v.tensor_tensor(x1b[p], x1b[p], xb[p], ALU.add).then_inc(a_ready, 1)
                dve.wait_ge(a_ready, now(i, p))
            stats_of(dve, c, i, x1b)
            normalise(dve, c, i, x1b)
            for p in range(2):
                dve.wait_ge(norm_ready, now(i, p))
                v.tensor_scalar_max(kh3[:, bass.ds(t + p, 1), 0:D].rearrange("p a f -> p (a f)"), nb[p],
                                    0.0).then_inc(b_ready, 1)
        c.leave(TI)

    def l0e_scalar(act):
        with act.Fori(TI, 2 * TI) as i:
            roots(act, i)

    stage_of(sync=l0e_sync, vector=l0e_vector, scalar=l0e_scalar)

    OUT_AT = ROW - SUMW
    srcb = [wts[:, h * GROUP:(h + 1) * GROUP] for h in range(2)]
    dup = [wts[:, 16 + h * GROUP:16 + (h + 1) * GROUP] for h in range(2)]
    away = [wts[:, 32 + h * GROUP:32 + (h + 1) * GROUP] for h in range(2)]
    scrap1 = wts[:, 64:64 + P]
    src_f = wts[:, 2560:2560 + SLOTS]
    merged = wts[:, 256:256 + 2 * GROUP * P].rearrange("p (h g e) -> p h g e", h=2, g=GROUP)
    srcb_ready, row_ps, same_ready = sem("srcb_ready"), sem("row_ps"), sem("same_ready")
    merged_ps, merged_sb = sem("merged_ps"), sem("merged_sb")
    out_ps, out_sb, idx2_ready = sem("out_ps"), sem("out_sb"), sem("idx2_ready")
    USES = RING // TABLES
    same = oht
    K1 = ITERS

    def l1_gpsimd(pool):
        pool.wait_ge(ones_set, 1)
        with pool.Fori(K1, K1 + ITERS) as j:
            i = j - K1
            for h in range(2):
                fetch_indices(pool, j, i * RING, h, src_i)
                for b in range(h * GROUP, (h + 1) * GROUP):
                    gather(pool, j, b, h1_tab, D)
                for b in range(h * GROUP, (h + 1) * GROUP):
                    k, n = b % TABLES, b // TABLES
                    pool.wait_ge(out_sb, now(i, b, RING))
                    pool.wait_ge(idx2_ready, now(i, h))
                    pool.wait_ge(table_done[k], ZEROED + 16 * (i * USES + n))
                    waited(pool)
                    nc.gpsimd.indirect_dma_start(
                        src_sum[k], bass.IndirectOffsetOnAxis(idx2[:, b:b + 1], 0),
                        rows[:, b, OUT_AT:OUT_AT + SUMW], None, compute_op=ALU.add).then_inc(table_done[k], 16)
        for k in range(TABLES):
            pool.wait_ge(table_done[k], ZEROED + 16 * ITERS * USES)

    def l1_vector(dve):
        v, c = nc.vector, v_own.bind(dve)
        v.memset(acc[:, :], 0.0)
        v.memset(rows[:, :, :], 1.0)
        c.then(v.tensor_copy(src_f, src_i[:, :]))
        dve.sem_inc(ones_set, 1)
        with dve.Fori(K1, K1 + ITERS) as j:
            i = j - K1
            c.enter(i, 2 * (GROUP + 2))
            s0 = i * RING
            tiles = slot_tiles(DVE, s0)
            for h in range(2):
                one_hots(dve, j, s0, h)
                for q in range(2):
                    dve.wait_ge(out_ps, prev(i, h * GROUP + 4 * q + 3, RING))
                v.tensor_copy(srcb[h], src_f[:, bass.ds(s0 + h * GROUP, GROUP)]).then_inc(srcb_ready, 1)
                dve.wait_ge(srcb_ready, now(i, h))
                for q in range(2):
                    dve.wait_ge(row_ps, now(i, 2 * h + q, 4))
                    v.tensor_tensor(same[:, h, 4 * q:4 * q + 4], psum[:, q, :].rearrange("p (g e) -> p g e", g=4),
                                    srcb[h][:, 4 * q:4 * q + 4].unsqueeze(2).to_broadcast([P, 4, P]),
                                    ALU.is_equal).then_inc(same_ready, 1)
                for q in range(2):
                    dve.wait_ge(same_ready, now(i, 2 * h + q, 4))
                    for b in range(4):
                        c.then(v.tensor_tensor_reduce(out=scrap1, in0=same[:, h, 4 * q + b], in1=lower[:, :],
                                                      scale=1.0, scalar=0.0, op0=ALU.mult, op1=ALU.add,
                                                      accum_out=dup[h][:, 4 * q + b:4 * q + b + 1]))
                c.then(v.tensor_scalar(away[h], srcb[h], -1.0, spare[:, :], ALU.mult, ALU.add))
                c.then(v.scalar_tensor_tensor(away[h], dup[h], 1.0, away[h], ALU.min, ALU.mult))
                for k in range(TABLES):
                    dve.wait_ge(table_done[k], ZEROED + 16 * ((i - 1) * USES + 2 * h + 2))
                v.tensor_tensor(idx2[:, h * GROUP:(h + 1) * GROUP], away[h], srcb[h], ALU.add).then_inc(idx2_ready, 1)
                for b in range(h * GROUP, (h + 1) * GROUP):
                    accumulate(dve, j, b, tiles[b], KHW)
        c.leave(ITERS)
        dve.wait_ge(acc_done, now(K1 + ITERS - 1, RING - 1, RING))

    def l1_scalar(act):
        act.wait_ge(ones_set, 1)
        with act.Fori(K1, K1 + ITERS) as j:
            i = j - K1
            for h in range(2):
                for q in range(2):
                    act.wait_ge(merged_ps, now(i, 2 * h + q, 4))
                    nc.scalar.copy(merged[:, h, 4 * q:4 * q + 4].rearrange("p g e -> p (g e)"),
                                   psum[:, 2 + q, :]).then_inc(merged_sb, 1)
                for b in range(h * GROUP, (h + 1) * GROUP):
                    act.wait_ge(out_ps, now(i, b, RING))
                    act.wait_ge(table_done[b % TABLES], ZEROED + 16 * ((i - 1) * USES + b // TABLES + 1))
                    nc.scalar.copy(rows[:, b, OUT_AT:OUT_AT + KHW], psum[:, 4 + b % 2, 0:KHW]).then_inc(out_sb, 1)

    def l1_tensor(pe):
        t = nc.tensor
        pe.wait_ge(ones_set, 1)
        with pe.Fori(K1, K1 + ITERS) as j:
            i = j - K1
            tiles = slot_tiles(PE, i * RING)
            for h in range(2):
                pe.wait_ge(srcb_ready, now(i, h))
                for q in range(2):
                    pe.wait_ge(same_ready, now(i, 2 * h + q - 2, 4))
                    for b in range(4):
                        mm = t.matmul(psum[:, q, b * P:(b + 1) * P],
                                      srcb[h][:, 4 * q + b:4 * q + b + 1].to_broadcast([P, P]), ident[:, :],
                                      start=True, stop=True)
                    mm.then_inc(row_ps, 1)
                pe.wait_ge(oh_ready, 2 * j + h + 1)
                for q in range(2):
                    pe.wait_ge(same_ready, now(i, 2 * h + q, 4))
                    pe.wait_ge(merged_sb, now(i, 2 * h + q - 2, 4))
                    for b in range(4):
                        mm = t.matmul(psum[:, 2 + q, b * P:(b + 1) * P], oh[:, h, 4 * q + b],
                                      same[:, h, 4 * q + b], start=True, stop=True)
                    mm.then_inc(merged_ps, 1)
                for b in range(GROUP):
                    n = h * GROUP + b
                    if b % 4 == 0:
                        pe.wait_ge(merged_sb, now(i, 2 * h + b // 4, 4))
                    pe.wait_ge(out_sb, now(i, n - 2, RING))
                    tile = kh3[:, bass.ds(tiles[n], 1), :].rearrange("p a f -> p (a f)")
                    t.matmul(psum[:, 4 + b % 2, 0:KHW], merged[:, h, b], tile, start=True, stop=True).then_inc(out_ps, 1)
                for b in range(GROUP):
                    n = h * GROUP + b
                    pe.wait_ge(ring[n], landed(use(j)))
                    aggregate(pe, j, n, 0, KHW)

    ones_set = sem("ones_set")
    stage_of(gpsimd=l1_gpsimd, vector=l1_vector, scalar=l1_scalar, tensor=l1_tensor)

    place[0] = 0
    gx, gsum, gin, gout, gh, ght = (carve(n) for n in (D, TABLES * SUMW, D, D, D, D))
    gate, cand, cnt, cmax, cinv, cone = (carve(n) for n in (2 * D, D, 2, 2, 2, 2))
    gind = carve(2 * P, part=1)
    oh_flat, place[0] = oh[:, :, :, :].rearrange("p h g e -> p (h g e)"), 0
    gt, gct = carve(4 * P, of=oh_flat), carve(4 * P, of=oh_flat)
    w_in, w_out = wts[:, 0:2 * D], wts[:, 2 * D:4 * D]
    w_ih, w_hh = wts[:, 4 * D:16 * D], wts[:, 16 * D:22 * D]
    b_in, b_out, b_ih, b_hh = brow[:, 0:D], brow[:, D:2 * D], brow[:, 2 * D:5 * D], brow[:, 5 * D:8 * D]
    g_in = [sem("g_in0"), sem("g_in1")]
    g_out = [sem("g_out0"), sem("g_out1")]
    pre_ready, gt_ps, gt_sb, conv_ps, conv_sb = (sem(n) for n in ("pre_ready", "gt_ps", "gt_sb", "conv_ps", "conv_sb"))
    gate_ps, gate_sb, new_ready, cand_ready, x2_ready = (
        sem(n) for n in ("gate_ps", "gate_sb", "new_ready", "cand_ready", "x2_ready"))

    def gru_sync(sp):
        load_weights(sp, (w_in.rearrange("p (k n) -> p k n", k=2), kmajor(a["w_in"], 2)),
                     (w_out.rearrange("p (k n) -> p k n", k=2), kmajor(a["w_out"], 2)),
                     (w_ih.rearrange("p (k n) -> p k n", k=4), kmajor(a["w_ih"], 4)),
                     (w_hh.rearrange("p (k n) -> p k n", k=2), kmajor(a["w_hh"], 2)),
                     (brow[:, 0:8 * D], a["b1"]))
        with sp.Fori(0, TI) as i:
            for p in range(2):
                sp.wait_ge(x2_ready, prev(i, p))
                sp.wait_ge(g_out[p], 16 * (i + 1))
                sp.dma_start(gx[p], tile_rows(x1_tab, 2 * i + p)).then_inc(g_in[p], 16)
                for k in range(TABLES):
                    sp.dma_start(gsum[p][:, k * SUMW:(k + 1) * SUMW],
                                 tile_rows(src_sum[k], 2 * i + p)).then_inc(g_in[p], 16)
            for p in range(2):
                sp.wait_ge(x2_ready, now(i, p))
                sp.dma_start(tile_rows(x2_tab, 2 * i + p), gx[p]).then_inc(g_out[p], 16)
        for p in range(2):
            sp.wait_ge(g_out[p], 16 * (TI + 1))

    def gru_vector(dve):
        v, c = nc.vector, v_own.bind(dve)
        with dve.Fori(0, TI) as i:
            c.enter(i, 2 * (9 + 5))
            for p in range(2):
                t = 2 * i + p
                total = acc3[:, bass.ds(t, 1), :].rearrange("p a f -> p (a f)")
                part = [gsum[p][:, k * SUMW:k * SUMW + KHW] for k in range(TABLES)]
                dve.wait_ge(g_in[p], 16 * (TABLES + 1) * (i + 1))
                for k in range(1, TABLES):
                    c.then(v.tensor_tensor(part[0], part[0], part[k], ALU.add))
                c.step(v.tensor_copy(cnt[p][:, 0:1], total[:, D:KHW]))
                c.then(v.tensor_copy(cnt[p][:, 1:2], part[0][:, D:KHW]))
                c.step(v.tensor_scalar_min(cone[p], cnt[p], 1.0))
                c.then(v.tensor_scalar_max(cmax[p], cnt[p], 1.0))
                c.then(v.reciprocal(cinv[p], cmax[p]))
                c.step(v.tensor_copy(rdeg[:, bass.ds(t, 1)], cinv[p][:, 0:1]))
                v.tensor_scalar(gin[p], total[:, 0:D], cinv[p][:, 0:1], None, ALU.mult)
                v.tensor_scalar(gout[p], part[0][:, 0:D], cinv[p][:, 1:2], None, ALU.mult)
                v.tensor_copy(gh[p], kh3[:, bass.ds(t, 1), 0:D].rearrange("p a f -> p (a f)")).then_inc(pre_ready, 1)
            for p in range(2):
                dve.wait_ge(gate_sb, now(i, p))
                c.then(v.tensor_tensor(gate[p][:, 0:D], gate[p][:, 0:D], psum[:, 4, D:2 * D], ALU.mult))
                v.tensor_tensor(gate[p][:, 0:D], gate[p][:, 0:D], psum[:, 4, 0:D], ALU.add).then_inc(new_ready, 1)
                c.then(v.tensor_tensor(gx[p], gx[p], gh[p], ALU.add))
                dve.wait_ge(cand_ready, now(i, p))
                c.then(v.tensor_tensor(cand[p], cand[p], gh[p], ALU.subtract))
                c.then(v.tensor_tensor(cand[p], cand[p], gate[p][:, D:2 * D], ALU.mult))
                c.then(v.tensor_tensor(gx[p], gx[p], cand[p], ALU.add))
                dve.sem_inc(x2_ready, 1)
        c.leave(TI)

    def gru_scalar(act):
        s = nc.scalar
        with act.Fori(0, TI) as i:
            for p in range(2):
                act.wait_ge(gt_ps, now(i, p))
                s.copy(gt[p], psum[:, 0, :])
                s.copy(ght[p], psum[:, 1, 0:D])
                s.copy(gind[p], psum[0:1, 1, D:2 * D]).then_inc(gt_sb, 1)
                act.wait_ge(conv_ps, now(i, p))
                s.copy(gct[p], psum[:, 2, :]).then_inc(conv_sb, 1)
                act.wait_ge(gate_ps, now(i, p))
                s.activation(gate[p], psum[:, 3, :], ACT.Sigmoid).then_inc(gate_sb, 1)
                act.wait_ge(new_ready, now(i, p))
                s.activation(cand[p], gate[p][:, 0:D], ACT.Tanh).then_inc(cand_ready, 1)

    def gru_tensor(pe):
        t = nc.tensor
        pe.wait_ge(weights_sem, 32 + 80)
        with pe.Fori(0, TI) as i:
            for p in range(2):
                pe.wait_ge(pre_ready, now(i, p))
                pe.wait_ge(gt_sb, now(i, p - 1))
                for w, of in enumerate((gin[p], gout[p])):
                    for k in range(2):
                        t.transpose(psum[:, 0, (2 * w + k) * P:(2 * w + k + 1) * P], of[:, k * P:(k + 1) * P], ident[:, :])
                for k in range(2):
                    t.transpose(psum[:, 1, k * P:(k + 1) * P], gh[p][:, k * P:(k + 1) * P], ident[:, :])
                for w in range(2):
                    mm = t.matmul(psum[0:1, 1, D + w * P:D + (w + 1) * P], cone[p][:, w:w + 1], ident[:, :],
                                  start=True, stop=True)
                mm.then_inc(gt_ps, 1)
                pe.wait_ge(gt_sb, now(i, p))
                pe.wait_ge(conv_sb, now(i, p - 1))
                for w, (wc, bc) in enumerate(((w_in, b_in), (w_out, b_out))):
                    for o in range(2):
                        to = psum[:, 2, (2 * w + o) * P:(2 * w + o + 1) * P]
                        for k in range(2):
                            t.matmul(to, wc[:, k * D + o * P:k * D + (o + 1) * P],
                                     gt[p][:, (2 * w + k) * P:(2 * w + k + 1) * P], start=k == 0, stop=False)
                        mm = t.matmul(to, bc[:, o * P:(o + 1) * P], gind[p][:, w * P:(w + 1) * P],
                                      start=False, stop=True)
                mm.then_inc(conv_ps, 1)
                pe.wait_ge(conv_sb, now(i, p))
                pe.wait_ge(new_ready, now(i, p - 1))
                for k in range(4):
                    t.matmul(psum[:, 3, :], gct[p][:, k * P:(k + 1) * P], w_ih[:, k * 3 * D:k * 3 * D + 2 * D],
                             start=k == 0, stop=False)
                for k in range(2):
                    t.matmul(psum[:, 3, :], ght[p][:, k * P:(k + 1) * P], w_hh[:, k * 3 * D:k * 3 * D + 2 * D],
                             start=False, stop=False)
                t.matmul(psum[:, 3, :], ones[0:1, :], b_ih[:, 0:2 * D], start=False, stop=False)
                t.matmul(psum[:, 3, :], ones[0:1, :], b_hh[:, 0:2 * D], start=False, stop=True)
                for k in range(4):
                    t.matmul(psum[:, 4, 0:D], gct[p][:, k * P:(k + 1) * P],
                             w_ih[:, k * 3 * D + 2 * D:(k + 1) * 3 * D], start=k == 0, stop=False)
                t.matmul(psum[:, 4, 0:D], ones[0:1, :], b_ih[:, 2 * D:3 * D], start=False, stop=True)
                for k in range(2):
                    t.matmul(psum[:, 4, D:2 * D], ght[p][:, k * P:(k + 1) * P],
                             w_hh[:, k * 3 * D + 2 * D:(k + 1) * 3 * D], start=k == 0, stop=False)
                t.matmul(psum[:, 4, D:2 * D], ones[0:1, :], b_hh[:, 2 * D:3 * D], start=False,
                         stop=True).then_inc(gate_ps, 1)

    stage_of(sync=gru_sync, vector=gru_vector, scalar=gru_scalar, tensor=gru_tensor)

    place[0] = common_end
    W2 = RELS * D + D
    kh_flat = kh[:, :]
    place[0] = 0
    hwb = carve(RELS * D, of=kh_flat)
    xsb = carve(D, of=kh_flat)
    chunk_ps, chunk_act, chunk_dve = sem("chunk_ps"), sem("chunk_act"), sem("chunk_dve")
    CHUNKS = [(0, 512), (512, 512), (1024, 512), (1536, 512), (2048, 256)]
    ON_ACT = 3

    def rel_sync(sp):
        load_weights(sp, (wts[:, 0:2 * W2].rearrange("p (k n) -> p k n", k=2), kmajor(a["w2"], 2)),
                     (brow[:, 0:D], a["b2"]))
        with sp.Fori(2 * TI, 3 * TI) as i:
            li = i - 2 * TI
            load_x(sp, i, 2 * li, x2_tab)
            for p in range(2):
                sp.wait_ge(a_ready, now(i, p))
                waited(sp, "sp")
                sp.wait_ge(chunk_act, now(li, 3 * p + 2, 6))
                sp.dma_start(hw_tab[bass.ds((2 * li + p) * P * RELS, P * RELS), :].rearrange("(n r) f -> n (r f)", r=RELS),
                             hwb[p]).then_inc(out_a[p], 16)
                sp.wait_ge(b_ready, now(i, p))
                sp.dma_start(tile_rows(xs_tab, 2 * li + p), xsb[p]).then_inc(out_b[p], 16)
        for p in range(2):
            sp.wait_ge(out_a[p], 16 * (3 * TI + 1))
            sp.wait_ge(out_b[p], 16 * (2 * TI + 1))

    def rel_vector(dve):
        v, c = nc.vector, v_own.bind(dve)
        c.then(v.memset(acc[:, :], 0.0))
        with dve.Fori(2 * TI, 3 * TI) as i:
            c.enter(i - 2 * TI, 6)
            li = i - 2 * TI
            for p in range(2):
                dve.wait_ge(x_in[p], 16 * (i + 2))
            stats_of(dve, c, i, xb)
            normalise(dve, c, i, xb)
            for p in range(2):
                dve.wait_ge(chunk_ps, now(li, 5 * p + 3, 10))
                dve.wait_ge(out_a[p], 16 * (i + 1))
                v.tensor_copy(hwb[p][:, 1536:2048], psum[:, 5, :]).then_inc(chunk_dve, 1)
                dve.wait_ge(chunk_dve, now(li, 2 * p, 4))
                dve.sem_inc(a_ready, 1)
                dve.wait_ge(chunk_ps, now(li, 5 * p + 4, 10))
                dve.wait_ge(out_b[p], 16 * (i - TI + 1))
                v.tensor_tensor(xsb[p], psum[:, 6, 0:D], xb[p], ALU.add).then_inc(chunk_dve, 1)
                dve.wait_ge(chunk_dve, now(li, 2 * p + 1, 4))
                dve.sem_inc(b_ready, 1)
        c.leave(TI)

    def rel_scalar(act):
        with act.Fori(2 * TI, 3 * TI) as i:
            li = i - 2 * TI
            roots(act, i)
            turned_relu(act, i - TI)
            for p in range(2):
                act.wait_ge(out_a[p], 16 * (i + 1))
                for k, (at, size) in enumerate(CHUNKS[:ON_ACT]):
                    act.wait_ge(chunk_ps, now(li, 5 * p + k, 10))
                    nc.scalar.copy(hwb[p][:, at:at + size], psum[:, 2 + k, :]).then_inc(chunk_act, 1)

    def rel_tensor(pe):
        pe.wait_ge(weights_sem, 32 + 80 + 32)
        with pe.Fori(2 * TI, 3 * TI) as i:
            li = i - 2 * TI
            turn(pe, i, i - TI)
            for p in range(2):
                pe.wait_ge(ht_ready, now(i - TI, p))
                for k, (at, size) in enumerate(CHUNKS):
                    if k < ON_ACT:
                        pe.wait_ge(chunk_act, now(li, 3 * (p - 1) + k, 6))
                    else:
                        pe.wait_ge(chunk_dve, now(li, 2 * (p - 1) + k - ON_ACT, 4))
                    project(psum[:, 2 + k, 0:size], p, wts, W2, at, size,
                            brow[:, 0:D] if k == 4 else None).then_inc(chunk_ps, 1)

    stage_of(sync=rel_sync, vector=rel_vector, scalar=rel_scalar, tensor=rel_tensor)

    K2 = 2 * ITERS

    def l2_gpsimd(pool):
        with pool.Fori(K2, K2 + ITERS) as j:
            for h in range(2):
                fetch_indices(pool, j, (j - K2) * RING, h, rel_i)
                for b in range(h * GROUP, (h + 1) * GROUP):
                    gather(pool, j, b, hw_tab, D)

    def l2_vector(dve):
        with dve.Fori(K2, K2 + ITERS) as j:
            s0 = (j - K2) * RING
            tiles = slot_tiles(DVE, s0)
            for h in range(2):
                one_hots(dve, j, s0, h)
                for b in range(h * GROUP, (h + 1) * GROUP):
                    accumulate(dve, j, b, tiles[b], D)
        dve.wait_ge(acc_done, now(K2 + ITERS - 1, RING - 1, RING))

    def l2_tensor(pe):
        with pe.Fori(K2, K2 + ITERS) as j:
            for h in range(2):
                pe.wait_ge(oh_ready, 2 * j + h + 1)
                for b in range(h * GROUP, (h + 1) * GROUP):
                    pe.wait_ge(ring[b], landed(use(j)))
                    aggregate(pe, j, b, 0, D)

    stage_of(gpsimd=l2_gpsimd, vector=l2_vector, tensor=l2_tensor)

    place[0] = common_end
    x3b, xr = carve(D), carve(ACCW)
    prod, aself, aleak = carve(2 * D), carve(HEADS), carve(HEADS)
    att_in, x_used = sem("att_in"), sem("x_used")
    att_src, att_dst = bcast[:, 0:D], bcast[:, D:2 * D]

    def l3_sync(sp):
        load_weights(sp, (wts[:, 0:2 * D].rearrange("p (k n) -> p k n", k=2), kmajor(a["w3"], 2)))
        sp.dma_start(bcast, a["rows3"].to_broadcast([P, 5 * D])).then_inc(att_in, 16)
        with sp.Fori(3 * TI, 4 * TI) as i:
            t = 2 * (i - 3 * TI)
            load_x(sp, i, t, xs_tab)
            for p in range(2):
                sp.wait_ge(a_ready, now(i, p))
                sp.dma_start(tile_rows(x3_tab, t + p), x3b[p]).then_inc(out_b[p], 16)
            for p in range(2):
                sp.wait_ge(b_ready, now(i, p))
                sp.dma_start(tile_rows(xh_tab, t + p), xr[p]).then_inc(out_a[p], 16)
        for p in range(2):
            sp.wait_ge(out_a[p], 16 * (4 * TI + 1))
            sp.wait_ge(out_b[p], 16 * (3 * TI + 1))

    def l3_vector(dve):
        v, c = nc.vector, v_own.bind(dve)
        dve.wait_ge(att_in, 16)
        c.then(v.memset(mnode[:, :], -BIG))
        with dve.Fori(3 * TI, 4 * TI) as i:
            c.enter(i - 3 * TI, 2 * (3 + 6))
            t = 2 * (i - 3 * TI)
            for p in range(2):
                dve.wait_ge(x_in[p], 16 * (i + 2))
                dve.wait_ge(out_b[p], 16 * (i - TI + 1))
                v.scalar_tensor_tensor(x3b[p], acc3[:, bass.ds(t + p, 1), 0:D].rearrange("p a f -> p (a f)"),
                                       rdeg[:, bass.ds(t + p, 1)], xb[p], ALU.mult, ALU.add).then_inc(x_used, 1)
                dve.wait_ge(x_used, 2 * (i - 3 * TI) + p + 1)
            stats_of(dve, c, i, x3b)
            normalise(dve, c, i, x3b)
            for p in range(2):
                dve.wait_ge(norm_ready, now(i, p))
                v.scalar_tensor_tensor(x3b[p], nb[p], 0.0, x3b[p], ALU.max, ALU.add).then_inc(a_ready, 1)
            for p in range(2):
                dve.wait_ge(act_evac, now(i - 3 * TI, p))
                c.step(v.tensor_tensor(prod[p][:, 0:D], xr[p][:, 0:D], att_src, ALU.mult))
                c.then(v.tensor_tensor(prod[p][:, D:], xr[p][:, 0:D], att_dst, ALU.mult))
                c.step(v.tensor_reduce(xr[p][:, D:ACCW], prod[p][:, 0:D].rearrange("p (h d) -> p h d", h=HEADS),
                                       axis=AX.X, op=ALU.add))
                tgt = adst3[:, bass.ds(t + p, 1), :].rearrange("p a f -> p (a f)")
                c.then(v.tensor_reduce(tgt, prod[p][:, D:].rearrange("p (h d) -> p h d", h=HEADS),
                                       axis=AX.X, op=ALU.add))
                c.then(v.tensor_tensor(aself[p], xr[p][:, D:ACCW], tgt, ALU.add))
                c.then(v.scalar_tensor_tensor(own3[:, bass.ds(t + p, 1), :].rearrange("p a f -> p (a f)"),
                                              aself[p], 0.2, aself[p], ALU.mult, ALU.max))
                dve.sem_inc(b_ready, 1)
        c.leave(TI)

    def l3_scalar(act):
        with act.Fori(3 * TI, 4 * TI) as i:
            t = 2 * (i - 3 * TI)
            roots(act, i)
            turned_relu(act, i - TI)
            for p in range(2):
                act.wait_ge(proj_ps, now(i - 2 * TI, p))
                act.wait_ge(out_a[p], 16 * (i + 1))
                nc.scalar.copy(xr[p][:, 0:D], psum[:, 2 + p, 0:D]).then_inc(act_evac, 1)

    def l3_tensor(pe):
        pe.wait_ge(weights_sem, 32 + 80 + 32 + 16)
        with pe.Fori(3 * TI, 4 * TI) as i:
            turn(pe, i, i - TI)
            for p in range(2):
                pe.wait_ge(ht_ready, now(i - TI, p))
                pe.wait_ge(act_evac, prev(i - 3 * TI, p))
                project(psum[:, 2 + p, 0:D], p, wts, D, 0, D).then_inc(proj_ps, 1)

    stage_of(sync=l3_sync, vector=l3_vector, scalar=l3_scalar, tensor=l3_tensor)
    attention(3, 1, False, xh_tab, ACCW, 0)

    bias_b, gamma_b, beta_b = bcast[:, 2 * D:3 * D], bcast[:, 3 * D:4 * D], bcast[:, 4 * D:5 * D]
    FULL, REST = N // P, N % P
    place[0] = 0
    sq, fx = carve(D), carve(D)
    fxh = carve(ACCW)
    by_edges, by_own, top_f = (kh[:, 4096 + k * TILES * HEADS:4096 + (k + 1) * TILES * HEADS] for k in range(3))

    def t8(ap):
        return ap.rearrange("p (t h) -> p t h", h=HEADS)

    xh_in, es_ready, wself_ready, own_added = [sem("xh_in0"), sem("xh_in1")], sem("es_ready"), sem("wself_ready"), sem("own_added")
    sum_b, mean_b, gain_b = (kh[:, k * D:(k + 1) * D] for k in range(3))
    sums_ready, mean_ps, sq_ready, var_ps, var_sb, gain_ready = (
        sem(n) for n in ("sums_ready", "mean_ps", "sq_ready", "var_ps", "var_sb", "gain_ready"))
    f_in, f_out = [sem("f_in0"), sem("f_in1")], [sem("f_out0"), sem("f_out1")]
    f_used, f_ready = sem("f_used"), sem("f_ready")

    def final_vector(dve):
        v, c = nc.vector, v_own.bind(dve)
        z = acc3[:, :, D:ACCW]
        c.then(v.tensor_tensor(mnode[:, :], mnode[:, :], adst, ALU.add))
        c.then(v.scalar_tensor_tensor(mnode[:, :], mnode[:, :], 0.2, mnode[:, :], ALU.mult, ALU.max))
        c.then(v.tensor_tensor(top_f, mnode[:, :], own, ALU.max))
        c.step(v.tensor_tensor(by_edges, mnode[:, :], top_f, ALU.subtract))
        c.then(v.tensor_tensor(by_own, own, top_f, ALU.subtract))
        dve.sem_inc(es_ready, 1)
        dve.wait_ge(wself_ready, 2)
        c.then(v.tensor_tensor(z, z, t8(by_edges), ALU.mult))
        c.then(v.tensor_tensor(z, z, t8(by_own), ALU.add))
        c.then(v.reciprocal(t8(top_f), z))
        c.step(v.tensor_tensor(by_edges, by_edges, top_f, ALU.mult))
        c.then(v.tensor_tensor(by_own, by_own, top_f, ALU.mult))

        def finish(t, n, p, i):
            total = acc3[0:n, bass.ds(t, 1), :].rearrange("p a f -> p (a f)")
            heads = total[:, 0:D].rearrange("p (h d) -> p h d", h=HEADS)
            row = fxh[p][0:n, 0:D].rearrange("p (h d) -> p h d", h=HEADS)

            def factor(f):
                return t8(f)[0:n, bass.ds(t, 1), :].rearrange("p a f -> p (a f)").unsqueeze(2) \
                    .to_broadcast([n, HEADS, DH])
            dve.wait_ge(xh_in[p], 16 * (i + 1))
            c.step(v.tensor_tensor(heads, heads, factor(by_edges), ALU.mult))
            c.then(v.tensor_tensor(row, row, factor(by_own), ALU.mult))
            v.tensor_tensor(total[:, 0:D], total[:, 0:D], fxh[p][0:n, 0:D], ALU.add).then_inc(own_added, 1)
            dve.wait_ge(own_added, t + 1)
            c.then(v.tensor_tensor(total[:, 0:D], total[:, 0:D], bias_b[0:n], ALU.add))
            c.then(v.tensor_tensor(sum_b[0:n], sum_b[0:n], total[:, 0:D], ALU.add))

        def centre(t, n, p):
            total = acc3[0:n, bass.ds(t, 1), 0:D].rearrange("p a f -> p (a f)")
            c.then(v.tensor_tensor(total, total, mean_b[0:n], ALU.subtract))
            c.then(v.tensor_tensor(sq[p][0:n], total, total, ALU.mult))
            c.then(v.tensor_tensor(sum_b[0:n], sum_b[0:n], sq[p][0:n], ALU.add))

        def scale(t, n, p, i):
            total = acc3[0:n, bass.ds(t, 1), 0:D].rearrange("p a f -> p (a f)")
            c.then(v.tensor_tensor(total, total, gain_b[0:n], ALU.mult))
            c.then(v.tensor_tensor(total, total, beta_b[0:n], ALU.add))
            dve.wait_ge(f_in[p], 16 * (i + 1))
            v.tensor_tensor(fx[p][0:n], fx[p][0:n], total, ALU.add).then_inc(f_ready, 1)

        c.then(v.memset(sum_b, 0.0))
        with dve.Fori(0, FULL // 2) as i:
            c.enter(i, 8)
            for p in range(2):
                finish(2 * i + p, P, p, i)
        c.leave(FULL // 2)
        finish(FULL, REST, 0, FULL // 2)
        dve.sem_inc(sums_ready, 1)
        dve.wait_ge(mean_ps, 1)
        c.step(v.tensor_scalar(mean_b, psum[:, 0, 0:D], 1.0 / N, None, ALU.mult))
        c.then(v.memset(sum_b, 0.0))
        with dve.Fori(0, FULL // 2) as i:
            c.enter(i, 6)
            for p in range(2):
                centre(2 * i + p, P, p)
        c.leave(FULL // 2)
        centre(FULL, REST, 0)
        dve.sem_inc(sq_ready, 1)
        dve.wait_ge(var_ps, 1)
        v.tensor_scalar(sum_b, psum[:, 1, 0:D], 1.0 / N, 1e-5, ALU.mult, ALU.add).then_inc(var_sb, 1)
        dve.wait_ge(gain_ready, 1)
        c.then(v.reciprocal(gain_b, gain_b))
        c.then(v.tensor_tensor(gain_b, gain_b, gamma_b, ALU.mult))
        with dve.Fori(0, FULL // 2) as i:
            c.enter(i, 4)
            for p in range(2):
                scale(2 * i + p, P, p, i)
        c.leave(FULL // 2)
        scale(FULL, REST, 0, FULL // 2)

    def final_tensor(pe):
        pe.wait_ge(sums_ready, 1)
        nc.tensor.matmul(psum[:, 0, 0:D], ones[:, :], sum_b, start=True, stop=True).then_inc(mean_ps, 1)
        pe.wait_ge(sq_ready, 1)
        nc.tensor.matmul(psum[:, 1, 0:D], ones[:, :], sum_b, start=True, stop=True).then_inc(var_ps, 1)

    def final_scalar(act):
        act.wait_ge(es_ready, 1)
        nc.scalar.activation(by_edges, by_edges, ACT.Exp).then_inc(wself_ready, 1)
        nc.scalar.activation(by_own, by_own, ACT.Exp).then_inc(wself_ready, 1)
        act.wait_ge(var_sb, 1)
        nc.scalar.activation(gain_b, sum_b, ACT.Sqrt).then_inc(gain_ready, 1)

    def final_sync(sp):
        for p in range(2):
            sp.dma_start(fxh[p], xh_tab[p * P:(p + 1) * P, :]).then_inc(xh_in[p], 16)
        with sp.Fori(1, FULL // 2) as i:
            for p in range(2):
                sp.wait_ge(own_added, 2 * i + p - 1)
                sp.dma_start(fxh[p], tile_rows(xh_tab, 2 * i + p)).then_inc(xh_in[p], 16)
        sp.wait_ge(own_added, FULL - 1)
        sp.dma_start(fxh[0][0:REST], xh_tab[FULL * P:N, :]).then_inc(xh_in[0], 16)
        with sp.Fori(0, FULL // 2) as i:
            for p in range(2):
                sp.wait_ge(f_out[p], 16 * (i + 1))
                sp.dma_start(fx[p], tile_rows(x3_tab, 2 * i + p)).then_inc(f_in[p], 16)
            for p in range(2):
                sp.wait_ge(f_ready, 2 * i + p + 1)
                sp.dma_start(tile_rows(out, 2 * i + p), fx[p]).then_inc(f_out[p], 16)
        sp.wait_ge(f_out[0], 16 * (FULL // 2 + 1))
        sp.dma_start(fx[0][0:REST], x3_tab[FULL * P:N, :]).then_inc(f_in[0], 16)
        sp.wait_ge(f_ready, FULL + 1)
        sp.dma_start(out[FULL * P:N, :], fx[0][0:REST]).then_inc(f_out[0], 16)
        sp.wait_ge(f_out[0], 16 * (FULL // 2 + 2))
        sp.wait_ge(f_out[1], 16 * (FULL // 2 + 1))

    stage_of(vector=final_vector, tensor=final_tensor, scalar=final_scalar, sync=final_sync)

    def start_sync(sp):
        for s in (*out_a, *out_b, *f_out, *g_out):
            sp.sem_inc(s, 16)
        for s in x_in:
            sp.sem_inc(s, 16)

    def start_gpsimd(pool):
        pass

    def start_vector(dve):
        give(dve, 2, var_ready, norm_ready, dve_evac, a_ready, b_ready, score_ready, scan_ready, best_ready,
             max_ready, fall_ready, shifted, srcb_ready, idx2_ready, pre_ready, new_ready, x2_ready)
        give(dve, 4, msg_ready, same_ready, chunk_dve)
        give(dve, 8, pair_used)
        give(dve, RING, acc_done)

    def start_scalar(act):
        give(act, 2, std_ready, ht_ready, act_evac, seg_ready, mark_ready, alpha_ready, weight_ready, gt_sb, conv_sb,
             gate_sb, cand_ready)
        give(act, 4, oht_sb, merged_sb)
        give(act, 6, chunk_act)
        give(act, RING, out_sb)

    def start_tensor(pe):
        give(pe, 2, turn_ps, proj_ps, score_ps, back_ps, best_ps, max_ps, gt_ps, conv_ps, gate_ps)
        give(pe, 4, oht_ps, row_ps, merged_ps)
        give(pe, 8, key_ps)
        give(pe, 10, chunk_ps)
        give(pe, RING, agg_done, out_ps)

    starts_of = {"sync": start_sync, "gpsimd": start_gpsimd, "vector": start_vector,
                 "scalar": start_scalar, "tensor": start_tensor}

    def engine_program(name, eng):
        starts_of[name](eng)
        for k, part in enumerate(progs[name][:UPTO]):
            if part is not None:
                part(eng)
            eng.drain().then_inc(stage, 1)
            eng.wait_ge(stage, len(progs) * (k + 1))

    block = ctx.enter_context(nc.Block())

    @block.sync
    def _(sp):
        engine_program("sync", sp)

    @block.gpsimd
    def _(pool):
        engine_program("gpsimd", pool)

    @block.vector
    def _(dve):
        engine_program("vector", dve)

    @block.scalar
    def _(act):
        engine_program("scalar", act)

    @block.tensor
    def _(pe):
        engine_program("tensor", pe)


UPTO = None


def kernel(**inputs):
    import concourse.bacc as bacc
    from concourse.bass_utils import run_bass_kernel_spmd

    g = {k: np.asarray(v) for k, v in inputs.items()}

    def edges(name, fill):
        padded = np.full(P * COLS, fill, np.int32)
        padded[:EDGES] = g[name]
        return padded.reshape(P, COLS)

    x = np.zeros((NP, D), np.float32)
    x[:N] = g["x"]
    row = lambda *names: np.concatenate([g[n].reshape(-1) for n in names])[None]
    arrays = {
        "x": x, "src": edges("src", N), "dst": edges("dst", N), "typ": edges("edge_type_8", 0),
        "w0": np.concatenate([g["L0_gnn_Wq"], g["L0_gnn_Wv"], g["L0_gnn_Wk"]], 1),
        "b0": row("L0_gnn_bq", "L0_gnn_bv", "L0_gnn_bk"),
        "w_in": g["L1_gnn_W_in"].T, "w_out": g["L1_gnn_W_out"].T,
        "w_ih": g["L1_gnn_W_ih"].T, "w_hh": g["L1_gnn_W_hh"].T,
        "b1": row("L1_gnn_b_in", "L1_gnn_b_out", "L1_gnn_b_ih", "L1_gnn_b_hh"),
        "w2": np.concatenate([*g["L2_gnn_weight"], g["L2_gnn_sl_w"].T], 1), "b2": row("L2_gnn_sl_b"),
        "w3": g["L3_gnn_W"],
        "rows3": row("L3_gnn_att_src", "L3_gnn_att_dst", "L3_gnn_bias", "L3_gnn_gamma", "L3_gnn_beta"),
    }
    arrays = {f"in_{k}": np.ascontiguousarray(v) for k, v in arrays.items()}
    nc = bacc.Bacc("TRN2", target_bir_lowering=False, num_devices=1)
    args = {k[3:]: nc.dram_tensor(k, v.shape, mybir.dt.from_np(v.dtype), kind="ExternalInput").ap()
            for k, v in arrays.items()}
    out = nc.dram_tensor("out", (N, D), F32, kind="ExternalOutput").ap()
    program(nc, args, out)
    r = run_bass_kernel_spmd(nc, [arrays], core_ids=[0])
    return r.results[0]["out"]
```

```python
from contextlib import ExitStack

import numpy as np

import concourse.bass as bass
from concourse import mybir

F32, I32, U8, BF16 = mybir.dt.float32, mybir.dt.int32, mybir.dt.uint8, mybir.dt.bfloat16
ALU, ACT, AX = mybir.AluOpType, mybir.ActivationFunctionType, mybir.AxisListType
DVE = mybir.EngineType.DVE
PE = mybir.EngineType.PE

P = 128
N, D, HEADS, DH, RELS, EDGES = 6250, 256, 8, 32, 8, 106250
TILES = 50
NP = TILES * P
COLS = 16 * -(-EDGES // (16 * P))
SLOTS = 896
GROUP = 8
RING = 16
ITERS = SLOTS // RING
NBLK = SLOTS // P
ACCW = D + HEADS
KHW = D + 1
ROW = 2 * D + HEADS
NOWHERE = 32767
BIG = 1e38
SUMW = D + 4
TABLES = 4
TROWS = NP + P
MIDS = 4 * D
assert COLS + TILES <= SLOTS and SLOTS % P == 0 and SLOTS * P % RING == 0


class Chain:

    def __init__(self, sem):
        self.sem, self.base, self.n = sem, 0, 0

    def bind(self, eng):
        self.eng = eng
        return self

    def enter(self, k, per):
        self.start = self.base + self.n
        self.per = per
        self.base, self.n = self.start + k * per, 0

    def leave(self, iters):
        assert self.n == self.per, f"{self.n} steps in an iteration, {self.per} were stated"
        self.base, self.n = self.start + iters * self.per, 0

    def step(self, ins):
        ins.then_inc(self.sem, 1)
        self.n += 1
        return self.n

    def wait(self, n=None):
        self.eng.wait_ge(self.sem, self.base + (self.n if n is None else n))

    def then(self, ins):
        self.step(ins)
        self.wait()


def program(nc, a, out):
    with ExitStack() as ctx:
        build(nc, ctx, a, out)


def build(nc, ctx, a, out):
    def sb(name, shape, dt=F32):
        return ctx.enter_context(nc.sbuf_tensor(name, shape, dt))

    def sem(name):
        return ctx.enter_context(nc.semaphore(name))

    def dram(name, shape, dt=F32):
        return nc.dram_tensor(name, shape, dt).ap()

    def tile_rows(table, t, width=None):
        return table[bass.ds(t * P, P), :] if width is None else table[bass.ds(t * P, P), 0:width]

    rec = dram("rec", [SLOTS * P, 2], I32)
    flags = dram("flags", [SLOTS, P], U8)
    qv_tab = dram("qv_tab", [NP, 2 * D])
    h1_tab = dram("h1_tab", [NP, D])
    src_sum = [dram(f"src_sum{k}", [TROWS, SUMW]) for k in range(TABLES)]
    hw_tab = dram("hw_tab", [NP * RELS, D])
    xh_tab = dram("xh_tab", [NP, ACCW])
    x1_tab, x2_tab, xs_tab, x3_tab = (dram(n, [NP, D]) for n in ("x1_tab", "x2_tab", "xs_tab", "x3_tab"))

    acc = sb("acc", [P, TILES * ACCW])
    kh = sb("kh", [P, TILES * KHW])
    acc3 = acc[:, :].rearrange("p (t f) -> p t f", f=ACCW)
    kh3 = kh[:, :].rearrange("p (t f) -> p t f", f=KHW)
    rows = sb("rows", [P, RING, ROW])
    oh = sb("oh", [P, 2, GROUP, P])
    oht = sb("oht", [P, 2, GROUP, P])
    mnode = sb("mnode", [P, TILES * HEADS])
    m3 = mnode[:, :].rearrange("p (t h) -> p t h", h=HEADS)
    bcast = kh[:, 1024:1024 + 5 * D]
    adst = kh[:, 2560:2560 + TILES * HEADS]
    own = kh[:, 2560 + TILES * HEADS:2560 + 2 * TILES * HEADS]
    own3 = own.rearrange("p (t h) -> p t h", h=HEADS)
    adst3 = adst.rearrange("p (t h) -> p t h", h=HEADS)
    src_i = sb("src_i", [P, SLOTS], I32)
    rel_i = sb("rel_i", [P, SLOTS], I32)
    dl = sb("dl", [P, SLOTS])
    last = sb("last", [P, SLOTS])
    new_tile = sb("new_tile", [P, SLOTS], U8)
    shared = sb("shared", [P, SLOTS // GROUP * P], U8)
    starts = shared[0:HEADS * GROUP, :].rearrange("p (g e) -> p g e", e=P)
    tile_i = shared[64:65, 0:4 * SLOTS].bitcast(I32)
    wts = sb("wts", [P, 22 * D])
    brow = oht[0:1, :, :, :].rearrange("p h g e -> p (h g e)")
    ident, lower, iota_row = sb("ident", [P, P]), sb("lower", [P, P]), sb("iota_row", [P, P])
    ones = sb("ones", [P, P])
    lt_tile = sb("lt_tile", [TILES, TILES])
    spare = sb("spare", [P, 1])
    idx = sb("idx", [P, RING], I32)
    idx2 = sb("idx2", [P, RING], I32)
    rdeg = sb("rdeg", [P, TILES])
    small = sb("small", [P, 64])
    psum = ctx.enter_context(nc.psum_tensor("psum", [P, 8, 512], F32))

    stage = sem("stage")
    ring = [sem(f"ring{b}") for b in range(RING)]
    RANK_ITERS = COLS // RING

    def landed(use):
        return 16 * (use + 2)

    waits = {e: sem(f"waits_{e}") for e in ("pool", "pe", "dve", "sp")}

    def waited(eng, name="pool"):
        eng.sem_inc(waits[name], 1)

    def now(i, p, n=2):
        return n * i + p + n + 1

    def prev(i, p, n=2):
        return n * i + p + 1

    progs = {k: [] for k in ("sync", "gpsimd", "vector", "scalar", "tensor")}

    def stage_of(**parts):
        for k in progs:
            progs[k].append(parts.get(k))

    weights_sem = sem("weights")
    weights = [0]

    u_src = oht[:, 0].rearrange("p a b -> p (a b)")[:, 0:COLS].bitcast(I32)
    u_dst = oht[:, 1].rearrange("p a b -> p (a b)")[:, 0:COLS].bitcast(I32)
    kh_i = kh[:, :].bitcast(I32)
    u_typ = kh_i[:, 0:COLS]
    key_f = kh[:, 1 * COLS:2 * COLS]
    hi_f = kh[:, 2 * COLS:3 * COLS]
    lo_f = kh[:, 3 * COLS:4 * COLS]
    hi_i = kh_i[:, 4 * COLS:5 * COLS]
    lo_i = kh_i[:, 5 * COLS:6 * COLS]
    u_rec = kh_i[:, 6 * COLS:8 * COLS].rearrange("p (c w) -> p c w", w=2)
    base_f = kh[:, 8 * COLS:9 * COLS]
    rank_f = kh[:, 9 * COLS:10 * COLS]
    iota_slot = kh[:, 10 * COLS:10 * COLS + SLOTS]
    tile_f = kh[:, 10 * COLS + SLOTS:10 * COLS + 2 * SLOTS]
    ge = kh[:, 10 * COLS + 2 * SLOTS:10 * COLS + 3 * SLOTS]
    blank = rows[:, :, :].rearrange("p r w -> p (r w)").bitcast(I32)[:, 0:2 * SLOTS] \
        .rearrange("p (s w) -> p s w", w=2)
    ohhi = wts[:, 0:16 * TILES].rearrange("p (h g t) -> p h g t", h=2, g=GROUP)
    ohhit = wts[:, 1024:1024 + 16 * P].rearrange("p (h g e) -> p h g e", h=2, g=GROUP)
    hist = wts[0:TILES, 3200:3328]
    incl = wts[0:TILES, 3328:3456]
    counts = wts[0:TILES, 3808:3808 + GROUP * P].rearrange("p (b e) -> p b e", e=P)
    count = counts[:, 0]
    keyb = wts[:, 3712:3728].rearrange("p (h g) -> p h g", h=2)
    posb = idx2[:, :].rearrange("p (h g) -> p h g", h=2)
    recb = wts[:, 3728:3760].bitcast(I32).rearrange("p (h g w) -> p h g w", h=2, w=2)
    posf = wts[:, 3760:3776].rearrange("p (h g) -> p h g", h=2)

    loaded = sem("loaded")
    consts = sem("consts")
    blank_set = sem("blank_set")
    table_done = [sem(f"table_done{k}") for k in range(TABLES)]
    ZEROED = 96
    zero_set = sem("zero_set")
    filled = sem("filled")
    v_own = Chain(sem("v_own"))

    def const_sync(sp):
        sp.dma_start(u_src, a["src"]).then_inc(loaded, 16)
        sp.dma_start(u_dst, a["dst"]).then_inc(loaded, 16)
        sp.dma_start(u_typ, a["typ"]).then_inc(loaded, 16)
        sp.wait_ge(blank_set, 2)
        sp.dma_start(rec.rearrange("(p s) w -> p (s w)", p=P), blank.rearrange("p s w -> p (s w)")) \
            .then_inc(filled, 16)
        sp.wait_ge(filled, 16)

    def const_gpsimd(pool):
        g = nc.gpsimd
        for b in range(RING):
            pool.dma_start(oh[:, 0, b, 0:8] if b < GROUP else oh[:, 1, b - GROUP, 0:8],
                           a["x"][0:P, 0:8]).then_inc(ring[b], 16)
        imprecise = dict(allow_small_or_imprecise_dtypes=True)
        g.iota(iota_row[:, :], [[1, P]], base=0, channel_multiplier=0, **imprecise).then_inc(consts, 1)
        g.iota(spare[:, :], [[1, 1]], base=NP, channel_multiplier=1, **imprecise).then_inc(consts, 1)
        g.iota(iota_slot[:, :], [[1, SLOTS]], base=0, channel_multiplier=0, **imprecise).then_inc(consts, 1)
        g.memset(ones[:, :], 1.0).then_inc(consts, 1)
        g.memset(ident[:, :], 0.0).then_inc(consts, 1)
        g.memset(lower[:, :], 1.0).then_inc(consts, 1)
        g.memset(lt_tile[:, :], 1.0).then_inc(consts, 1)
        pool.wait_ge(consts, 7)
        g.affine_select(out=ident[:, :], in_=ident[:, :], compare_op=ALU.not_equal, fill=1.0,
                        base=0, pattern=[[-1, P]], channel_multiplier=1).then_inc(consts, 1)
        g.affine_select(out=lower[:, :], in_=lower[:, :], compare_op=ALU.is_gt, fill=0.0,
                        base=0, pattern=[[-1, P]], channel_multiplier=1).then_inc(consts, 1)
        g.affine_select(out=lt_tile[:, :], in_=lt_tile[:, :], compare_op=ALU.is_gt, fill=0.0,
                        base=0, pattern=[[1, TILES]], channel_multiplier=-1).then_inc(consts, 1)
        pool.wait_ge(consts, 10)
        pool.wait_ge(zero_set, 1)
        for k in range(TABLES):
            view = src_sum[k].rearrange("(p j) f -> p (j f)", p=P)
            piece = TROWS // P * SUMW // 3
            for n in range(3):
                pool.dma_start(view[:, n * piece:(n + 1) * piece], acc[:, 0:piece]).then_inc(table_done[k], 32)
        for b in range(RING):
            pool.wait_ge(ring[b], landed(-1))

    def const_vector(dve):
        v, c = nc.vector, v_own.bind(dve)
        v.memset(blank[:, :, 0], N).then_inc(blank_set, 1)
        v.memset(blank[:, :, 1], NOWHERE).then_inc(blank_set, 1)
        v.memset(acc[:, :], 0.0).then_inc(zero_set, 1)
        c.step(v.memset(hist, 0.0))
        dve.wait_ge(loaded, 48)
        c.step(v.tensor_scalar(hi_i, u_dst, 7, None, ALU.logical_shift_right))
        c.step(v.tensor_scalar(lo_i, u_dst, P - 1, None, ALU.bitwise_and))
        c.step(v.tensor_copy(key_f, u_dst))
        c.wait()
        c.step(v.tensor_copy(hi_f, hi_i))
        c.step(v.tensor_copy(lo_f, lo_i))
        c.step(v.tensor_copy(u_rec[:, :, 1], u_dst))
        c.then(v.scalar_tensor_tensor(u_rec[:, :, 0], u_typ, 8192.0, u_src, ALU.mult, ALU.add))

    stage_of(sync=const_sync, gpsimd=const_gpsimd, vector=const_vector)

    hot_ready = sem("hot_ready")
    hist_ps = sem("hist_ps")
    hist_add = sem("hist_add")
    hp = psum[0:TILES, 0:2, 0:P]

    oh16 = oh[:, :, 0:GROUP // 2, :].bitcast(BF16).rearrange("p h g (a e) -> p h (g a) e", a=2)
    ohhi16 = wts[:, 0:8 * TILES].bitcast(BF16).rearrange("p (h g t) -> p h g t", h=2, g=GROUP)

    def hot_pair(dve, i, half, signal, ohhi=ohhi, oh=oh):
        cols = bass.ds(i * RING + half * GROUP, GROUP)
        nc.vector.tensor_tensor(
            ohhi[:, half], iota_row[:, 0:TILES].unsqueeze(1).to_broadcast([P, GROUP, TILES]),
            hi_f[:, cols].unsqueeze(2).to_broadcast([P, GROUP, TILES]), ALU.is_equal).then_inc(signal, 1)
        nc.vector.tensor_tensor(
            oh[:, half], iota_row[:, :].unsqueeze(1).to_broadcast([P, GROUP, P]),
            lo_f[:, cols].unsqueeze(2).to_broadcast([P, GROUP, P]), ALU.is_equal).then_inc(signal, 1)

    def hist_vector(dve):
        def hots(i, h):
            dve.wait_ge(hist_ps, 2 * i + h + 1)
            hot_pair(dve, i, h, hot_ready, ohhi16, oh16)

        def add(i):
            dve.wait_ge(hist_ps, 2 * i + 4)
            dve.wait_ge(hist_add, i + 1)
            nc.vector.tensor_tensor(hist, hist, hp[:, 0], ALU.add).then_inc(hist_add, 1)

        dve.sem_inc(hist_add, 1)
        hots(0, 0)
        hots(0, 1)
        with dve.Fori(1, RANK_ITERS) as i:
            hots(i, 0)
            add(i - 1)
            hots(i, 1)
        add(RANK_ITERS - 1)
        dve.wait_ge(hist_add, RANK_ITERS + 1)

    def hist_tensor(pe):
        pe.sem_inc(hist_ps, 2)
        with pe.Fori(0, RANK_ITERS) as i:
            for h in range(2):
                pe.wait_ge(hot_ready, 4 * i + 2 * h + 2)
                if h == 0:
                    pe.wait_ge(hist_add, i + 1)
                for b in range(GROUP):
                    mm = nc.tensor.matmul(hp[:, 0], ohhi16[:, h, b], oh16[:, h, b],
                                          start=h == 0 and b == 0, stop=h == 1 and b == GROUP - 1)
                mm.then_inc(hist_ps, 1)

    stage_of(vector=hist_vector, tensor=hist_tensor)

    n_f, n_i = small[0:TILES, 0:1], small[0:TILES, 1:2].bitcast(I32)
    sl_i, sl_f = small[0:TILES, 2:3].bitcast(I32), small[0:TILES, 3:4]
    first, end = small[0:TILES, 4:5], small[0:TILES, 5:6]
    nslots_ready = sem("nslots_ready")
    first_ps = sem("first_ps")
    ge_ready = sem("ge_ready")
    tile_ps = sem("tile_ps")

    def layout_vector(dve):
        v, c = nc.vector, v_own.bind(dve)
        c.then(v.reduce_sum(n_f, hist, axis=AX.X))
        c.then(v.tensor_scalar(n_i, n_f, float(P - 1), None, ALU.add))
        c.then(v.tensor_scalar(sl_i, n_i, 7, None, ALU.logical_shift_right))
        v.tensor_copy(sl_f, sl_i).then_inc(nslots_ready, 1)
        c.then(v.tensor_tensor_scan(incl, ones[0:TILES, :], hist, 0.0, ALU.mult, ALU.add))
        dve.wait_ge(nslots_ready, 1)
        dve.wait_ge(first_ps, 1)
        c.step(v.tensor_scalar(first, psum[0:TILES, 0, 0:1], float(P), None, ALU.mult))
        c.then(v.tensor_tensor(end, psum[0:TILES, 0, 0:1], sl_f, ALU.add))
        c.step(v.scalar_tensor_tensor(count, incl, first, hist, ALU.add, ALU.subtract))
        v.tensor_scalar(ge[0:TILES, :], iota_slot[0:TILES, :], end, None, ALU.is_ge).then_inc(ge_ready, 1)
        dve.wait_ge(tile_ps, 1)
        half = SLOTS // 2
        c.then(v.tensor_scalar(tile_f.rearrange("p (a b) -> p a b", a=2), psum[:, 1:3, 0:half],
                               float(TILES - 1), None, ALU.min))
        c.step(v.tensor_copy(tile_i, tile_f[64:65, :]))
        c.step(v.memset(new_tile[:, 0:1], 1))
        c.then(v.tensor_tensor(new_tile[:, 1:], tile_f[:, 1:], tile_f[:, 0:SLOTS - 1], ALU.not_equal))
        c.then(v.tensor_scalar(tile_f, tile_f, float(P), None, ALU.mult))

    def layout_tensor(pe):
        pe.wait_ge(nslots_ready, 1)
        nc.tensor.matmul(psum[0:TILES, 0, 0:1], lt_tile[:, :], sl_f, start=True, stop=True).then_inc(first_ps, 1)
        pe.wait_ge(ge_ready, 1)
        half = SLOTS // 2
        for k in range(2):
            mm = nc.tensor.matmul(psum[:, 1 + k, 0:half], ones[0:TILES, :],
                                  ge[0:TILES, k * half:(k + 1) * half], start=True, stop=True)
        mm.then_inc(tile_ps, 1)

    stage_of(vector=layout_vector, tensor=layout_tensor)

    rhot, keys_ready = sem("rhot"), sem("keys_ready")
    hit_ps, hit_sb = sem("hit_ps"), sem("hit_sb")
    added_ps, keyrow_ps, look_ps = sem("added_ps"), sem("keyrow_ps"), sem("look_ps")
    counted, ranked, looked, pos_ready = sem("counted"), sem("ranked"), sem("looked"), sem("pos_ready")
    AHEAD = {"hit_sb": 3, "counted": 6, "ranked": 6, "looked": 10, "look_ps": 4}

    def quad(bank, q):
        return psum[:, bank + q, :].rearrange("p (b e) -> p b e", b=4)

    def halves_of(step, i, final=False):
        step(i, 0, i, 1)
        step(i, 1, None if final else i + 1, 0)

    def rank_vector(dve):
        v = nc.vector
        c = v_own.bind(dve)

        def hots(i, h):
            m, n = 4 * i + 2 * h, i * RING + h * GROUP
            dve.wait_ge(look_ps, m - 3 + AHEAD["look_ps"])
            dve.wait_ge(looked, n - 9 + AHEAD["looked"])
            hot_pair(dve, i, h, rhot)
            v.tensor_copy(keyb[:, h], key_f[:, bass.ds(i * RING + h * GROUP, GROUP)]).then_inc(keys_ready, 1)

        def step(i, h, jn, hn):
            n = i * RING + h * GROUP
            if jn is not None:
                hots(jn, hn)
            dve.wait_ge(keys_ready, 2 * i + h + 1)
            dve.wait_ge(rhot, 4 * i + 2 * h + 2)
            m = 4 * i + 2 * h
            for b in range(GROUP):
                q = b // 4
                if b % 4 == 0:
                    dve.wait_ge(keyrow_ps, 4 * i + 2 * h + q + 1)
                    dve.wait_ge(added_ps, 4 * i + 2 * h + q + 1)
                if b < 4:
                    dve.wait_ge(looked, n + b - 4 + AHEAD["looked"])
                else:
                    dve.wait_ge(ranked, n + b - 4 + AHEAD["ranked"])
                v.scalar_tensor_tensor(scraps[:, b % 4], quad(6, q)[:, b % 4], keyb[:, h, b:b + 1], lower[:, :],
                                       ALU.is_equal, ALU.mult, accum_out=rank8[:, h, b:b + 1]).then_inc(ranked, 1)
                if b == GROUP - 1:
                    dve.wait_ge(look_ps, m + AHEAD["look_ps"])
                dve.wait_ge(counted, n + b - 1 + AHEAD["counted"])
                v.tensor_tensor(counts[:, (b + 1) % GROUP], counts[:, b], quad(4, q)[0:TILES, b % 4],
                                ALU.add).then_inc(counted, 1)
            for b in range(GROUP):
                q = b // 4
                if b % 4 == 0:
                    dve.wait_ge(look_ps, m + q + AHEAD["look_ps"])
                if b < 4:
                    dve.wait_ge(ranked, n + b + 4 + AHEAD["ranked"])
                else:
                    dve.wait_ge(looked, n + b - 4 + AHEAD["looked"])
                v.tensor_tensor_reduce(out=scraps[:, b % 4], in0=quad(0, q)[:, b % 4], in1=oh[:, h, b], scale=1.0,
                                       scalar=0.0, op0=ALU.mult, op1=ALU.add,
                                       accum_out=base8[:, h, b:b + 1]).then_inc(looked, 1)
            for b in range(GROUP):
                dve.wait_ge(ring[h * GROUP + b], landed(i - 1))
            dve.wait_ge(looked, n + GROUP - 1 + AHEAD["looked"])
            c.step(v.tensor_copy(recb[:, h], u_rec[:, bass.ds(i * RING + h * GROUP, GROUP), :]))
            c.then(v.tensor_tensor(posf[:, h], base8[:, h], rank8[:, h], ALU.add))
            v.tensor_copy(posb[:, h], posf[:, h]).then_inc(pos_ready, 1)

        for s in ("counted", "ranked", "looked"):
            dve.sem_inc({"counted": counted, "ranked": ranked, "looked": looked}[s], AHEAD[s] - 1)
        hots(0, 0)
        with dve.Fori(0, RANK_ITERS - 1) as i:
            c.enter(i, 4)
            halves_of(step, i)
        c.leave(RANK_ITERS - 1)
        halves_of(step, RANK_ITERS - 1, True)

    base8 = wts[:, 3776:3792].rearrange("p (h g) -> p h g", h=2)
    rank8 = wts[:, 3792:3808].rearrange("p (h g) -> p h g", h=2)
    scraps = wts[:, 3808 + GROUP * P:3808 + (GROUP + 4) * P].rearrange("p (b e) -> p b e", e=P)

    def rank_scalar(act):
        act.sem_inc(hit_sb, AHEAD["hit_sb"] - 1)
        with act.Fori(0, RANK_ITERS) as i:
            for h in range(2):
                for q in range(2):
                    act.wait_ge(hit_ps, 4 * i + 2 * h + q + 1)
                    nc.scalar.copy(ohhit[0:TILES, h, 4 * q:4 * q + 4].rearrange("p g e -> p (g e)"),
                                   psum[0:TILES, 2 + q, :]).then_inc(hit_sb, 1)

    def rank_tensor(pe):
        t = nc.tensor

        def prepare(i, h):
            m = 4 * i + 2 * h
            pe.wait_ge(rhot, 4 * i + 2 * h + 2)
            for q in range(2):
                pe.wait_ge(hit_sb, m + q - 2 + AHEAD["hit_sb"])
                waited(pe, "pe")
                for b in range(4):
                    mm = t.transpose(psum[0:TILES, 2 + q, b * P:(b + 1) * P], ohhi[:, h, 4 * q + b], ident[:, :])
                mm.then_inc(hit_ps, 1)
            for q in range(2):
                pe.wait_ge(counted, 4 * (m + q) - 5 + AHEAD["counted"])
                for b in range(4):
                    mm = t.matmul(quad(4, q)[0:TILES, b], ohhi[:, h, 4 * q + b], oh[:, h, 4 * q + b],
                                  start=True, stop=True)
                mm.then_inc(added_ps, 1)
            pe.wait_ge(keys_ready, 2 * i + h + 1)
            for q in range(2):
                pe.wait_ge(ranked, 4 * (m + q) - 5 + AHEAD["ranked"])
                for b in range(4):
                    mm = t.matmul(quad(6, q)[:, b], keyb[:, h, 4 * q + b:4 * q + b + 1].to_broadcast([P, P]),
                                  ident[:, :], start=True, stop=True)
                mm.then_inc(keyrow_ps, 1)

        def step(i, h, jn, hn):
            m = 4 * i + 2 * h
            for q in range(2):
                pe.wait_ge(hit_sb, m + q + AHEAD["hit_sb"])
                pe.wait_ge(looked, 4 * (m + q) - 5 + AHEAD["looked"])
                pe.wait_ge(counted, 4 * (m + q) + 2 + AHEAD["counted"])
                for b in range(4 * q, 4 * q + 4):
                    mm = t.matmul(quad(0, q)[:, b % 4], ohhit[0:TILES, h, b], counts[:, b], start=True, stop=True)
                mm.then_inc(look_ps, 1)
            if jn is not None:
                prepare(jn, hn)

        pe.sem_inc(look_ps, AHEAD["look_ps"] - 1)
        prepare(0, 0)
        with pe.Fori(0, RANK_ITERS - 1) as i:
            halves_of(step, i)
        halves_of(step, RANK_ITERS - 1, True)

    def rank_gpsimd(pool):
        for k in range(TABLES):
            pool.wait_ge(table_done[k], ZEROED)
        with pool.Fori(0, RANK_ITERS) as i:
            for b in range(RING):
                if b % GROUP == 0:
                    pool.wait_ge(pos_ready, 2 * i + b // GROUP + 1)
                    waited(pool)
                nc.gpsimd.indirect_dma_start(
                    rec, bass.IndirectOffsetOnAxis(posb[:, b // GROUP, b % GROUP:b % GROUP + 1], 0),
                    recb[:, b // GROUP, b % GROUP, :], None).then_inc(ring[b], 16)
        for b in range(RING):
            pool.wait_ge(ring[b], landed(RANK_ITERS - 1))

    stage_of(vector=rank_vector, scalar=rank_scalar, tensor=rank_tensor, gpsimd=rank_gpsimd)

    rs = kh_i[:, 0:2 * SLOTS].rearrange("p (k e w) -> p k e w", k=NBLK, w=2)
    rsf = kh[:, 2 * SLOTS:4 * SLOTS].rearrange("p (k e w) -> p k e w", k=NBLK, w=2)
    flag_f = kh[:, 4 * SLOTS:5 * SLOTS].rearrange("p (k e) -> p k e", k=NBLK)
    last_f = kh[:, 5 * SLOTS:6 * SLOTS].rearrange("p (k e) -> p k e", k=NBLK)
    word0, word1 = kh[:, 6 * SLOTS:7 * SLOTS], kh[:, 7 * SLOTS:8 * SLOTS]
    word0_i, typ_i = wts[:, 0:SLOTS].bitcast(I32), wts[:, SLOTS:2 * SLOTS].bitcast(I32)
    flag_u = wts[:, 2 * SLOTS:3 * SLOTS].bitcast(U8)[:, 0:SLOTS].rearrange("p (k e) -> p k e", k=NBLK)
    assert 8 * SLOTS <= 10 * COLS + SLOTS
    records_in = sem("records_in")
    flags_set = sem("flags_set")
    flags_out = sem("flags_out")
    starts_in = sem("starts_in")
    words_f = sem("words_f")
    turned = sem("turned")

    def reload_sync(sp):
        sp.dma_start(rs.rearrange("p k e w -> p k (e w)"),
                     rec.rearrange("(k s e) w -> s k (e w)", s=P, e=P)).then_inc(records_in, 16)
        sp.wait_ge(flags_set, 1)
        sp.dma_start(flags.rearrange("(k s) e -> s k e", s=P), flag_u).then_inc(flags_out, 16)
        sp.wait_ge(flags_out, 16)
        for h in range(HEADS):
            sp.dma_start(starts[h * GROUP:(h + 1) * GROUP, :, :],
                         flags.rearrange("(g s) e -> s g e", s=GROUP)).then_inc(starts_in, 16)
        sp.wait_ge(starts_in, 16 * HEADS)

    def reload_vector(dve):
        v, c = nc.vector, v_own.bind(dve)
        dve.wait_ge(records_in, 16)
        c.step(v.tensor_copy(rsf.rearrange("p k e w -> p (k e w)"), rs.rearrange("p k e w -> p (k e w)")))
        c.step(v.memset(flag_f[:, :, 0:1], 1.0))
        c.then(v.memset(last_f[:, :, P - 1:P], 1.0))
        c.step(v.tensor_tensor(flag_f[:, :, 1:P], rsf[:, :, 1:P, 1], rsf[:, :, 0:P - 1, 1], ALU.not_equal))
        v.tensor_tensor(last_f[:, :, 0:P - 1], rsf[:, :, 0:P - 1, 1], rsf[:, :, 1:P, 1],
                        ALU.not_equal).then_inc(words_f, 1)
        c.wait()
        v.tensor_copy(flag_u, flag_f).then_inc(flags_set, 1)
        dve.wait_ge(turned, 3 * NBLK)
        for w, to in enumerate((word0, word1, last[:, :])):
            c.step(v.tensor_copy(to[:, 0:4 * P], psum[:, w, 0:4 * P]))
            c.step(v.tensor_copy(to[:, 4 * P:], psum[:, w + 3, 0:(NBLK - 4) * P]))
        c.wait()
        c.step(v.tensor_tensor(dl[:, :], word1, tile_f, ALU.subtract))
        c.then(v.tensor_copy(word0_i, word0))
        c.step(v.tensor_scalar(src_i[:, :], word0_i, 8191, None, ALU.bitwise_and))
        c.then(v.tensor_scalar(typ_i, word0_i, 13, None, ALU.logical_shift_right))
        c.then(v.scalar_tensor_tensor(rel_i[:, :], src_i[:, :], float(RELS), typ_i, ALU.mult, ALU.add))

    def reload_tensor(pe):
        pe.wait_ge(words_f, 1)
        for w in range(3):
            for k in range(NBLK):
                block = last_f[:, k, :] if w == 2 else rsf[:, k, :, w]
                nc.tensor.transpose(psum[:, w + 3 * (k // 4), (k % 4) * P:(k % 4 + 1) * P],
                                    block, ident[:, :]).then_inc(turned, 1)

    stage_of(sync=reload_sync, vector=reload_vector, tensor=reload_tensor)

    TI = TILES // 2
    flat = rows[:, :, :].rearrange("p r w -> p (r w)")
    place = [0]

    def carve(*shape, part=P, of=flat):
        size = int(np.prod(shape))
        at = place[0]
        place[0] += 2 * size
        assert place[0] <= of.shape[1]
        return [of[0:part, at + p * size:at + (p + 1) * size] for p in range(2)]

    xb, nb, ht = carve(D), carve(D), carve(D)
    stats, mv = carve(6), carve(2)
    ve, sd, rsd, zinv = carve(1), carve(1), carve(1), carve(HEADS)
    common_end = place[0]
    x_in, out_a, out_b = ([sem(f"{n}{p}") for p in range(2)] for n in ("x_in", "out_a", "out_b"))
    var_ready, std_ready, norm_ready = sem("var_ready"), sem("std_ready"), sem("norm_ready")
    turn_ps, ht_ready, proj_ps = sem("turn_ps"), sem("ht_ready"), sem("proj_ps")
    act_evac, dve_evac = sem("act_evac"), sem("dve_evac")
    a_ready, b_ready = sem("a_ready"), sem("b_ready")

    def give(eng, n, *sems):
        for s in sems:
            eng.sem_inc(s, n)

    def tile_loop(eng, lo, step, count=None):
        def both(i, final=False):
            step(i, 0, i, 1)
            step(i, 1, None if final else i + 1, 0)
        with eng.Fori(lo, lo + TI - 1) as i:
            if count:
                v_own.enter(i - lo, count)
            both(i)
        if count:
            v_own.leave(TI - 1)
        both(lo + TI - 1, True)

    def stream(sp, lo, table, outputs, used):
        def load(i, p):
            sp.wait_ge(used, prev(i, p))
            sp.dma_start(xb[p], tile_rows(table, 2 * (i - lo) + p)).then_inc(x_in[p], 16)

        def step(i, p, more):
            if more:
                load(i + 1, p)
            outputs(i, p)
        load(lo, 0)
        load(lo, 1)
        with sp.Fori(lo, lo + TI - 1) as i:
            for p in range(2):
                step(i, p, True)
        for p in range(2):
            step(lo + TI - 1, p, False)

    def stats_of(dve, c, i, p, x):
        c.then(nc.vector.bn_stats(stats[p], x[p]))
        waited(dve, "dve")
        c.then(nc.vector.bn_aggr(mv[p], stats[p]))
        nc.vector.tensor_scalar_add(ve[p], mv[p][:, 1:2], 1e-5).then_inc(var_ready, 1)

    def root(act, i, p):
        act.wait_ge(var_ready, now(i, p))
        nc.scalar.activation(sd[p], ve[p], ACT.Sqrt).then_inc(std_ready, 1)

    def normalise(dve, c, i, p, x):
        dve.wait_ge(std_ready, now(i, p))
        c.then(nc.vector.reciprocal(rsd[p], sd[p]))
        nc.vector.tensor_scalar(nb[p], x[p], mv[p][:, 0:1], rsd[p], ALU.subtract,
                                ALU.mult).then_inc(norm_ready, 1)

    def turn(pe, i, p):
        pe.wait_ge(norm_ready, now(i, p))
        for k in range(2):
            mm = nc.tensor.transpose(psum[:, p, k * P:(k + 1) * P], nb[p][:, k * P:(k + 1) * P], ident[:, :])
        mm.then_inc(turn_ps, 1)

    def turned_relu(act, ip, p):
        act.wait_ge(turn_ps, now(ip, p))
        nc.scalar.activation(ht[p], psum[:, p, 0:D], ACT.Relu).then_inc(ht_ready, 1)

    def project(to, p, w, width, at, size, bias=None):
        for k in range(2):
            mm = nc.tensor.matmul(to, ht[p][:, k * P:(k + 1) * P], w[:, k * width + at:k * width + at + size],
                                  start=k == 0, stop=bias is None and k == 1)
        if bias is not None:
            mm = nc.tensor.matmul(to, ones[0:1, :], bias, start=False, stop=True)
        return mm

    def load_weights(sp, *pairs):
        for to, of in pairs:
            sp.dma_start(to, of).then_inc(weights_sem, 16)

    def kmajor(w, k):
        return w.rearrange("(k p) n -> p k n", p=P)

    W0 = 3 * D
    qv = carve(2 * D)
    qv_ps = sem("qv_ps")
    scale_q = 1.0 / float(np.sqrt(DH))

    def l0_sync(sp):
        load_weights(sp, (wts[:, 0:2 * W0].rearrange("p (k n) -> p k n", k=2), kmajor(a["w0"], 2)),
                     (brow[:, 0:W0], a["b0"]))

        def outputs(i, p):
            sp.wait_ge(a_ready, now(i, p))
            sp.dma_start(tile_rows(qv_tab, 2 * i + p), qv[p]).then_inc(out_a[p], 16)
        stream(sp, 0, a["x"], outputs, b_ready)
        for p in range(2):
            sp.wait_ge(out_a[p], 16 * (TI + 1))

    def l0_vector(dve):
        c = v_own.bind(dve)

        def prepare(i, p):
            dve.wait_ge(x_in[p], 16 * (i + 2))
            stats_of(dve, c, i, p, xb)
            normalise(dve, c, i, p, xb)
            dve.wait_ge(norm_ready, now(i, p))
            dve.sem_inc(b_ready, 1)

        def step(i, p, ni, np_):
            if ni is not None:
                prepare(ni, np_)
            dve.wait_ge(proj_ps, now(i, p))
            nc.vector.tensor_copy(kh3[:, bass.ds(2 * i + p, 1), 0:D].rearrange("p a f -> p (a f)"),
                                  psum[:, 4 + p, 0:D]).then_inc(dve_evac, 1)
        prepare(0, 0)
        tile_loop(dve, 0, step, 2 * 3)

    def l0_scalar(act):
        def prepare(i, p):
            root(act, i, p)
            turned_relu(act, i, p)

        def step(i, p, ni, np_):
            if ni is not None:
                prepare(ni, np_)
            act.wait_ge(qv_ps, now(i, p))
            act.wait_ge(out_a[p], 16 * (i + 1))
            nc.scalar.mul(qv[p][:, 0:D], psum[:, 2 + p, 0:D], scale_q)
            nc.scalar.copy(qv[p][:, D:], psum[:, 2 + p, D:2 * D]).then_inc(a_ready, 1)
        prepare(0, 0)
        tile_loop(act, 0, step)

    def l0_tensor(pe):
        def step(i, p, ni, np_):
            pe.wait_ge(ht_ready, now(i, p))
            pe.wait_ge(a_ready, prev(i, p))
            project(psum[:, 2 + p, :], p, wts, W0, 0, 2 * D, brow[:, 0:2 * D]).then_inc(qv_ps, 1)
            if ni is not None:
                turn(pe, ni, np_)
            pe.wait_ge(dve_evac, prev(i, p))
            project(psum[:, 4 + p, 0:D], p, wts, W0, 2 * D, D, brow[:, 2 * D:3 * D]).then_inc(proj_ps, 1)
        pe.wait_ge(weights_sem, 32)
        turn(pe, 0, 0)
        tile_loop(pe, 0, step)

    def clear_sums(pool):
        nc.gpsimd.memset(acc[:, :], 0.0).then_inc(sums_clear, 1)
    sums_clear = sem("sums_clear")

    stage_of(gpsimd=clear_sums, sync=l0_sync, vector=l0_vector, scalar=l0_scalar, tensor=l0_tensor)

    idx_ready = sem("idx_ready")
    oh_ready, agg_done, acc_done = sem("oh_ready"), sem("agg_done"), sem("acc_done")

    def use(j):
        return j + RANK_ITERS

    def fetch_indices(pool, j, s0, h, table_idx):
        pool.wait_ge(ring[h * GROUP + GROUP - 1], landed(use(j) - 1))
        nc.gpsimd.tensor_copy(idx[:, h * GROUP:(h + 1) * GROUP],
                              table_idx[:, bass.ds(s0 + h * GROUP, GROUP)]).then_inc(idx_ready, 1)
        pool.wait_ge(idx_ready, 2 * j + h + 1)

    def gather(pool, j, b, table, width):
        pool.wait_ge(agg_done, prev(j, b, RING))
        waited(pool)
        nc.gpsimd.indirect_dma_start(rows[:, b, 0:width], None, table,
                                     bass.IndirectOffsetOnAxis(idx[:, b:b + 1], 0)).then_inc(ring[b], 16)

    def slot_tiles(engine, s0, count=RING):
        _, tiles = nc.values_load_multi_w_load_instructions(
            tile_i[0:1, bass.ds(s0, count)], engines=[engine], min_val=0, max_val=TILES - 1,
            skip_runtime_bounds_check_because="a minimum with TILES - 1 made them")
        return tiles

    def one_hots(dve, j, s0, h):
        dve.wait_ge(agg_done, prev(j, h * GROUP + GROUP - 1, RING))
        nc.vector.tensor_tensor(
            oh[:, h], iota_row[:, :].unsqueeze(1).to_broadcast([P, GROUP, P]),
            dl[:, bass.ds(s0 + h * GROUP, GROUP)].unsqueeze(2).to_broadcast([P, GROUP, P]),
            ALU.is_equal).then_inc(oh_ready, 1)

    def aggregate(pe, j, b, at, width, banks=(6, 7)):
        pe.wait_ge(acc_done, now(j, b - len(banks), RING))
        nc.tensor.matmul(psum[:, banks[b % len(banks)], 0:width], oh[:, b // GROUP, b % GROUP],
                         rows[:, b, at:at + width], start=True, stop=True).then_inc(agg_done, 1)

    def accumulate(dve, j, b, tile, width, banks=(6, 7)):
        dve.wait_ge(agg_done, now(j, b, RING))
        dve.wait_ge(acc_done, now(j, b - 1, RING))
        to = acc3[:, bass.ds(tile, 1), 0:width].rearrange("p a f -> p (a f)")
        nc.vector.tensor_tensor(to, to, psum[:, banks[b % len(banks)], 0:width], ALU.add).then_inc(acc_done, 1)

    oht_ps, oht_sb = sem("oht_ps"), sem("oht_sb")
    key_ps, pair_used = sem("key_ps"), sem("pair_used")
    score_ready, score_ps, seg_ready = sem("score_ready"), sem("score_ps"), sem("seg_ready")
    scan_ready, back_ps, best_ready = sem("scan_ready"), sem("back_ps"), sem("best_ready")
    best_ps, max_ready, max_ps = sem("best_ps"), sem("max_ready"), sem("max_ps")
    fall_ready, alpha_ready = sem("fall_ready"), sem("alpha_ready")
    shifted, weight_ready, msg_ready = sem("shifted"), sem("weight_ready"), sem("msg_ready")
    mark_ready, kept, halves_set = sem("mark_ready"), sem("kept"), sem("halves_set")

    def att_place(*shape, part=P, count=2):
        size = int(np.prod(shape))
        at = att_at[0]
        att_at[0] += count * size
        assert att_at[0] <= wts.shape[1]
        return [wts[0:part, at + k * size:at + (k + 1) * size] for k in range(count)]

    att_at = [0]
    GH = GROUP * HEADS
    score = att_place(GH)
    shift = att_place(GH)
    best = att_place(GROUP * (HEADS + 1))
    seg = att_place(P, part=GH)
    run = att_place(P, part=GH)
    pen = att_place(GROUP)
    mark = att_place(9 * HEADS + 1)
    found, ahead = att_place(9 * HEADS), att_place(9 * HEADS)
    both = att_place(2 * 9 * HEADS)
    top, halves = [b[:, 0:9 * HEADS] for b in both], [b[:, 9 * HEADS:] for b in both]
    pair2 = att_place(2 * HEADS)
    edge_half, edge_sum = att_place(2 * GH), att_place(2 * GH)
    mold = att_place(HEADS)
    alpha = att_place(HEADS)

    def hs(ap):
        return ap.rearrange("p (h s) -> p h s", s=GROUP)

    def sh(ap):
        return ap.rearrange("p (s h) -> p s h", h=HEADS)

    def both9(h):
        return both[h].rearrange("p (k h s) -> p k h s", k=2, s=GROUP + 1)

    def h9(ap):
        return ap.rearrange("p (h s) -> p h s", s=GROUP + 1)

    ps_turn = psum[:, 0, :]
    ps_pair = lambda q: psum[:, 2 + q % 2, :]
    ps_score = psum[0:GH, 4, 0:P]
    ps_back = psum[:, 4, P:P + GH]
    ps_best = psum[:, 4, 256:256 + GROUP * 9].rearrange("p (s c) -> p s c", c=9)
    ps_max = psum[:, 4, 384:384 + GH]
    ps_both = psum[:, 4, 384:384 + 2 * GH].rearrange("p (s k h) -> p s k h", k=2, h=HEADS)

    def attention(k, ka, dot, table, width, vat):
        lo = k * ITERS
        shift_j = lo - ka * ITERS
        hi = lo + ITERS - 1
        banks = (1, 5, 6, 7)

        def steps(step, j, final=False):
            step(j, 0, j, 1)
            step(j, 1, None if final else j + 1, 0)

        def slot(j, h):
            return (j - lo) * RING + h * GROUP

        def on_gpsimd(pool):
            with pool.Fori(lo, lo + ITERS) as j:
                for h in range(2):
                    fetch_indices(pool, j, (j - lo) * RING, h, src_i)
                    for b in range(h * GROUP, (h + 1) * GROUP):
                        gather(pool, j, b, table, width)

        def turn_hot(pe, j, h, q):
            i = j - shift_j
            if q == 0:
                pe.wait_ge(oh_ready, 2 * j + h + 1)
            pe.wait_ge(oht_sb, now(i, 2 * h + q - 1, 4))
            for b in range(4):
                mm = nc.tensor.transpose(ps_turn[:, b * P:(b + 1) * P], oh[:, h, 4 * q + b], ident[:, :])
            mm.then_inc(oht_ps, 1)

        def keys_of(pe, j, h, q, tiles):
            i = j - shift_j
            pe.wait_ge(oht_sb, now(i, 2 * h + 1, 4))
            pe.wait_ge(pair_used, now(i, 4 * h + q - 2, 8))
            for b in range(2):
                tile = kh3[:, bass.ds(tiles[2 * q + b], 1), 0:D].rearrange("p a f -> p (a f)")
                mm = nc.tensor.matmul(ps_pair(q)[:, b * D:(b + 1) * D], oht[:, h, 2 * q + b], tile,
                                      start=True, stop=True)
            mm.then_inc(key_ps, 1)

        def turn_scores(pe, j, h):
            pe.wait_ge(score_ready, now(j - shift_j, h))
            waited(pe, "pe")
            nc.tensor.transpose(ps_score, score[h], ident[:, :]).then_inc(score_ps, 1)

        def turn_back(pe, j, h):
            pe.wait_ge(scan_ready, now(j - shift_j, h))
            waited(pe, "pe")
            nc.tensor.transpose(ps_back, run[h], ident[0:GH, 0:GH]).then_inc(back_ps, 1)

        def best_of(pe, j, h):
            pe.wait_ge(best_ready, now(j - shift_j, h))
            for s in range(GROUP):
                mm = nc.tensor.matmul(ps_best[:, s, :], oh[:, h, s],
                                      best[h].rearrange("p (c s) -> p c s", s=GROUP)[:, :, s],
                                      start=True, stop=True)
            mm.then_inc(best_ps, 1)

        def maxima_of(pe, j, h):
            pe.wait_ge(oht_sb, now(j - shift_j, 2 * h + 1, 4))
            if not dot:
                pe.wait_ge(halves_set, 2 * (j - lo) + h + 1)
            pe.wait_ge(max_ready, now(j - shift_j, h))
            for s in range(GROUP):
                if dot:
                    mm = nc.tensor.matmul(sh(ps_max)[:, s, :], oht[:, h, s], h9(top[h])[:, :, s + 1],
                                          start=True, stop=True)
                else:
                    mm = nc.tensor.matmul(ps_both[:, s], oht[:, h, s], both9(h)[:, :, :, s + 1],
                                          start=True, stop=True)
            mm.then_inc(max_ps, 1)

        def sums_of(pe, j, h, slots):
            for s in slots:
                if s % 2 == 0:
                    pe.wait_ge(msg_ready, now(j - shift_j, 4 * h + s // 2, 8))
                aggregate(pe, j, h * GROUP + s, vat, ACCW, banks)

        def tensor_step(pe, j, h, jn, hn):
            more = jn is not None
            if more and dot:
                tiles = slot_tiles(PE, slot(jn, hn), GROUP)
            best_of(pe, j, h)
            if more:
                turn_hot(pe, jn, hn, 0)
            maxima_of(pe, j, h)
            if more:
                turn_hot(pe, jn, hn, 1)
                if dot:
                    keys_of(pe, jn, hn, 0, tiles)
                    keys_of(pe, jn, hn, 1, tiles)
            sums_of(pe, j, h, range(0, 2))
            if more and dot:
                keys_of(pe, jn, hn, 2, tiles)
            if more and not dot:
                turn_scores(pe, jn, hn)
            sums_of(pe, j, h, range(2, 4))
            if more and dot:
                keys_of(pe, jn, hn, 3, tiles)
            if more and not dot:
                turn_back(pe, jn, hn)
            sums_of(pe, j, h, range(4, 8))
            if more and dot:
                turn_scores(pe, jn, hn)
                turn_back(pe, jn, hn)

        def on_tensor(pe):
            turn_hot(pe, lo, 0, 0)
            turn_hot(pe, lo, 0, 1)
            if dot:
                tiles = slot_tiles(PE, 0, GROUP)
                for q in range(4):
                    keys_of(pe, lo, 0, q, tiles)
            turn_scores(pe, lo, 0)
            turn_back(pe, lo, 0)
            with pe.Fori(lo, hi) as j:
                steps(lambda *a: tensor_step(pe, *a), j)
            steps(lambda *a: tensor_step(pe, *a), hi, True)

        def keep_turned(act, j, h, q):
            act.wait_ge(oht_ps, now(j - shift_j, 2 * h + q, 4))
            if q == 0:
                act.wait_ge(max_ps, prev(j - shift_j, h))
            nc.scalar.copy(oht[:, h, 4 * q:4 * q + 4].rearrange("p g e -> p (g e)"),
                           ps_turn).then_inc(oht_sb, 1)

        def marks_of(act, j, h):
            i = j - shift_j
            act.wait_ge(scan_ready, prev(i, h))
            nc.scalar.mul(seg[h], starts[:, bass.ds(2 * (j - lo) + h, 1), :].rearrange("p a e -> p (a e)"),
                          -BIG).then_inc(seg_ready, 1)
            act.wait_ge(max_ready, prev(i, h))
            nc.scalar.mul(h9(mark[h][:, 0:9 * HEADS])[:, :, 1:9],
                          new_tile[:, bass.ds(slot(j, h), GROUP)].unsqueeze(1).to_broadcast([P, HEADS, GROUP]),
                          -BIG).then_inc(mark_ready, 1)

        def fetch_halves(act, j, h):
            act.wait_ge(shifted, prev(j - shift_j, h))
            tiles = slot_tiles(mybir.EngineType.Activation, slot(j, h), GROUP)
            for s in range(GROUP):
                ins = nc.scalar.copy(h9(halves[h])[:, :, s + 1],
                                     adst3[:, bass.ds(tiles[s], 1), :].rearrange("p a f -> p (a f)"))
            ins.then_inc(halves_set, 1)

        def scalar_step(act, j, h, jn, hn):
            i = j - shift_j
            if not dot:
                tiles = slot_tiles(mybir.EngineType.Activation, slot(j, h), GROUP)
            if jn is not None:
                keep_turned(act, jn, hn, 0)
            act.wait_ge(fall_ready, now(i, h))
            nc.scalar.activation(alpha[h], mold[h], ACT.Exp).then_inc(alpha_ready, 1)
            if jn is not None and not dot:
                keep_turned(act, jn, hn, 1)
            act.wait_ge(shifted, now(i, h))
            nc.scalar.activation(rows[:, h * GROUP:(h + 1) * GROUP, vat + D:vat + ACCW], sh(shift[h]),
                                 ACT.Exp).then_inc(weight_ready, 1)
            if jn is not None and dot:
                keep_turned(act, jn, hn, 1)
            if jn is not None:
                marks_of(act, jn, hn)
                if not dot:
                    fetch_halves(act, jn, hn)
            if not dot:
                for s in range(GROUP):
                    act.wait_ge(kept, (j - lo) * RING + h * GROUP + s + 1)
                    nc.scalar.copy(m3[:, bass.ds(tiles[s], 1), :].rearrange("p a f -> p (a f)"),
                                   h9(top[h])[:, :, s + 1]).then_inc(kept, 1)

        def on_scalar(act):
            if not dot:
                act.sem_inc(kept, 1)
            keep_turned(act, lo, 0, 0)
            keep_turned(act, lo, 0, 1)
            marks_of(act, lo, 0)
            if not dot:
                fetch_halves(act, lo, 0)
            with act.Fori(lo, hi) as j:
                steps(lambda *a: scalar_step(act, *a), j)
            steps(lambda *a: scalar_step(act, *a), hi, True)

        def group_rows(h):
            return rows[:, h * GROUP:(h + 1) * GROUP, :]

        def multiply_keys(dve, j, h, q):
            for b in range(2):
                dve.wait_ge(ring[h * GROUP + 2 * q + b], landed(use(j)))
            dve.wait_ge(key_ps, now(j - shift_j, 4 * h + q, 8))
            pair = group_rows(h)[:, 2 * q:2 * q + 2, 0:D]
            nc.vector.tensor_tensor(pair, ps_pair(q).rearrange("p (s f) -> p s f", s=2), pair,
                                    ALU.mult).then_inc(pair_used, 1)

        def sum_scores(dve, j, h):
            dve.wait_ge(pair_used, now(j - shift_j, 4 * h + 3, 8))
            nc.vector.tensor_reduce(score[h].rearrange("p (h s) -> p s h", s=GROUP),
                                    group_rows(h)[:, :, 0:D].rearrange("p s (h d) -> p s h d", h=HEADS),
                                    axis=AX.X, op=ALU.add).then_inc(score_ready, 1)

        def source_scores(dve, c, j, h):
            for b in range(GROUP):
                dve.wait_ge(ring[h * GROUP + b], landed(use(j)))
            nc.vector.tensor_copy(score[h].rearrange("p (h s) -> p s h", s=GROUP),
                                  group_rows(h)[:, :, D:ACCW]).then_inc(score_ready, 1)

        def scan_scores(dve, c, j, h):
            i = j - shift_j
            dve.wait_ge(score_ps, now(i, h))
            dve.wait_ge(seg_ready, now(i, h))
            nc.vector.tensor_tensor_scan(run[h], seg[h], ps_score, -BIG, ALU.add, ALU.max).then_inc(scan_ready, 1)
            c.step(nc.vector.tensor_copy(best[h][:, GH:], last[:, bass.ds(slot(j, h), GROUP)]))

        def take_best(dve, j, h):
            dve.wait_ge(back_ps, now(j - shift_j, h))
            lastg = last[:, bass.ds(slot(j, h), GROUP)]
            nc.vector.tensor_tensor(hs(best[h][:, 0:GH]), hs(ps_back), lastg.unsqueeze(1).to_broadcast([P, HEADS, GROUP]),
                                    ALU.mult).then_inc(best_ready, 1)

        def update_maxima(dve, c, j, h):
            v, i = nc.vector, j - shift_j
            dve.wait_ge(best_ps, now(i, h))
            c.then(v.tensor_scalar(pen[h].unsqueeze(2), ps_best[:, :, HEADS:HEADS + 1], -1.0, BIG,
                                   ALU.add, ALU.mult))
            c.step(v.tensor_tensor(h9(found[h])[:, :, 1:9].rearrange("p h s -> p s h"), ps_best[:, :, 0:HEADS],
                                   pen[h].unsqueeze(2).to_broadcast([P, GROUP, HEADS]), ALU.add))
            c.then(v.tensor_copy(h9(found[h])[:, :, 0], h9(top[1 - h])[:, :, 8]))
            dve.wait_ge(mark_ready, now(i, h))
            c.then(v.tensor_tensor_scan(ahead[h], mark[h][:, 0:9 * HEADS], found[h], -BIG, ALU.add, ALU.max))
            v.tensor_tensor_scan(top[h][:, ::-1], mark[h][:, 1:9 * HEADS + 1][:, ::-1], ahead[h][:, ::-1],
                                 -BIG, ALU.add, ALU.max).then_inc(max_ready, 1)
            dve.wait_ge(max_ready, now(i, h))
            old, new = h9(found[h])[:, :, 0], h9(top[h])[:, :, 0]
            if not dot:
                dve.wait_ge(halves_set, 2 * (j - lo) + h + 1)
                half = h9(halves[h])[:, :, 1]
                c.step(v.tensor_tensor(pair2[h][:, 0:HEADS], old, half, ALU.add))
                c.then(v.tensor_tensor(pair2[h][:, HEADS:], new, half, ALU.add))
                c.then(v.scalar_tensor_tensor(pair2[h], pair2[h], 0.2, pair2[h], ALU.mult, ALU.max))
                old, new = pair2[h][:, 0:HEADS], pair2[h][:, HEADS:]
            v.tensor_tensor(mold[h], old, new, ALU.subtract).then_inc(fall_ready, 1)

        def shift_scores(dve, c, j, h):
            v, i = nc.vector, j - shift_j
            dve.wait_ge(max_ps, now(i, h))
            if dot:
                v.tensor_tensor(sh(shift[h]), score[h].rearrange("p (h s) -> p s h", s=GROUP), sh(ps_max),
                                ALU.subtract).then_inc(shifted, 1)
                return
            c.then(v.tensor_copy(edge_half[h], ps_both.rearrange("p s k h -> p (s k h)")))
            part = edge_half[h].rearrange("p (s k h) -> p s k h", k=2, h=HEADS)
            sums = edge_sum[h].rearrange("p (k s h) -> p k s h", k=2, h=HEADS)
            c.step(v.tensor_tensor(sums[:, 0], score[h].rearrange("p (h s) -> p s h", s=GROUP), part[:, :, 1],
                                   ALU.add))
            c.then(v.tensor_tensor(sums[:, 1], part[:, :, 0], part[:, :, 1], ALU.add))
            c.then(v.scalar_tensor_tensor(edge_sum[h], edge_sum[h], 0.2, edge_sum[h], ALU.mult, ALU.max))
            v.tensor_tensor(shift[h], edge_sum[h][:, 0:GH], edge_sum[h][:, GH:], ALU.subtract).then_inc(shifted, 1)

        def lower_sums(dve, c, j, h, tile):
            v = nc.vector
            dve.wait_ge(alpha_ready, now(j - shift_j, h))
            acc0 = acc3[:, bass.ds(tile, 1), :].rearrange("p a f -> p (a f)")
            dve.wait_ge(acc_done, now(j, h * GROUP - 1, RING))
            c.step(v.tensor_tensor(acc0[:, 0:D].rearrange("p (h d) -> p h d", h=HEADS),
                                   acc0[:, 0:D].rearrange("p (h d) -> p h d", h=HEADS),
                                   alpha[h].unsqueeze(2).to_broadcast([P, HEADS, DH]), ALU.mult))
            c.step(v.tensor_tensor(acc0[:, D:ACCW], acc0[:, D:ACCW], alpha[h], ALU.mult))

        def weigh_values(dve, j, h, q):
            if q == 0:
                dve.wait_ge(weight_ready, now(j - shift_j, h))
            val = group_rows(h)[:, 2 * q:2 * q + 2, vat:vat + D].rearrange("p s (h d) -> p s h d", h=HEADS)
            wgt = group_rows(h)[:, 2 * q:2 * q + 2, vat + D:vat + ACCW]
            nc.vector.tensor_tensor(val, val, wgt.unsqueeze(3).to_broadcast([P, 2, HEADS, DH]),
                                    ALU.mult).then_inc(msg_ready, 1)

        def vector_step(dve, c, j, h, jn, hn, first=False):
            more = jn is not None
            back = 0 if first else 4
            tiles = slot_tiles(DVE, slot(j, h) - back, GROUP + back)

            def add_before(slots):
                for s in slots:
                    b = h * GROUP - 4 + s
                    accumulate(dve, j if b >= 0 else j - 1, b % RING, tiles[s], ACCW, banks)

            def add(s):
                accumulate(dve, j, h * GROUP + s, tiles[back + s], ACCW, banks)

            take_best(dve, j, h)
            if more:
                one_hots(dve, jn, slot(jn, 0), hn)
            add_before(range(0, back // 2))
            update_maxima(dve, c, j, h)
            add_before(range(back // 2, back))
            shift_scores(dve, c, j, h)
            lower_sums(dve, c, j, h, tiles[back])
            weigh_values(dve, j, h, 0)
            if more and not dot:
                source_scores(dve, c, jn, hn)
            for q in range(1, 4):
                weigh_values(dve, j, h, q)
            c.wait()
            if dot:
                for s in range(4):
                    if more:
                        multiply_keys(dve, jn, hn, s)
                    add(s)
                if more:
                    sum_scores(dve, jn, hn)
                    scan_scores(dve, c, jn, hn)
            else:
                add(0)
                add(1)
                if more:
                    scan_scores(dve, c, jn, hn)
                add(2)
                add(3)
            if not more:
                for s in range(4, 8):
                    accumulate(dve, j, h * GROUP + s, tiles[back + s], ACCW, banks)

        def on_vector(dve):
            v, c = nc.vector, v_own.bind(dve)
            if dot:
                dve.wait_ge(sums_clear, 1)
            else:
                c.step(v.memset(acc[:, :], 0.0))
            for h in range(2):
                c.step(v.memset(h9(mark[h][:, 0:9 * HEADS])[:, :, 0], -BIG))
                c.step(v.memset(mark[h][:, 9 * HEADS:], -BIG))
            c.then(v.memset(top[1], -BIG))
            one_hots(dve, lo, 0, 0)
            if dot:
                for q in range(4):
                    multiply_keys(dve, lo, 0, q)
                sum_scores(dve, lo, 0)
            else:
                source_scores(dve, c, lo, 0)
            scan_scores(dve, c, lo, 0)
            vector_step(dve, c, lo, 0, lo, 1, first=True)
            vector_step(dve, c, lo, 1, lo + 1, 0)
            with dve.Fori(lo + 1, hi) as j:
                c.enter(j - lo - 1, ATT_STEPS[dot])
                steps(lambda *a: vector_step(dve, c, *a), j)
            c.leave(ITERS - 2)
            steps(lambda *a: vector_step(dve, c, *a), hi, True)
            dve.wait_ge(acc_done, now(hi, RING - 1, RING))

        stage_of(gpsimd=on_gpsimd, tensor=on_tensor, scalar=on_scalar, vector=on_vector)

    ATT_STEPS = {True: 2 * 7, False: 2 * 14}
    attention(0, 0, True, qv_tab, 2 * D, D)

    place[0] = common_end
    x1b, h1f = carve(D), carve(2)

    def l0e_sync(sp):
        def outputs(i, p):
            t = 2 * (i - TI) + p
            sp.wait_ge(a_ready, now(i, p))
            sp.dma_start(tile_rows(x1_tab, t), x1b[p]).then_inc(out_a[p], 16)
            sp.wait_ge(b_ready, now(i, p))
            sp.dma_start(tile_rows(h1_tab, t),
                         kh3[:, bass.ds(t, 1), 0:D].rearrange("p a f -> p (a f)")).then_inc(out_b[p], 16)
        stream(sp, TI, a["x"], outputs, a_ready)
        for p in range(2):
            sp.wait_ge(out_a[p], 16 * (2 * TI + 1))
            sp.wait_ge(out_b[p], 16 * (TI + 1))

    def l0e_vector(dve):
        v, c = nc.vector, v_own.bind(dve)

        def prepare(i, p):
            total = acc3[:, bass.ds(2 * (i - TI) + p, 1), :].rearrange("p a f -> p (a f)")
            c.then(v.tensor_scalar_max(zinv[p], total[:, D:ACCW], 1e-16))
            c.then(v.reciprocal(zinv[p], zinv[p]))
            dve.wait_ge(out_a[p], 16 * (i + 1))
            c.then(v.tensor_tensor(x1b[p].rearrange("p (h d) -> p h d", h=HEADS),
                                   total[:, 0:D].rearrange("p (h d) -> p h d", h=HEADS),
                                   zinv[p].unsqueeze(2).to_broadcast([P, HEADS, DH]), ALU.mult))
            dve.wait_ge(x_in[p], 16 * (i + 2))
            v.tensor_tensor(x1b[p], x1b[p], xb[p], ALU.add).then_inc(a_ready, 1)
            dve.wait_ge(a_ready, now(i, p))
            stats_of(dve, c, i, p, x1b)

        def step(i, p, ni, np_):
            if ni is not None:
                prepare(ni, np_)
            normalise(dve, c, i, p, x1b)
            dve.wait_ge(norm_ready, now(i, p))
            v.tensor_scalar_max(kh3[:, bass.ds(2 * (i - TI) + p, 1), 0:D].rearrange("p a f -> p (a f)"), nb[p],
                                0.0).then_inc(b_ready, 1)
        c.then(v.memset(kh3[:, :, D:KHW], 1.0))
        prepare(TI, 0)
        tile_loop(dve, TI, step, 2 * 6)

    def l0e_scalar(act):
        root(act, TI, 0)
        tile_loop(act, TI, lambda i, p, ni, np_: ni is not None and root(act, ni, np_))

    stage_of(sync=l0e_sync, vector=l0e_vector, scalar=l0e_scalar)

    OUT_AT = ROW - SUMW
    srcb = [wts[:, h * GROUP:(h + 1) * GROUP] for h in range(2)]
    dup = [wts[:, 16 + h * GROUP:16 + (h + 1) * GROUP] for h in range(2)]
    away = [wts[:, 32 + h * GROUP:32 + (h + 1) * GROUP] for h in range(2)]
    scrap1 = wts[:, 64:64 + P]
    src_f = wts[:, 2560:2560 + SLOTS]
    merged = wts[:, 256:256 + 2 * GROUP * P].rearrange("p (h g e) -> p h g e", h=2, g=GROUP)
    srcb_ready, row_ps, same_ready = sem("srcb_ready"), sem("row_ps"), sem("same_ready")
    merged_ps, merged_sb = sem("merged_ps"), sem("merged_sb")
    out_ps, out_sb, idx2_ready = sem("out_ps"), sem("out_sb"), sem("idx2_ready")
    USES = RING // TABLES
    same = oht
    K1 = ITERS

    def l1_gpsimd(pool):
        pool.wait_ge(ones_set, 1)
        with pool.Fori(K1, K1 + ITERS) as j:
            i = j - K1
            for h in range(2):
                fetch_indices(pool, j, i * RING, h, src_i)
                for b in range(h * GROUP, (h + 1) * GROUP):
                    gather(pool, j, b, h1_tab, D)
                for b in range(h * GROUP, (h + 1) * GROUP):
                    k, n = b % TABLES, b // TABLES
                    pool.wait_ge(out_sb, now(i, b, RING))
                    pool.wait_ge(idx2_ready, now(i, h))
                    pool.wait_ge(table_done[k], ZEROED + 16 * (i * USES + n))
                    waited(pool)
                    nc.gpsimd.indirect_dma_start(
                        src_sum[k], bass.IndirectOffsetOnAxis(idx2[:, b:b + 1], 0),
                        rows[:, b, OUT_AT:OUT_AT + SUMW], None, compute_op=ALU.add).then_inc(table_done[k], 16)
        for k in range(TABLES):
            pool.wait_ge(table_done[k], ZEROED + 16 * ITERS * USES)

    def l1_vector(dve):
        v, c = nc.vector, v_own.bind(dve)
        v.memset(acc[:, :], 0.0)
        v.memset(rows[:, :, :], 1.0)
        c.then(v.tensor_copy(src_f, src_i[:, :]))
        dve.sem_inc(ones_set, 1)
        with dve.Fori(K1, K1 + ITERS) as j:
            i = j - K1
            c.enter(i, 2 * (GROUP + 2))
            s0 = i * RING
            tiles = slot_tiles(DVE, s0)
            for h in range(2):
                one_hots(dve, j, s0, h)
                for q in range(2):
                    dve.wait_ge(out_ps, prev(i, h * GROUP + 4 * q + 3, RING))
                v.tensor_copy(srcb[h], src_f[:, bass.ds(s0 + h * GROUP, GROUP)]).then_inc(srcb_ready, 1)
                dve.wait_ge(srcb_ready, now(i, h))
                for q in range(2):
                    dve.wait_ge(row_ps, now(i, 2 * h + q, 4))
                    v.tensor_tensor(same[:, h, 4 * q:4 * q + 4], psum[:, q, :].rearrange("p (g e) -> p g e", g=4),
                                    srcb[h][:, 4 * q:4 * q + 4].unsqueeze(2).to_broadcast([P, 4, P]),
                                    ALU.is_equal).then_inc(same_ready, 1)
                for q in range(2):
                    dve.wait_ge(same_ready, now(i, 2 * h + q, 4))
                    for b in range(4):
                        c.then(v.tensor_tensor_reduce(out=scrap1, in0=same[:, h, 4 * q + b], in1=lower[:, :],
                                                      scale=1.0, scalar=0.0, op0=ALU.mult, op1=ALU.add,
                                                      accum_out=dup[h][:, 4 * q + b:4 * q + b + 1]))
                c.then(v.tensor_scalar(away[h], srcb[h], -1.0, spare[:, :], ALU.mult, ALU.add))
                c.then(v.scalar_tensor_tensor(away[h], dup[h], 1.0, away[h], ALU.min, ALU.mult))
                for k in range(TABLES):
                    dve.wait_ge(table_done[k], ZEROED + 16 * ((i - 1) * USES + 2 * h + 2))
                v.tensor_tensor(idx2[:, h * GROUP:(h + 1) * GROUP], away[h], srcb[h], ALU.add).then_inc(idx2_ready, 1)
                for b in range(h * GROUP, (h + 1) * GROUP):
                    accumulate(dve, j, b, tiles[b], KHW)
        c.leave(ITERS)
        dve.wait_ge(acc_done, now(K1 + ITERS - 1, RING - 1, RING))

    def l1_scalar(act):
        act.wait_ge(ones_set, 1)
        with act.Fori(K1, K1 + ITERS) as j:
            i = j - K1
            for h in range(2):
                for q in range(2):
                    act.wait_ge(merged_ps, now(i, 2 * h + q, 4))
                    nc.scalar.copy(merged[:, h, 4 * q:4 * q + 4].rearrange("p g e -> p (g e)"),
                                   psum[:, 2 + q, :]).then_inc(merged_sb, 1)
                for b in range(h * GROUP, (h + 1) * GROUP):
                    act.wait_ge(out_ps, now(i, b, RING))
                    act.wait_ge(table_done[b % TABLES], ZEROED + 16 * ((i - 1) * USES + b // TABLES + 1))
                    nc.scalar.copy(rows[:, b, OUT_AT:OUT_AT + KHW], psum[:, 4 + b % 2, 0:KHW]).then_inc(out_sb, 1)

    def l1_tensor(pe):
        t = nc.tensor
        pe.wait_ge(ones_set, 1)
        with pe.Fori(K1, K1 + ITERS) as j:
            i = j - K1
            tiles = slot_tiles(PE, i * RING)
            for h in range(2):
                pe.wait_ge(srcb_ready, now(i, h))
                for q in range(2):
                    pe.wait_ge(same_ready, now(i, 2 * h + q - 2, 4))
                    for b in range(4):
                        mm = t.matmul(psum[:, q, b * P:(b + 1) * P],
                                      srcb[h][:, 4 * q + b:4 * q + b + 1].to_broadcast([P, P]), ident[:, :],
                                      start=True, stop=True)
                    mm.then_inc(row_ps, 1)
                pe.wait_ge(oh_ready, 2 * j + h + 1)
                for q in range(2):
                    pe.wait_ge(same_ready, now(i, 2 * h + q, 4))
                    pe.wait_ge(merged_sb, now(i, 2 * h + q - 2, 4))
                    for b in range(4):
                        mm = t.matmul(psum[:, 2 + q, b * P:(b + 1) * P], oh[:, h, 4 * q + b],
                                      same[:, h, 4 * q + b], start=True, stop=True)
                    mm.then_inc(merged_ps, 1)
                for b in range(GROUP):
                    n = h * GROUP + b
                    if b % 4 == 0:
                        pe.wait_ge(merged_sb, now(i, 2 * h + b // 4, 4))
                    pe.wait_ge(out_sb, now(i, n - 2, RING))
                    tile = kh3[:, bass.ds(tiles[n], 1), :].rearrange("p a f -> p (a f)")
                    t.matmul(psum[:, 4 + b % 2, 0:KHW], merged[:, h, b], tile, start=True, stop=True).then_inc(out_ps, 1)
                for b in range(GROUP):
                    n = h * GROUP + b
                    pe.wait_ge(ring[n], landed(use(j)))
                    aggregate(pe, j, n, 0, KHW)

    ones_set = sem("ones_set")
    stage_of(gpsimd=l1_gpsimd, vector=l1_vector, scalar=l1_scalar, tensor=l1_tensor)

    place[0] = 0
    gx, gsum, gin, gout, gh, ght = (carve(n) for n in (D, TABLES * SUMW, D, D, D, D))
    gate, cand, cnt, cmax, cinv, cone = (carve(n) for n in (2 * D, D, 2, 2, 2, 2))
    gind = carve(2 * P, part=1)
    oh_flat, place[0] = oh[:, :, :, :].rearrange("p h g e -> p (h g e)"), 0
    gt, gct = carve(4 * P, of=oh_flat), carve(4 * P, of=oh_flat)
    w_in, w_out = wts[:, 0:2 * D], wts[:, 2 * D:4 * D]
    w_ih, w_hh = wts[:, 4 * D:16 * D], wts[:, 16 * D:22 * D]
    b_in, b_out, b_ih, b_hh = brow[:, 0:D], brow[:, D:2 * D], brow[:, 2 * D:5 * D], brow[:, 5 * D:8 * D]
    g_in = [sem("g_in0"), sem("g_in1")]
    gx_in = [sem("gx_in0"), sem("gx_in1")]
    g_out = [sem("g_out0"), sem("g_out1")]
    cand_ps, bias_ready = sem("cand_ps"), sem("bias_ready")
    pre_ready, gt_ps, gt_sb, conv_ps, conv_sb = (sem(n) for n in ("pre_ready", "gt_ps", "gt_sb", "conv_ps", "conv_sb"))
    gate_ps, gate_sb, new_ready, cand_ready, x2_ready = (
        sem(n) for n in ("gate_ps", "gate_sb", "new_ready", "cand_ready", "x2_ready"))

    def gru_sync(sp):
        load_weights(sp, (w_in.rearrange("p (k n) -> p k n", k=2), kmajor(a["w_in"], 2)),
                     (w_out.rearrange("p (k n) -> p k n", k=2), kmajor(a["w_out"], 2)),
                     (w_ih.rearrange("p (k n) -> p k n", k=4), kmajor(a["w_ih"], 4)),
                     (w_hh.rearrange("p (k n) -> p k n", k=2), kmajor(a["w_hh"], 2)),
                     (brow[:, 0:8 * D], a["b1"]))

        def load_sums(i, p):
            sp.wait_ge(pre_ready, prev(i, p))
            for k in range(TABLES):
                sp.dma_start(gsum[p][:, k * SUMW:(k + 1) * SUMW],
                             tile_rows(src_sum[k], 2 * i + p)).then_inc(g_in[p], 16)

        def load_x1(i, p):
            sp.wait_ge(g_out[p], 16 * (i + 1))
            sp.dma_start(gx[p], tile_rows(x1_tab, 2 * i + p)).then_inc(gx_in[p], 16)

        def store(i, p):
            sp.wait_ge(x2_ready, now(i, p))
            sp.dma_start(tile_rows(x2_tab, 2 * i + p), gx[p]).then_inc(g_out[p], 16)
        for p in range(2):
            load_sums(0, p)
            load_x1(0, p)
        with sp.Fori(0, TI - 1) as i:
            for p in range(2):
                load_sums(i + 1, p)
                store(i, p)
                load_x1(i + 1, p)
        for p in range(2):
            store(TI - 1, p)
            sp.wait_ge(g_out[p], 16 * (TI + 1))

    def gru_vector(dve):
        v, c = nc.vector, v_own.bind(dve)

        def prepare(i, p):
            t = 2 * i + p
            total = acc3[:, bass.ds(t, 1), :].rearrange("p a f -> p (a f)")
            part = [gsum[p][:, k * SUMW:k * SUMW + KHW] for k in range(TABLES)]
            dve.wait_ge(g_in[p], 16 * TABLES * (i + 1))
            c.step(v.tensor_tensor(part[2], part[2], part[3], ALU.add))
            c.step(v.tensor_tensor(part[0], part[0], part[1], ALU.add))
            c.then(v.tensor_copy(cnt[p][:, 0:1], total[:, D:KHW]))
            c.then(v.tensor_tensor(part[0], part[0], part[2], ALU.add))
            c.then(v.tensor_copy(cnt[p][:, 1:2], part[0][:, D:KHW]))
            c.step(v.tensor_scalar_min(cone[p], cnt[p], 1.0))
            c.then(v.tensor_scalar_max(cmax[p], cnt[p], 1.0))
            c.then(v.reciprocal(cinv[p], cmax[p]))
            c.step(v.tensor_copy(rdeg[:, bass.ds(t, 1)], cinv[p][:, 0:1]))
            v.tensor_scalar(gin[p], total[:, 0:D], cinv[p][:, 0:1], None, ALU.mult)
            v.tensor_scalar(gout[p], part[0][:, 0:D], cinv[p][:, 1:2], None, ALU.mult)
            v.tensor_copy(gh[p], kh3[:, bass.ds(t, 1), 0:D].rearrange("p a f -> p (a f)")).then_inc(pre_ready, 1)

        def step(i, p, ni, np_):
            if ni is not None:
                prepare(ni, np_)
            dve.wait_ge(pre_ready, now(i, p))
            dve.wait_ge(gx_in[p], 16 * (i + 1))
            c.step(v.tensor_tensor(gx[p], gx[p], gh[p], ALU.add))
            dve.wait_ge(gate_sb, now(i, p))
            dve.wait_ge(cand_ps, now(i, p))
            c.then(v.tensor_tensor(gate[p][:, 0:D], gate[p][:, 0:D], psum[:, 5 + 2 * p, D:2 * D], ALU.mult))
            v.tensor_tensor(gate[p][:, 0:D], gate[p][:, 0:D], psum[:, 5 + 2 * p, 0:D], ALU.add).then_inc(new_ready, 1)
            dve.wait_ge(cand_ready, now(i, p))
            c.then(v.tensor_tensor(cand[p], cand[p], gh[p], ALU.subtract))
            c.then(v.tensor_tensor(cand[p], cand[p], gate[p][:, D:2 * D], ALU.mult))
            c.then(v.tensor_tensor(gx[p], gx[p], cand[p], ALU.add))
            dve.sem_inc(x2_ready, 1)
        dve.wait_ge(weights_sem, 32 + 80)
        c.then(v.tensor_tensor(b_ih[:, 0:2 * D], b_ih[:, 0:2 * D], b_hh[:, 0:2 * D], ALU.add))
        dve.sem_inc(bias_ready, 1)
        prepare(0, 0)
        tile_loop(dve, 0, step, 2 * 14)

    def gru_scalar(act):
        s = nc.scalar

        def turned(i, p):
            act.wait_ge(gt_ps, now(i, p))
            s.copy(gt[p], psum[:, 0, :])
            s.copy(ght[p], psum[:, 1, 0:D])
            s.copy(gind[p], psum[0:1, 1, D:2 * D]).then_inc(gt_sb, 1)

        def convolved(i, p):
            act.wait_ge(conv_ps, now(i, p))
            s.copy(gct[p], psum[:, 2 + p, :]).then_inc(conv_sb, 1)

        def step(i, p, ni, np_):
            act.wait_ge(gate_ps, now(i, p))
            s.activation(gate[p], psum[:, 4 + 2 * p, :], ACT.Sigmoid).then_inc(gate_sb, 1)
            if ni is not None:
                turned(ni, np_)
                convolved(ni, np_)
            act.wait_ge(new_ready, now(i, p))
            s.activation(cand[p], gate[p][:, 0:D], ACT.Tanh).then_inc(cand_ready, 1)
        turned(0, 0)
        convolved(0, 0)
        tile_loop(act, 0, step)

    def gru_tensor(pe):
        t = nc.tensor

        def turn_all(i, p):
            pe.wait_ge(pre_ready, now(i, p))
            pe.wait_ge(gt_sb, now(i, p - 1))
            for w, of in enumerate((gin[p], gout[p])):
                for k in range(2):
                    t.transpose(psum[:, 0, (2 * w + k) * P:(2 * w + k + 1) * P], of[:, k * P:(k + 1) * P], ident[:, :])
            for k in range(2):
                t.transpose(psum[:, 1, k * P:(k + 1) * P], gh[p][:, k * P:(k + 1) * P], ident[:, :])
            for w in range(2):
                mm = t.matmul(psum[0:1, 1, D + w * P:D + (w + 1) * P], cone[p][:, w:w + 1], ident[:, :],
                              start=True, stop=True)
            mm.then_inc(gt_ps, 1)

        def convolve(i, p):
            pe.wait_ge(gt_sb, now(i, p))
            pe.wait_ge(conv_sb, prev(i, p))
            for w, (wc, bc) in enumerate(((w_in, b_in), (w_out, b_out))):
                for o in range(2):
                    to = psum[:, 2 + p, (2 * w + o) * P:(2 * w + o + 1) * P]
                    for k in range(2):
                        t.matmul(to, wc[:, k * D + o * P:k * D + (o + 1) * P],
                                 gt[p][:, (2 * w + k) * P:(2 * w + k + 1) * P], start=k == 0, stop=False)
                    mm = t.matmul(to, bc[:, o * P:(o + 1) * P], gind[p][:, w * P:(w + 1) * P],
                                  start=False, stop=True)
            mm.then_inc(conv_ps, 1)

        def gates(i, p):
            bank = psum[:, 4 + 2 * p, :]
            pe.wait_ge(conv_sb, now(i, p))
            pe.wait_ge(gate_sb, prev(i, p))
            for k in range(4):
                t.matmul(bank, gct[p][:, k * P:(k + 1) * P], w_ih[:, k * 3 * D:k * 3 * D + 2 * D],
                         start=k == 0, stop=False)
            for k in range(2):
                t.matmul(bank, ght[p][:, k * P:(k + 1) * P], w_hh[:, k * 3 * D:k * 3 * D + 2 * D],
                         start=False, stop=False)
            t.matmul(bank, ones[0:1, :], b_ih[:, 0:2 * D], start=False, stop=True).then_inc(gate_ps, 1)

        def candidate_in(i, p):
            bank = psum[:, 5 + 2 * p, :]
            pe.wait_ge(new_ready, prev(i, p))
            for k in range(4):
                t.matmul(bank[:, 0:D], gct[p][:, k * P:(k + 1) * P],
                         w_ih[:, k * 3 * D + 2 * D:(k + 1) * 3 * D], start=k == 0, stop=False)
            t.matmul(bank[:, 0:D], ones[0:1, :], b_ih[:, 2 * D:3 * D], start=False, stop=True)

        def candidate_hidden(i, p):
            bank = psum[:, 5 + 2 * p, :]
            for k in range(2):
                t.matmul(bank[:, D:2 * D], ght[p][:, k * P:(k + 1) * P],
                         w_hh[:, k * 3 * D + 2 * D:(k + 1) * 3 * D], start=k == 0, stop=False)
            t.matmul(bank[:, D:2 * D], ones[0:1, :], b_hh[:, 2 * D:3 * D], start=False,
                     stop=True).then_inc(cand_ps, 1)

        def step(i, p, ni, np_):
            gates(i, p)
            if ni is not None:
                turn_all(ni, np_)
            candidate_in(i, p)
            if ni is not None:
                convolve(ni, np_)
            candidate_hidden(i, p)
        pe.wait_ge(weights_sem, 32 + 80)
        pe.wait_ge(bias_ready, 1)
        turn_all(0, 0)
        convolve(0, 0)
        tile_loop(pe, 0, step)

    stage_of(sync=gru_sync, vector=gru_vector, scalar=gru_scalar, tensor=gru_tensor)

    place[0] = common_end
    W2 = RELS * D + D
    kh_flat = kh[:, :]
    place[0] = 0
    hwb = carve(RELS * D, of=kh_flat)
    xsb = carve(D, of=kh_flat)
    chunk_ps, chunk_act, chunk_dve = sem("chunk_ps"), sem("chunk_act"), sem("chunk_dve")
    CHUNKS = [(0, 512), (512, 512), (1024, 512), (1536, 512), (2048, 256)]
    ON_ACT = 3

    def rel_sync(sp):
        load_weights(sp, (wts[:, 0:2 * W2].rearrange("p (k n) -> p k n", k=2), kmajor(a["w2"], 2)),
                     (brow[:, 0:D], a["b2"]))

        def outputs(i, p):
            li = i - 2 * TI
            sp.wait_ge(a_ready, now(i, p))
            waited(sp, "sp")
            sp.wait_ge(chunk_act, now(li, 3 * p + 2, 6))
            sp.dma_start(hw_tab[bass.ds((2 * li + p) * P * RELS, P * RELS), :].rearrange("(n r) f -> n (r f)", r=RELS),
                         hwb[p]).then_inc(out_a[p], 16)
            sp.wait_ge(b_ready, now(i, p))
            sp.dma_start(tile_rows(xs_tab, 2 * li + p), xsb[p]).then_inc(out_b[p], 16)
        stream(sp, 2 * TI, x2_tab, outputs, norm_ready)
        for p in range(2):
            sp.wait_ge(out_a[p], 16 * (3 * TI + 1))
            sp.wait_ge(out_b[p], 16 * (2 * TI + 1))

    def rel_vector(dve):
        v, c = nc.vector, v_own.bind(dve)

        def prepare(i, p):
            dve.wait_ge(x_in[p], 16 * (i + 2))
            dve.wait_ge(out_b[p], 16 * (i - TI + 1))
            c.then(v.tensor_copy(xsb[p], xb[p]))
            stats_of(dve, c, i, p, xb)
            normalise(dve, c, i, p, xb)

        def step(i, p, ni, np_):
            li = i - 2 * TI
            if ni is not None:
                prepare(ni, np_)
            dve.wait_ge(chunk_ps, now(li, 5 * p + 3, 10))
            dve.wait_ge(out_a[p], 16 * (i + 1))
            v.tensor_copy(hwb[p][:, 1536:2048], psum[:, 5, :]).then_inc(chunk_dve, 1)
            dve.wait_ge(chunk_dve, now(li, 2 * p, 4))
            dve.sem_inc(a_ready, 1)
            dve.wait_ge(chunk_ps, now(li, 5 * p + 4, 10))
            v.tensor_tensor(xsb[p], psum[:, 6, 0:D], xsb[p], ALU.add).then_inc(chunk_dve, 1)
            dve.wait_ge(chunk_dve, now(li, 2 * p + 1, 4))
            dve.sem_inc(b_ready, 1)
        prepare(2 * TI, 0)
        tile_loop(dve, 2 * TI, step, 2 * 4)

    def rel_scalar(act):
        def prepare(i, p):
            root(act, i, p)
            turned_relu(act, i - TI, p)

        def step(i, p, ni, np_):
            li = i - 2 * TI
            act.wait_ge(out_a[p], 16 * (i + 1))
            for k, (at, size) in enumerate(CHUNKS[:ON_ACT]):
                act.wait_ge(chunk_ps, now(li, 5 * p + k, 10))
                nc.scalar.copy(hwb[p][:, at:at + size], psum[:, 2 + k, :]).then_inc(chunk_act, 1)
                if k == 1 and ni is not None:
                    prepare(ni, np_)
        prepare(2 * TI, 0)
        tile_loop(act, 2 * TI, step)

    def rel_tensor(pe):
        def step(i, p, ni, np_):
            li = i - 2 * TI
            pe.wait_ge(ht_ready, now(i - TI, p))
            for k, (at, size) in enumerate(CHUNKS):
                if k == 3 and ni is not None:
                    turn(pe, ni, np_)
                if k < ON_ACT:
                    pe.wait_ge(chunk_act, now(li, 3 * (p - 1) + k, 6))
                else:
                    pe.wait_ge(chunk_dve, now(li, 2 * (p - 1) + k - ON_ACT, 4))
                project(psum[:, 2 + k, 0:size], p, wts, W2, at, size,
                        brow[:, 0:D] if k == 4 else None).then_inc(chunk_ps, 1)
        pe.wait_ge(weights_sem, 32 + 80 + 32)
        turn(pe, 2 * TI, 0)
        tile_loop(pe, 2 * TI, step)

    stage_of(gpsimd=clear_sums, sync=rel_sync, vector=rel_vector, scalar=rel_scalar, tensor=rel_tensor)

    K2 = 2 * ITERS

    def l2_gpsimd(pool):
        with pool.Fori(K2, K2 + ITERS) as j:
            for h in range(2):
                fetch_indices(pool, j, (j - K2) * RING, h, rel_i)
                for b in range(h * GROUP, (h + 1) * GROUP):
                    gather(pool, j, b, hw_tab, D)

    def l2_vector(dve):
        dve.wait_ge(sums_clear, 2)
        with dve.Fori(K2, K2 + ITERS) as j:
            s0 = (j - K2) * RING
            tiles = slot_tiles(DVE, s0)
            for h in range(2):
                one_hots(dve, j, s0, h)
                for b in range(h * GROUP, (h + 1) * GROUP):
                    accumulate(dve, j, b, tiles[b], D)
        dve.wait_ge(acc_done, now(K2 + ITERS - 1, RING - 1, RING))

    def l2_tensor(pe):
        with pe.Fori(K2, K2 + ITERS) as j:
            for h in range(2):
                pe.wait_ge(oh_ready, 2 * j + h + 1)
                for b in range(h * GROUP, (h + 1) * GROUP):
                    pe.wait_ge(ring[b], landed(use(j)))
                    aggregate(pe, j, b, 0, D)

    stage_of(gpsimd=l2_gpsimd, vector=l2_vector, tensor=l2_tensor)

    place[0] = common_end
    x3b, xr = carve(D), carve(ACCW)
    prod, aself, aleak = carve(2 * D), carve(HEADS), carve(HEADS)
    att_in, x_used = sem("att_in"), sem("x_used")
    att_src, att_dst = bcast[:, 0:D], bcast[:, D:2 * D]

    def l3_sync(sp):
        load_weights(sp, (wts[:, 0:2 * D].rearrange("p (k n) -> p k n", k=2), kmajor(a["w3"], 2)))
        sp.dma_start(bcast, a["rows3"].to_broadcast([P, 5 * D])).then_inc(att_in, 16)

        def outputs(i, p):
            t = 2 * (i - 3 * TI) + p
            sp.wait_ge(a_ready, now(i, p))
            sp.dma_start(tile_rows(x3_tab, t), x3b[p]).then_inc(out_b[p], 16)
            sp.wait_ge(b_ready, now(i, p))
            sp.dma_start(tile_rows(xh_tab, t), xr[p]).then_inc(out_a[p], 16)
        stream(sp, 3 * TI, xs_tab, outputs, a_ready)
        for p in range(2):
            sp.wait_ge(out_a[p], 16 * (4 * TI + 1))
            sp.wait_ge(out_b[p], 16 * (3 * TI + 1))

    def l3_vector(dve):
        v, c = nc.vector, v_own.bind(dve)

        def prepare(i, p):
            t = 2 * (i - 3 * TI) + p
            dve.wait_ge(x_in[p], 16 * (i + 2))
            dve.wait_ge(out_b[p], 16 * (i - TI + 1))
            v.scalar_tensor_tensor(x3b[p], acc3[:, bass.ds(t, 1), 0:D].rearrange("p a f -> p (a f)"),
                                   rdeg[:, bass.ds(t, 1)], xb[p], ALU.mult, ALU.add).then_inc(x_used, 1)
            dve.wait_ge(x_used, 2 * (i - 3 * TI) + p + 1)
            stats_of(dve, c, i, p, x3b)
            normalise(dve, c, i, p, x3b)
            dve.wait_ge(norm_ready, now(i, p))
            v.scalar_tensor_tensor(x3b[p], nb[p], 0.0, x3b[p], ALU.max, ALU.add).then_inc(a_ready, 1)

        def step(i, p, ni, np_):
            t = 2 * (i - 3 * TI) + p
            if ni is not None:
                prepare(ni, np_)
            dve.wait_ge(act_evac, now(i - 3 * TI, p))
            c.step(v.tensor_tensor(prod[p][:, 0:D], xr[p][:, 0:D], att_src, ALU.mult))
            n = c.step(v.tensor_tensor(prod[p][:, D:], xr[p][:, 0:D], att_dst, ALU.mult))
            c.wait(n - 1)
            c.step(v.tensor_reduce(xr[p][:, D:ACCW], prod[p][:, 0:D].rearrange("p (h d) -> p h d", h=HEADS),
                                   axis=AX.X, op=ALU.add))
            tgt = adst3[:, bass.ds(t, 1), :].rearrange("p a f -> p (a f)")
            c.wait(n)
            c.then(v.tensor_reduce(tgt, prod[p][:, D:].rearrange("p (h d) -> p h d", h=HEADS),
                                   axis=AX.X, op=ALU.add))
            c.then(v.tensor_tensor(aself[p], xr[p][:, D:ACCW], tgt, ALU.add))
            c.then(v.scalar_tensor_tensor(own3[:, bass.ds(t, 1), :].rearrange("p a f -> p (a f)"),
                                          aself[p], 0.2, aself[p], ALU.mult, ALU.max))
            dve.sem_inc(b_ready, 1)
        dve.wait_ge(att_in, 16)
        c.then(v.memset(mnode[:, :], -BIG))
        prepare(3 * TI, 0)
        tile_loop(dve, 3 * TI, step, 2 * 9)

    def l3_scalar(act):
        def prepare(i, p):
            root(act, i, p)
            turned_relu(act, i - TI, p)

        def step(i, p, ni, np_):
            act.wait_ge(proj_ps, now(i - 2 * TI, p))
            act.wait_ge(out_a[p], 16 * (i + 1))
            nc.scalar.copy(xr[p][:, 0:D], psum[:, 2 + p, 0:D]).then_inc(act_evac, 1)
            if ni is not None:
                prepare(ni, np_)
        prepare(3 * TI, 0)
        tile_loop(act, 3 * TI, step)

    def l3_tensor(pe):
        def step(i, p, ni, np_):
            pe.wait_ge(ht_ready, now(i - TI, p))
            pe.wait_ge(act_evac, prev(i - 3 * TI, p))
            project(psum[:, 2 + p, 0:D], p, wts, D, 0, D).then_inc(proj_ps, 1)
            if ni is not None:
                turn(pe, ni, np_)
        pe.wait_ge(weights_sem, 32 + 80 + 32 + 16)
        turn(pe, 3 * TI, 0)
        tile_loop(pe, 3 * TI, step)

    stage_of(sync=l3_sync, vector=l3_vector, scalar=l3_scalar, tensor=l3_tensor)
    attention(3, 1, False, xh_tab, ACCW, 0)

    bias_b, gamma_b, beta_b = bcast[:, 2 * D:3 * D], bcast[:, 3 * D:4 * D], bcast[:, 4 * D:5 * D]
    FULL, REST = N // P, N % P
    place[0] = 0
    sq, fx = carve(D), carve(D)
    fxh = carve(ACCW)
    by_edges, by_own, top_f = (kh[:, 4096 + k * TILES * HEADS:4096 + (k + 1) * TILES * HEADS] for k in range(3))

    def t8(ap):
        return ap.rearrange("p (t h) -> p t h", h=HEADS)

    xh_in, es_ready, wself_ready, own_added = [sem("xh_in0"), sem("xh_in1")], sem("es_ready"), sem("wself_ready"), sem("own_added")
    sum_b, mean_b, gain_b = (kh[:, k * D:(k + 1) * D] for k in range(3))
    row_ready, sq_used = sem("row_ready"), sem("sq_used")
    mean_ps, sq_ready, var_ps, var_sb, gain_ready = (
        sem(n) for n in ("mean_ps", "sq_ready", "var_ps", "var_sb", "gain_ready"))
    f_in, f_out = [sem("f_in0"), sem("f_in1")], [sem("f_out0"), sem("f_out1")]
    f_used, f_ready = sem("f_used"), sem("f_ready")

    def final_vector(dve):
        v, c = nc.vector, v_own.bind(dve)
        z = acc3[:, :, D:ACCW]
        c.then(v.tensor_tensor(mnode[:, :], mnode[:, :], adst, ALU.add))
        c.then(v.scalar_tensor_tensor(mnode[:, :], mnode[:, :], 0.2, mnode[:, :], ALU.mult, ALU.max))
        c.then(v.tensor_tensor(top_f, mnode[:, :], own, ALU.max))
        c.step(v.tensor_tensor(by_edges, mnode[:, :], top_f, ALU.subtract))
        c.then(v.tensor_tensor(by_own, own, top_f, ALU.subtract))
        dve.sem_inc(es_ready, 1)
        dve.wait_ge(wself_ready, 2)
        c.then(v.tensor_tensor(z, z, t8(by_edges), ALU.mult))
        c.then(v.tensor_tensor(z, z, t8(by_own), ALU.add))
        c.then(v.reciprocal(t8(top_f), z))
        c.step(v.tensor_tensor(by_edges, by_edges, top_f, ALU.mult))
        c.then(v.tensor_tensor(by_own, by_own, top_f, ALU.mult))

        def total_of(t, n):
            return acc3[0:n, bass.ds(t, 1), 0:D].rearrange("p a f -> p (a f)")

        def finish(tiles, i):
            for t, n, p in tiles:
                def factor(f):
                    return t8(f)[0:n, bass.ds(t, 1), :].rearrange("p a f -> p (a f)").unsqueeze(2) \
                        .to_broadcast([n, HEADS, DH])
                heads = total_of(t, n).rearrange("p (h d) -> p h d", h=HEADS)
                row = fxh[p][0:n, 0:D].rearrange("p (h d) -> p h d", h=HEADS)
                dve.wait_ge(xh_in[p], 16 * (i + 1))
                c.step(v.tensor_tensor(heads, heads, factor(by_edges), ALU.mult))
                c.step(v.tensor_tensor(row, row, factor(by_own), ALU.mult))
            first = c.n - 2 * len(tiles)
            for k, (t, n, p) in enumerate(tiles):
                c.wait(first + 2 * k + 2)
                v.tensor_tensor(total_of(t, n), total_of(t, n), fxh[p][0:n, 0:D], ALU.add).then_inc(own_added, 1)
            for t, n, p in tiles:
                dve.wait_ge(own_added, t + 1)
                v.tensor_tensor(total_of(t, n), total_of(t, n), bias_b[0:n], ALU.add).then_inc(row_ready, 1)

        def centre(tiles):
            for t, n, p in tiles:
                c.step(v.tensor_tensor(total_of(t, n), total_of(t, n), mean_b[0:n], ALU.subtract))
            first = c.n - len(tiles)
            for k, (t, n, p) in enumerate(tiles):
                c.wait(first + k + 1)
                dve.wait_ge(sq_used, t + 1)
                v.tensor_tensor(sq[p][0:n], total_of(t, n), total_of(t, n), ALU.mult).then_inc(sq_ready, 1)

        def scale(tiles, i):
            for t, n, p in tiles:
                c.step(v.tensor_tensor(total_of(t, n), total_of(t, n), gain_b[0:n], ALU.mult))
            first = c.n - len(tiles)
            for k, (t, n, p) in enumerate(tiles):
                c.wait(first + k + 1)
                c.step(v.tensor_tensor(total_of(t, n), total_of(t, n), beta_b[0:n], ALU.add))
            for k, (t, n, p) in enumerate(tiles):
                c.wait(first + len(tiles) + k + 1)
                dve.wait_ge(f_in[p], 16 * (i + 1))
                v.tensor_tensor(fx[p][0:n], fx[p][0:n], total_of(t, n), ALU.add).then_inc(f_ready, 1)

        def pair(i):
            return [(2 * i, P, 0), (2 * i + 1, P, 1)]
        rest = [(FULL, REST, 0)]

        with dve.Fori(0, FULL // 2) as i:
            c.enter(i, 4)
            finish(pair(i), i)
        c.leave(FULL // 2)
        finish(rest, FULL // 2)
        dve.wait_ge(row_ready, FULL + 1)
        dve.wait_ge(mean_ps, 1)
        c.then(v.tensor_scalar(mean_b, psum[:, 0, 0:D], 1.0 / N, None, ALU.mult))
        with dve.Fori(0, FULL // 2) as i:
            c.enter(i, 2)
            centre(pair(i))
        c.leave(FULL // 2)
        centre(rest)
        dve.wait_ge(var_ps, 1)
        v.tensor_scalar(sum_b, psum[:, 1, 0:D], 1.0 / N, 1e-5, ALU.mult, ALU.add).then_inc(var_sb, 1)
        dve.wait_ge(gain_ready, 1)
        c.then(v.reciprocal(gain_b, gain_b))
        c.then(v.tensor_tensor(gain_b, gain_b, gamma_b, ALU.mult))
        with dve.Fori(0, FULL // 2) as i:
            c.enter(i, 4)
            scale(pair(i), i)
        c.leave(FULL // 2)
        scale(rest, FULL // 2)

    def final_tensor(pe):
        def rows_of(t, n, start=False, stop=False):
            pe.wait_ge(row_ready, t + 1)
            row = acc3[0:n, bass.ds(t, 1), 0:D].rearrange("p a f -> p (a f)")
            return nc.tensor.matmul(psum[:, 0, 0:D], ones[0:n, :], row, start=start, stop=stop)

        def squares_of(t, n, p, start=False, stop=False):
            pe.wait_ge(sq_ready, t + 1)
            mm = nc.tensor.matmul(psum[:, 1, 0:D], ones[0:n, :], sq[p][0:n], start=start, stop=stop)
            return mm.then_inc(var_ps if stop else sq_used, 1)

        pe.sem_inc(sq_used, 2)
        rows_of(0, P, start=True)
        rows_of(1, P)
        with pe.Fori(1, FULL // 2) as i:
            for p in range(2):
                rows_of(2 * i + p, P)
        rows_of(FULL, REST, stop=True).then_inc(mean_ps, 1)
        squares_of(0, P, 0, start=True)
        squares_of(1, P, 1)
        with pe.Fori(1, FULL // 2) as i:
            for p in range(2):
                squares_of(2 * i + p, P, p)
        squares_of(FULL, REST, 0, stop=True)

    def final_scalar(act):
        act.wait_ge(es_ready, 1)
        nc.scalar.activation(by_edges, by_edges, ACT.Exp).then_inc(wself_ready, 1)
        nc.scalar.activation(by_own, by_own, ACT.Exp).then_inc(wself_ready, 1)
        act.wait_ge(var_sb, 1)
        nc.scalar.activation(gain_b, sum_b, ACT.Sqrt).then_inc(gain_ready, 1)

    def final_sync(sp):
        for p in range(2):
            sp.dma_start(fxh[p], xh_tab[p * P:(p + 1) * P, :]).then_inc(xh_in[p], 16)
        with sp.Fori(1, FULL // 2) as i:
            for p in range(2):
                sp.wait_ge(own_added, 2 * i + p - 1)
                sp.dma_start(fxh[p], tile_rows(xh_tab, 2 * i + p)).then_inc(xh_in[p], 16)
        sp.wait_ge(own_added, FULL - 1)
        sp.dma_start(fxh[0][0:REST], xh_tab[FULL * P:N, :]).then_inc(xh_in[0], 16)
        with sp.Fori(0, FULL // 2) as i:
            for p in range(2):
                sp.wait_ge(f_out[p], 16 * (i + 1))
                sp.dma_start(fx[p], tile_rows(x3_tab, 2 * i + p)).then_inc(f_in[p], 16)
            for p in range(2):
                sp.wait_ge(f_ready, 2 * i + p + 1)
                sp.dma_start(tile_rows(out, 2 * i + p), fx[p]).then_inc(f_out[p], 16)
        sp.wait_ge(f_out[0], 16 * (FULL // 2 + 1))
        sp.dma_start(fx[0][0:REST], x3_tab[FULL * P:N, :]).then_inc(f_in[0], 16)
        sp.wait_ge(f_ready, FULL + 1)
        sp.dma_start(out[FULL * P:N, :], fx[0][0:REST]).then_inc(f_out[0], 16)
        sp.wait_ge(f_out[0], 16 * (FULL // 2 + 2))
        sp.wait_ge(f_out[1], 16 * (FULL // 2 + 1))

    stage_of(vector=final_vector, tensor=final_tensor, scalar=final_scalar, sync=final_sync)

    def start_sync(sp):
        for s in (*out_a, *out_b, *f_out, *g_out):
            sp.sem_inc(s, 16)
        for s in x_in:
            sp.sem_inc(s, 16)

    def start_gpsimd(pool):
        pass

    def start_vector(dve):
        give(dve, 2, var_ready, norm_ready, dve_evac, a_ready, b_ready, score_ready, scan_ready, best_ready,
             max_ready, fall_ready, shifted, srcb_ready, idx2_ready, pre_ready, new_ready, x2_ready)
        give(dve, 4, same_ready, chunk_dve)
        give(dve, 8, pair_used, msg_ready)
        give(dve, RING, acc_done)

    def start_scalar(act):
        give(act, 2, std_ready, ht_ready, act_evac, seg_ready, mark_ready, alpha_ready, weight_ready, gt_sb, conv_sb,
             gate_sb, cand_ready)
        give(act, 4, oht_sb, merged_sb)
        give(act, 6, chunk_act)
        give(act, RING, out_sb)

    def start_tensor(pe):
        give(pe, 2, turn_ps, proj_ps, score_ps, back_ps, best_ps, max_ps, gt_ps, conv_ps, gate_ps, qv_ps, cand_ps)
        give(pe, 4, oht_ps, row_ps, merged_ps)
        give(pe, 8, key_ps)
        give(pe, 10, chunk_ps)
        give(pe, RING, agg_done, out_ps)

    starts_of = {"sync": start_sync, "gpsimd": start_gpsimd, "vector": start_vector,
                 "scalar": start_scalar, "tensor": start_tensor}

    def engine_program(name, eng):
        starts_of[name](eng)
        for k, part in enumerate(progs[name][:UPTO]):
            if part is not None:
                part(eng)
            eng.drain().then_inc(stage, 1)
            eng.wait_ge(stage, len(progs) * (k + 1))

    block = ctx.enter_context(nc.Block())

    @block.sync
    def _(sp):
        engine_program("sync", sp)

    @block.gpsimd
    def _(pool):
        engine_program("gpsimd", pool)

    @block.vector
    def _(dve):
        engine_program("vector", dve)

    @block.scalar
    def _(act):
        engine_program("scalar", act)

    @block.tensor
    def _(pe):
        engine_program("tensor", pe)


UPTO = None


def kernel(**inputs):
    import concourse.bacc as bacc
    from concourse.bass_utils import run_bass_kernel_spmd

    g = {k: np.asarray(v) for k, v in inputs.items()}

    def edges(name, fill):
        padded = np.full(P * COLS, fill, np.int32)
        padded[:EDGES] = g[name]
        return padded.reshape(P, COLS)

    x = np.zeros((NP, D), np.float32)
    x[:N] = g["x"]
    row = lambda *names: np.concatenate([g[n].reshape(-1) for n in names])[None]
    arrays = {
        "x": x, "src": edges("src", N), "dst": edges("dst", N), "typ": edges("edge_type_8", 0),
        "w0": np.concatenate([g["L0_gnn_Wq"], g["L0_gnn_Wv"], g["L0_gnn_Wk"]], 1),
        "b0": row("L0_gnn_bq", "L0_gnn_bv", "L0_gnn_bk"),
        "w_in": g["L1_gnn_W_in"].T, "w_out": g["L1_gnn_W_out"].T,
        "w_ih": g["L1_gnn_W_ih"].T, "w_hh": g["L1_gnn_W_hh"].T,
        "b1": row("L1_gnn_b_in", "L1_gnn_b_out", "L1_gnn_b_ih", "L1_gnn_b_hh"),
        "w2": np.concatenate([*g["L2_gnn_weight"], g["L2_gnn_sl_w"].T], 1), "b2": row("L2_gnn_sl_b"),
        "w3": g["L3_gnn_W"],
        "rows3": row("L3_gnn_att_src", "L3_gnn_att_dst", "L3_gnn_bias", "L3_gnn_gamma", "L3_gnn_beta"),
    }
    arrays = {f"in_{k}": np.ascontiguousarray(v) for k, v in arrays.items()}
    nc = bacc.Bacc("TRN2", target_bir_lowering=False, num_devices=1)
    args = {k[3:]: nc.dram_tensor(k, v.shape, mybir.dt.from_np(v.dtype), kind="ExternalInput").ap()
            for k, v in arrays.items()}
    out = nc.dram_tensor("out", (N, D), F32, kind="ExternalOutput").ap()
    program(nc, args, out)
    r = run_bass_kernel_spmd(nc, [arrays], core_ids=[0])
    return r.results[0]["out"]
```
